# Optimizing a Trainium2 kernel written in Bass

```python
import numpy as np
import jax
import jax.numpy as jnp

def _softmax(x, axis=-1):
    return jax.nn.softmax(x, axis=axis)

def _gelu(x):
    return jax.nn.gelu(x, approximate=True)

def _silu(x):
    return jax.nn.silu(x)

def _sigmoid(x):
    return jax.nn.sigmoid(x)

def _layernorm(x, axis=-1, eps=1e-05):
    m = jnp.mean(x, axis=axis, keepdims=True)
    v = jnp.var(x, axis=axis, keepdims=True)
    return (x - m) / jnp.sqrt(v + eps)

def _scatter_add(tgt, idx, src, axis=0):
    return tgt.at[idx].add(src)

def _segment_sum(src, seg, n):
    return jax.ops.segment_sum(src, seg, n)
kernel_name = 'mk_xattn_seq_d4_seqx_r8_858b66'

def setup_inputs(seed: int=0):
    np.random.seed(seed)
    _w = jnp.asarray

    def _rec_inputs():
        import jax
        import jax.numpy as jnp
        _rk = jax.random.key(seed)
        x = -0.0002928 + 1 * jax.random.normal(jax.random.fold_in(_rk, 1), (1, 1024, 128), jnp.float32)
        _lenS = 1024 - jax.random.randint(jax.random.fold_in(_rk, 7), (1,), 0, max(1, 1024 // 4) + 1, jnp.int32)
        _lenS2 = 6404 - jax.random.randint(jax.random.fold_in(_rk, 8), (1,), 0, max(1, 6404 // 4) + 1, jnp.int32)
        _ctx_1024P = jax.random.normal(jax.random.fold_in(_rk, 11), (1, 16, 128), jnp.float32)
        _ctx_1024c = jax.random.dirichlet(jax.random.fold_in(_rk, 511), 0.3 * jnp.ones((16,), jnp.float32), (1, 6404))
        _ctx_1024t = jnp.einsum('bsk,bkd->bsd', _ctx_1024c, _ctx_1024P)
        _ctx_1024t = _ctx_1024t * jax.lax.rsqrt(jnp.mean(jnp.square(_ctx_1024t)) + 1e-12) * 0.953939
        ctx_1024 = -1.39393e-06 + 0.999914 * (_ctx_1024t + 0.3 * jax.random.normal(jax.random.fold_in(_rk, 611), (1, 6404, 128), jnp.float32))
        _validS = jnp.arange(1024)[None, :] < _lenS[:, None]
        _validS2 = jnp.arange(6404)[None, :] < _lenS2[:, None]
        _causal = jnp.tril(jnp.ones((1024, 1024), dtype=bool))
        mask_1x1xSxS_bk0 = jnp.logical_not(jnp.broadcast_to(_validS[0:1, None, None, :], (1, 1, 1024, 1024)))
        return (x, ctx_1024, mask_1x1xSxS_bk0)
    x, ctx_1024, mask_1x1xSxS_bk0 = _rec_inputs()

    def _L0_xattn_setup():
        import jax, jax.numpy as jnp
        import numpy as np
        B, N, DIM = (2, 256, 128)
        HEADS, DH = (16, 64)
        SEG = 64
        NPM = 16
        NM = 16
        DFF = int(DIM * 4 * 2 / 3)
        EPS = 1.1920929e-07

        def rms_norm(x, w):
            return x * jax.lax.rsqrt(jnp.mean(x * x, axis=-1, keepdims=True) + EPS) * w
        key = jax.random.key(seed)
        ks = jax.random.split(key, 10)
        p = lambda i, shape: jax.random.normal(ks[i], shape, jnp.float32) * 0.02
        return {'x': jax.random.normal(ks[0], (B, N, DIM), jnp.float32), 'mem_out': jax.random.normal(ks[1], (B, N, DIM), jnp.float32), 'attn_norm_w': jnp.ones((DIM,), jnp.float32), 'to_qkv_w': p(2, (DIM, 3 * HEADS * DH)), 'to_out_w': p(3, (HEADS * DH, DIM)), 'persist_mem': jax.random.normal(ks[4], (HEADS, NPM, DH), jnp.float32), 'mem_pool_norm_w': jnp.ones((DIM,), jnp.float32), 'to_mem_tokens_w': p(5, (DIM, DIM)), 'ff_norm_w': jnp.ones((DIM,), jnp.float32), 'ff_w1': p(6, (DIM, 2 * DFF)), 'ff_b1': jnp.zeros((2 * DFF,), jnp.float32), 'ff_w2': p(7, (DFF, DIM)), 'ff_b2': jnp.zeros((DIM,), jnp.float32)}
    _L0_xattn_all = _L0_xattn_setup()
    _L0_xattn_in = {k: v for k, v in _L0_xattn_all.items() if k in ('attn_norm_w', 'to_qkv_w', 'to_out_w', 'persist_mem', 'mem_pool_norm_w', 'to_mem_tokens_w', 'ff_norm_w', 'ff_w1', 'ff_b1', 'ff_w2', 'ff_b2')}
    del _L0_xattn_all

    def _L1_xattn_setup():
        import jax, jax.numpy as jnp
        import numpy as np
        DIM = 128
        NUM_HEADS = 16
        HEAD_DIM = DIM // NUM_HEADS
        FF = 4 * DIM
        B, T, S = (8, 64, 512)

        def _perceiver_layer(x, inp, Wq, bq, Wk, bk, Wv, bv, Wo, bo, W1, b1, W2, b2):
            b, t, _ = x.shape
            s = inp.shape[1]
            q = (x @ Wq + bq).reshape(b, t, NUM_HEADS, HEAD_DIM)
            k = (inp @ Wk + bk).reshape(b, s, NUM_HEADS, HEAD_DIM)
            v = (inp @ Wv + bv).reshape(b, s, NUM_HEADS, HEAD_DIM)
            attn = jnp.einsum('bthd,bshd->bhts', q, k)
            attn = jax.nn.softmax(attn / jnp.sqrt(jnp.float32(HEAD_DIM)), axis=-1)
            out = jnp.einsum('bhts,bshd->bthd', attn, v).reshape(b, t, DIM)
            attn_out = out @ Wo + bo
            x = x + attn_out
            h = jax.nn.gelu(x @ W1 + b1, approximate=True)
            x = x + (h @ W2 + b2)
            return x
        key = jax.random.key(seed)
        ks = jax.random.split(key, 14)
        sc = 1.0 / np.sqrt(DIM)
        inp = {'x': jax.random.normal(ks[0], (B, T, DIM), jnp.float32), 'inp': jax.random.normal(ks[1], (B, S, DIM), jnp.float32), 'Wq': jax.random.normal(ks[2], (DIM, DIM), jnp.float32) * sc, 'bq': jnp.zeros((DIM,), jnp.float32), 'Wk': jax.random.normal(ks[3], (DIM, DIM), jnp.float32) * sc, 'bk': jnp.zeros((DIM,), jnp.float32), 'Wv': jax.random.normal(ks[4], (DIM, DIM), jnp.float32) * sc, 'bv': jnp.zeros((DIM,), jnp.float32), 'Wo': jax.random.normal(ks[5], (DIM, DIM), jnp.float32) * sc, 'bo': jnp.zeros((DIM,), jnp.float32), 'W1': jax.random.normal(ks[6], (DIM, FF), jnp.float32) * sc, 'b1': jnp.zeros((FF,), jnp.float32), 'W2': jax.random.normal(ks[7], (FF, DIM), jnp.float32) * (1.0 / np.sqrt(FF)), 'b2': jnp.zeros((DIM,), jnp.float32)}
        return inp
    _L1_xattn_all = _L1_xattn_setup()
    _L1_xattn_in = {k: v for k, v in _L1_xattn_all.items() if k in ('Wq', 'bq', 'Wk', 'bk', 'Wv', 'bv', 'Wo', 'bo', 'W1', 'b1', 'W2', 'b2')}
    del _L1_xattn_all

    def _L2_xattn_setup():
        import jax, jax.numpy as jnp
        import numpy as np
        B, S, H = (2, 256, 128)
        NH = 16
        HD = H // NH
        LN_EPS = 1e-05

        def _split_heads(x):
            b, s, _ = x.shape
            return x.reshape(b, s, NH, HD).transpose(0, 2, 1, 3)
        key = jax.random.key(seed)
        ks = jax.random.split(key, 10)
        sc = 1.0 / np.sqrt(H)
        return {'query': jax.random.normal(ks[0], (B, S, H), jnp.float32), 'key': jax.random.normal(ks[1], (B, S, H), jnp.float32), 'value': jax.random.normal(ks[2], (B, S, H), jnp.float32), 'Wq': jax.random.normal(ks[3], (H, H), jnp.float32) * sc, 'Wk': jax.random.normal(ks[4], (H, H), jnp.float32) * sc, 'Wv': jax.random.normal(ks[5], (H, H), jnp.float32) * sc, 'Wo': jax.random.normal(ks[6], (H, H), jnp.float32) * sc, 'bo': jnp.zeros((H,), jnp.float32), 'ln_gamma': jnp.ones((H,), jnp.float32), 'ln_beta': jnp.zeros((H,), jnp.float32)}
    _L2_xattn_all = _L2_xattn_setup()
    _L2_xattn_in = {k: v for k, v in _L2_xattn_all.items() if k in ('Wq', 'Wk', 'Wv', 'Wo', 'bo', 'ln_gamma', 'ln_beta')}
    del _L2_xattn_all

    def _L3_xattn_setup():
        import jax, jax.numpy as jnp
        import numpy as np
        EMBED_DIM = 128
        NUM_HEADS = 16
        HEAD_DIM = EMBED_DIM // NUM_HEADS
        FF_DIM = 512
        B, T, S = (2, 256, 256)
        LN_EPS = 1e-05

        def _layernorm(x, g, b):
            mu = jnp.mean(x, -1, keepdims=True)
            var = jnp.mean(jnp.square(x - mu), -1, keepdims=True)
            return (x - mu) * jax.lax.rsqrt(var + LN_EPS) * g + b

        def _mha(q_in, k_in, v_in, wq, bq, wk, bk, wv, bv, wo, bo, mask=None):
            Bq, Tq, C = q_in.shape
            Tk = k_in.shape[1]
            Q = (q_in @ wq + bq).reshape(Bq, Tq, NUM_HEADS, HEAD_DIM)
            K = (k_in @ wk + bk).reshape(Bq, Tk, NUM_HEADS, HEAD_DIM)
            V = (v_in @ wv + bv).reshape(Bq, Tk, NUM_HEADS, HEAD_DIM)
            scores = jnp.einsum('bqhd,bkhd->bhqk', Q, K) / np.sqrt(HEAD_DIM)
            if mask is not None:
                scores = jnp.where(mask, scores, -jnp.inf)
            attn = jax.nn.softmax(scores, axis=-1)
            out = jnp.einsum('bhqk,bkhd->bqhd', attn, V).reshape(Bq, Tq, C)
            return out @ wo + bo
        key = jax.random.key(seed)
        ks = jax.random.split(key, 20)
        sd = 1.0 / np.sqrt(EMBED_DIM)
        d = {'x': jax.random.normal(ks[0], (B, T, EMBED_DIM), jnp.float32), 'encoder_outputs': jax.random.normal(ks[1], (B, S, EMBED_DIM), jnp.float32), 'tgt_mask': jnp.tril(jnp.ones((T, T), bool))[None, None]}
        names = ['sa_wq', 'sa_wk', 'sa_wv', 'sa_wo', 'ca_wq', 'ca_wk', 'ca_wv', 'ca_wo']
        for i, n in enumerate(names):
            d[n] = jax.random.normal(ks[2 + i], (EMBED_DIM, EMBED_DIM), jnp.float32) * sd
            d[n.replace('w', 'b')] = jnp.zeros((EMBED_DIM,), jnp.float32)
        d['ff_w1'] = jax.random.normal(ks[10], (EMBED_DIM, FF_DIM), jnp.float32) * sd
        d['ff_b1'] = jnp.zeros((FF_DIM,), jnp.float32)
        d['ff_w2'] = jax.random.normal(ks[11], (FF_DIM, EMBED_DIM), jnp.float32) * (1.0 / np.sqrt(FF_DIM))
        d['ff_b2'] = jnp.zeros((EMBED_DIM,), jnp.float32)
        for i in (1, 2, 3):
            d[f'ln{i}_g'] = jnp.ones((EMBED_DIM,), jnp.float32)
            d[f'ln{i}_b'] = jnp.zeros((EMBED_DIM,), jnp.float32)
        return d
    _L3_xattn_all = _L3_xattn_setup()
    _L3_xattn_in = {k: v for k, v in _L3_xattn_all.items() if k in ('sa_wq', 'sa_bq', 'sa_wk', 'sa_bk', 'sa_wv', 'sa_bv', 'sa_wo', 'sa_bo', 'ca_wq', 'ca_bq', 'ca_wk', 'ca_bk', 'ca_wv', 'ca_bv', 'ca_wo', 'ca_bo', 'ff_w1', 'ff_b1', 'ff_w2', 'ff_b2', 'ln1_g', 'ln1_b', 'ln2_g', 'ln2_b', 'ln3_g', 'ln3_b')}
    del _L3_xattn_all
    return {'x': x, 'ctx_1024': ctx_1024, 'mask_1x1xSxS_bk0': mask_1x1xSxS_bk0, 'L0_xattn_attn_norm_w': _L0_xattn_in['attn_norm_w'], 'L0_xattn_to_qkv_w': _L0_xattn_in['to_qkv_w'], 'L0_xattn_to_out_w': _L0_xattn_in['to_out_w'], 'L0_xattn_persist_mem': _L0_xattn_in['persist_mem'], 'L0_xattn_mem_pool_norm_w': _L0_xattn_in['mem_pool_norm_w'], 'L0_xattn_to_mem_tokens_w': _L0_xattn_in['to_mem_tokens_w'], 'L0_xattn_ff_norm_w': _L0_xattn_in['ff_norm_w'], 'L0_xattn_ff_w1': _L0_xattn_in['ff_w1'], 'L0_xattn_ff_b1': _L0_xattn_in['ff_b1'], 'L0_xattn_ff_w2': _L0_xattn_in['ff_w2'], 'L0_xattn_ff_b2': _L0_xattn_in['ff_b2'], 'L1_xattn_Wq': _L1_xattn_in['Wq'], 'L1_xattn_bq': _L1_xattn_in['bq'], 'L1_xattn_Wk': _L1_xattn_in['Wk'], 'L1_xattn_bk': _L1_xattn_in['bk'], 'L1_xattn_Wv': _L1_xattn_in['Wv'], 'L1_xattn_bv': _L1_xattn_in['bv'], 'L1_xattn_Wo': _L1_xattn_in['Wo'], 'L1_xattn_bo': _L1_xattn_in['bo'], 'L1_xattn_W1': _L1_xattn_in['W1'], 'L1_xattn_b1': _L1_xattn_in['b1'], 'L1_xattn_W2': _L1_xattn_in['W2'], 'L1_xattn_b2': _L1_xattn_in['b2'], 'L2_xattn_Wq': _L2_xattn_in['Wq'], 'L2_xattn_Wk': _L2_xattn_in['Wk'], 'L2_xattn_Wv': _L2_xattn_in['Wv'], 'L2_xattn_Wo': _L2_xattn_in['Wo'], 'L2_xattn_bo': _L2_xattn_in['bo'], 'L2_xattn_ln_gamma': _L2_xattn_in['ln_gamma'], 'L2_xattn_ln_beta': _L2_xattn_in['ln_beta'], 'L3_xattn_sa_wq': _L3_xattn_in['sa_wq'], 'L3_xattn_sa_bq': _L3_xattn_in['sa_bq'], 'L3_xattn_sa_wk': _L3_xattn_in['sa_wk'], 'L3_xattn_sa_bk': _L3_xattn_in['sa_bk'], 'L3_xattn_sa_wv': _L3_xattn_in['sa_wv'], 'L3_xattn_sa_bv': _L3_xattn_in['sa_bv'], 'L3_xattn_sa_wo': _L3_xattn_in['sa_wo'], 'L3_xattn_sa_bo': _L3_xattn_in['sa_bo'], 'L3_xattn_ca_wq': _L3_xattn_in['ca_wq'], 'L3_xattn_ca_bq': _L3_xattn_in['ca_bq'], 'L3_xattn_ca_wk': _L3_xattn_in['ca_wk'], 'L3_xattn_ca_bk': _L3_xattn_in['ca_bk'], 'L3_xattn_ca_wv': _L3_xattn_in['ca_wv'], 'L3_xattn_ca_bv': _L3_xattn_in['ca_bv'], 'L3_xattn_ca_wo': _L3_xattn_in['ca_wo'], 'L3_xattn_ca_bo': _L3_xattn_in['ca_bo'], 'L3_xattn_ff_w1': _L3_xattn_in['ff_w1'], 'L3_xattn_ff_b1': _L3_xattn_in['ff_b1'], 'L3_xattn_ff_w2': _L3_xattn_in['ff_w2'], 'L3_xattn_ff_b2': _L3_xattn_in['ff_b2'], 'L3_xattn_ln1_g': _L3_xattn_in['ln1_g'], 'L3_xattn_ln1_b': _L3_xattn_in['ln1_b'], 'L3_xattn_ln2_g': _L3_xattn_in['ln2_g'], 'L3_xattn_ln2_b': _L3_xattn_in['ln2_b'], 'L3_xattn_ln3_g': _L3_xattn_in['ln3_g'], 'L3_xattn_ln3_b': _L3_xattn_in['ln3_b']}

def reference(x, ctx_1024, mask_1x1xSxS_bk0, L0_xattn_attn_norm_w, L0_xattn_to_qkv_w, L0_xattn_to_out_w, L0_xattn_persist_mem, L0_xattn_mem_pool_norm_w, L0_xattn_to_mem_tokens_w, L0_xattn_ff_norm_w, L0_xattn_ff_w1, L0_xattn_ff_b1, L0_xattn_ff_w2, L0_xattn_ff_b2, L1_xattn_Wq, L1_xattn_bq, L1_xattn_Wk, L1_xattn_bk, L1_xattn_Wv, L1_xattn_bv, L1_xattn_Wo, L1_xattn_bo, L1_xattn_W1, L1_xattn_b1, L1_xattn_W2, L1_xattn_b2, L2_xattn_Wq, L2_xattn_Wk, L2_xattn_Wv, L2_xattn_Wo, L2_xattn_bo, L2_xattn_ln_gamma, L2_xattn_ln_beta, L3_xattn_sa_wq, L3_xattn_sa_bq, L3_xattn_sa_wk, L3_xattn_sa_bk, L3_xattn_sa_wv, L3_xattn_sa_bv, L3_xattn_sa_wo, L3_xattn_sa_bo, L3_xattn_ca_wq, L3_xattn_ca_bq, L3_xattn_ca_wk, L3_xattn_ca_bk, L3_xattn_ca_wv, L3_xattn_ca_bv, L3_xattn_ca_wo, L3_xattn_ca_bo, L3_xattn_ff_w1, L3_xattn_ff_b1, L3_xattn_ff_w2, L3_xattn_ff_b2, L3_xattn_ln1_g, L3_xattn_ln1_b, L3_xattn_ln2_g, L3_xattn_ln2_b, L3_xattn_ln3_g, L3_xattn_ln3_b):
    import jax
    import jax.numpy as jnp

    def _L0_xattn_ref(x, mem_out, attn_norm_w, to_qkv_w, to_out_w, persist_mem, mem_pool_norm_w, to_mem_tokens_w, ff_norm_w, ff_w1, ff_b1, ff_w2, ff_b2):
        import jax, jax.numpy as jnp
        import numpy as np
        B, N, DIM = (2, 256, 128)
        HEADS, DH = (16, 64)
        SEG = 64
        NPM = 16
        NM = 16
        DFF = int(DIM * 4 * 2 / 3)
        EPS = 1.1920929e-07

        def rms_norm(x, w):
            return x * jax.lax.rsqrt(jnp.mean(x * x, axis=-1, keepdims=True) + EPS) * w
        b, n, _ = x.shape
        split_heads = lambda t: t.reshape(b, -1, HEADS, DH).transpose(0, 2, 1, 3)
        pooled = rms_norm(mem_out.mean(axis=1), mem_pool_norm_w)
        mem_tok = jnp.broadcast_to((pooled @ to_mem_tokens_w)[:, None, :], (b, NM, DIM))
        _, k_c, v_c = jnp.split(mem_tok @ to_qkv_w, 3, axis=-1)
        k_extra, v_extra = (split_heads(k_c), split_heads(v_c))
        xn = rms_norm(x, attn_norm_w)
        q, k, v = jnp.split(xn @ to_qkv_w, 3, axis=-1)
        q, k, v = (split_heads(q), split_heads(k), split_heads(v))
        pos = jnp.arange(n)
        inv = 1.0 / 10000.0 ** (jnp.arange(0, DH, 2, dtype=jnp.float32) / DH)
        ang = jnp.repeat(pos[:, None].astype(jnp.float32) * inv[None, :], 2, axis=-1)
        cos, sin = (jnp.cos(ang), jnp.sin(ang))

        def rope(t):
            z = t.reshape(t.shape[:-1] + (-1, 2))
            rh = jnp.stack([-z[..., 1], z[..., 0]], axis=-1).reshape(t.shape)
            return t * cos + rh * sin
        q, k = (rope(q), rope(k))
        pm = jnp.broadcast_to(persist_mem[None], (b, HEADS, NPM, DH))
        kf = jnp.concatenate([k_extra, pm, k], axis=2)
        vf = jnp.concatenate([v_extra, pm, v], axis=2)
        P = NPM + NM
        ki = jnp.arange(kf.shape[2])[None, :]
        qi = pos[:, None]
        causal = qi >= ki - P
        seg = qi // SEG == (ki - P) // SEG
        mask = causal & seg | (ki < P)
        scores = jnp.einsum('bhid,bhjd->bhij', q, kf) * DH ** (-0.5)
        scores = jnp.where(mask[None, None], scores, -1e+30)
        probs = jax.nn.softmax(scores, axis=-1)
        o = jnp.einsum('bhij,bhjd->bhid', probs, vf)
        attn_out = o.transpose(0, 2, 1, 3).reshape(b, n, HEADS * DH) @ to_out_w
        x = x + attn_out
        h = rms_norm(x, ff_norm_w) @ ff_w1 + ff_b1
        a, g = jnp.split(h, 2, axis=-1)
        x = x + jax.nn.silu(g) * a @ ff_w2 + ff_b2
        return x

    def _L1_xattn_ref(x, inp, Wq, bq, Wk, bk, Wv, bv, Wo, bo, W1, b1, W2, b2):
        import jax, jax.numpy as jnp
        import numpy as np
        DIM = 128
        NUM_HEADS = 16
        HEAD_DIM = DIM // NUM_HEADS
        FF = 4 * DIM
        B, T, S = (8, 64, 512)

        def _perceiver_layer(x, inp, Wq, bq, Wk, bk, Wv, bv, Wo, bo, W1, b1, W2, b2):
            b, t, _ = x.shape
            s = inp.shape[1]
            q = (x @ Wq + bq).reshape(b, t, NUM_HEADS, HEAD_DIM)
            k = (inp @ Wk + bk).reshape(b, s, NUM_HEADS, HEAD_DIM)
            v = (inp @ Wv + bv).reshape(b, s, NUM_HEADS, HEAD_DIM)
            attn = jnp.einsum('bthd,bshd->bhts', q, k)
            attn = jax.nn.softmax(attn / jnp.sqrt(jnp.float32(HEAD_DIM)), axis=-1)
            out = jnp.einsum('bhts,bshd->bthd', attn, v).reshape(b, t, DIM)
            attn_out = out @ Wo + bo
            x = x + attn_out
            h = jax.nn.gelu(x @ W1 + b1, approximate=True)
            x = x + (h @ W2 + b2)
            return x
        return _perceiver_layer(x, inp, Wq, bq, Wk, bk, Wv, bv, Wo, bo, W1, b1, W2, b2)

    def _L2_xattn_ref(query, key, value, Wq, Wk, Wv, Wo, bo, ln_gamma, ln_beta):
        import jax, jax.numpy as jnp
        import numpy as np
        B, S, H = (2, 256, 128)
        NH = 16
        HD = H // NH
        LN_EPS = 1e-05

        def _split_heads(x):
            b, s, _ = x.shape
            return x.reshape(b, s, NH, HD).transpose(0, 2, 1, 3)
        q = _split_heads(query @ Wq.T)
        k = _split_heads(key @ Wk.T)
        v = _split_heads(value @ Wv.T)
        scaling = 1.0 / jnp.sqrt(jnp.asarray(HD, q.dtype))
        logits = scaling * jnp.einsum('bhqd,bhkd->bhqk', q, k)
        attn = jax.nn.softmax(logits, axis=-1)
        ctx = jnp.einsum('bhqk,bhkd->bhqd', attn, v)
        ctx = ctx.transpose(0, 2, 1, 3).reshape(query.shape[0], q.shape[2], H)
        projected = ctx @ Wo.T + bo
        resid = query + projected
        mu = jnp.mean(resid, axis=-1, keepdims=True)
        var = jnp.var(resid, axis=-1, keepdims=True)
        return (resid - mu) / jnp.sqrt(var + LN_EPS) * ln_gamma + ln_beta

    def _L3_xattn_ref(x, encoder_outputs, tgt_mask, sa_wq, sa_bq, sa_wk, sa_bk, sa_wv, sa_bv, sa_wo, sa_bo, ca_wq, ca_bq, ca_wk, ca_bk, ca_wv, ca_bv, ca_wo, ca_bo, ff_w1, ff_b1, ff_w2, ff_b2, ln1_g, ln1_b, ln2_g, ln2_b, ln3_g, ln3_b):
        import jax, jax.numpy as jnp
        import numpy as np
        EMBED_DIM = 128
        NUM_HEADS = 16
        HEAD_DIM = EMBED_DIM // NUM_HEADS
        FF_DIM = 512
        B, T, S = (2, 256, 256)
        LN_EPS = 1e-05

        def _layernorm(x, g, b):
            mu = jnp.mean(x, -1, keepdims=True)
            var = jnp.mean(jnp.square(x - mu), -1, keepdims=True)
            return (x - mu) * jax.lax.rsqrt(var + LN_EPS) * g + b

        def _mha(q_in, k_in, v_in, wq, bq, wk, bk, wv, bv, wo, bo, mask=None):
            Bq, Tq, C = q_in.shape
            Tk = k_in.shape[1]
            Q = (q_in @ wq + bq).reshape(Bq, Tq, NUM_HEADS, HEAD_DIM)
            K = (k_in @ wk + bk).reshape(Bq, Tk, NUM_HEADS, HEAD_DIM)
            V = (v_in @ wv + bv).reshape(Bq, Tk, NUM_HEADS, HEAD_DIM)
            scores = jnp.einsum('bqhd,bkhd->bhqk', Q, K) / np.sqrt(HEAD_DIM)
            if mask is not None:
                scores = jnp.where(mask, scores, -jnp.inf)
            attn = jax.nn.softmax(scores, axis=-1)
            out = jnp.einsum('bhqk,bkhd->bqhd', attn, V).reshape(Bq, Tq, C)
            return out @ wo + bo
        h = _layernorm(x, ln1_g, ln1_b)
        x = x + _mha(h, h, h, sa_wq, sa_bq, sa_wk, sa_bk, sa_wv, sa_bv, sa_wo, sa_bo, tgt_mask)
        h = _layernorm(x, ln2_g, ln2_b)
        x = x + _mha(h, encoder_outputs, encoder_outputs, ca_wq, ca_bq, ca_wk, ca_bk, ca_wv, ca_bv, ca_wo, ca_bo, None)
        h = _layernorm(x, ln3_g, ln3_b)
        ff = jax.nn.relu(h @ ff_w1 + ff_b1) @ ff_w2 + ff_b2
        return x + ff
    x = _L0_xattn_ref(x, ctx_1024, L0_xattn_attn_norm_w, L0_xattn_to_qkv_w, L0_xattn_to_out_w, L0_xattn_persist_mem, L0_xattn_mem_pool_norm_w, L0_xattn_to_mem_tokens_w, L0_xattn_ff_norm_w, L0_xattn_ff_w1, L0_xattn_ff_b1, L0_xattn_ff_w2, L0_xattn_ff_b2)
    x = _L1_xattn_ref(x, ctx_1024, L1_xattn_Wq, L1_xattn_bq, L1_xattn_Wk, L1_xattn_bk, L1_xattn_Wv, L1_xattn_bv, L1_xattn_Wo, L1_xattn_bo, L1_xattn_W1, L1_xattn_b1, L1_xattn_W2, L1_xattn_b2)
    x = _L2_xattn_ref(x, ctx_1024, ctx_1024, L2_xattn_Wq, L2_xattn_Wk, L2_xattn_Wv, L2_xattn_Wo, L2_xattn_bo, L2_xattn_ln_gamma, L2_xattn_ln_beta)
    x = _L3_xattn_ref(x, ctx_1024, mask_1x1xSxS_bk0, L3_xattn_sa_wq, L3_xattn_sa_bq, L3_xattn_sa_wk, L3_xattn_sa_bk, L3_xattn_sa_wv, L3_xattn_sa_bv, L3_xattn_sa_wo, L3_xattn_sa_bo, L3_xattn_ca_wq, L3_xattn_ca_bq, L3_xattn_ca_wk, L3_xattn_ca_bk, L3_xattn_ca_wv, L3_xattn_ca_bv, L3_xattn_ca_wo, L3_xattn_ca_bo, L3_xattn_ff_w1, L3_xattn_ff_b1, L3_xattn_ff_w2, L3_xattn_ff_b2, L3_xattn_ln1_g, L3_xattn_ln1_b, L3_xattn_ln2_g, L3_xattn_ln2_b, L3_xattn_ln3_g, L3_xattn_ln3_b)
    return x

_drawn_inputs = setup_inputs


def setup_inputs(seed=0):
    import zlib

    import numpy as np

    out = dict(_drawn_inputs(seed))
    spreads = {'L0_xattn_attn_norm_w': (1.0, 0.6),
     'L0_xattn_mem_pool_norm_w': (1.0, 0.6),
     'L0_xattn_ff_norm_w': (1.0, 0.6),
     'L0_xattn_ff_b1': (0.0, 0.8),
     'L0_xattn_ff_b2': (0.0, 0.354),
     'L1_xattn_bq': (0.0, 1.135),
     'L1_xattn_bk': (0.0, 2.0),
     'L1_xattn_bv': (0.0, 0.422),
     'L1_xattn_bo': (0.0, 0.41),
     'L1_xattn_b1': (0.0, 0.8),
     'L1_xattn_b2': (0.0, 0.429),
     'L2_xattn_bo': (0.0, 0.51),
     'L2_xattn_ln_gamma': (1.0, 0.2),
     'L2_xattn_ln_beta': (0.0, 0.1),
     'L3_xattn_sa_bq': (0.0, 0.385),
     'L3_xattn_sa_bk': (0.0, 2.0),
     'L3_xattn_sa_bv': (0.0, 0.1),
     'L3_xattn_sa_bo': (0.0, 0.1),
     'L3_xattn_ca_bq': (0.0, 0.468),
     'L3_xattn_ca_bk': (0.0, 2.0),
     'L3_xattn_ca_bv': (0.0, 0.1),
     'L3_xattn_ca_bo': (0.0, 0.1),
     'L3_xattn_ff_b1': (0.0, 0.1),
     'L3_xattn_ff_b2': (0.0, 0.1),
     'L3_xattn_ln1_g': (1.0, 0.2),
     'L3_xattn_ln1_b': (0.0, 0.1),
     'L3_xattn_ln2_g': (1.0, 0.557),
     'L3_xattn_ln2_b': (0.0, 0.622),
     'L3_xattn_ln3_g': (1.0, 0.2),
     'L3_xattn_ln3_b': (0.0, 0.1)}
    factors = {'L0_xattn_to_qkv_w': 3.54,
     'L0_xattn_to_mem_tokens_w': 8.0,
     'L0_xattn_ff_w1': 5.737,
     'L0_xattn_ff_w2': 5.757}
    for name, (base, spread) in spreads.items():
        noise = np.random.default_rng([zlib.crc32(name.encode()), seed]).standard_normal(out[name].shape)
        drawn = base * np.exp(spread * noise) if base else spread * noise
        out[name] = jnp.asarray(drawn.astype(out[name].dtype))
    for name, factor in factors.items():
        out[name] = (out[name] * factor).astype(out[name].dtype)
    return out
```

```python
from contextlib import ExitStack

import numpy as np

import concourse.bass as bass
from concourse import mybir

F32 = mybir.dt.float32
BF16 = mybir.dt.bfloat16
U8 = mybir.dt.uint8
ACT = mybir.ActivationFunctionType
ALU = mybir.AluOpType
AX = mybir.AxisListType

P = 128
N = 1024
C = 128
H = 16
HD = C // H
M = 6404
TPI = 4
TK = 124
CW = TPI * TK
NI = -(-M // CW)
MP = NI * CW
NT = MP // TK
LAST_VALID = M - (NT - 1) * TK
NTERM = 6
Q_PARTS = (0, 0, 1, 1, 0, 2)
K_PARTS = (0, 1, 0, 1, 2, 0)
NR = NTERM * HD
VC = 3 * HD + 1
QT = N // P
HALF = 512
KRING = 3
ROW_DMAS = 16 * QT
BIG = 1.0e30
SCALE = 1.0 / np.sqrt(np.float32(HD))

DH = 64
SEG = 64
NEX = 32
WK = NEX + P
DFF = 341
FFT = [(0, 128), (128, 128), (256, 85)]
FF = 512
RMS_EPS = 1.1920929e-07
LN_EPS = 1e-05

VECS = ["L0_xattn_attn_norm_w", "L0_xattn_mem_pool_norm_w", "L0_xattn_ff_norm_w", "L0_xattn_ff_b2",
        "L1_xattn_bq", "L1_xattn_bk", "L1_xattn_bo", "L1_xattn_b2", "L2_xattn_bo", "L2_xattn_ln_gamma",
        "L2_xattn_ln_beta", "L3_xattn_sa_bq", "L3_xattn_sa_bk", "L3_xattn_sa_bo", "L3_xattn_ca_bq",
        "L3_xattn_ca_bk", "L3_xattn_ca_bo", "L3_xattn_ff_b2", "L3_xattn_ln1_g", "L3_xattn_ln1_b",
        "L3_xattn_ln2_g", "L3_xattn_ln2_b", "L3_xattn_ln3_g", "L3_xattn_ln3_b"]
SQUARES = ["L0_xattn_to_mem_tokens_w", "L1_xattn_Wq", "L1_xattn_Wk", "L1_xattn_Wv", "L1_xattn_Wo",
           "L2_xattn_Wq", "L2_xattn_Wk", "L2_xattn_Wv", "L2_xattn_Wo", "L3_xattn_sa_wq", "L3_xattn_sa_wk",
           "L3_xattn_sa_wv", "L3_xattn_sa_wo", "L3_xattn_ca_wq", "L3_xattn_ca_wk", "L3_xattn_ca_wv",
           "L3_xattn_ca_wo"]


class Core:

    def __init__(self, nc, ctx):
        self.nc = nc
        self.ctx = ctx
        self.count = 0
        self.product_ready = ctx.enter_context(nc.semaphore("product_ready"))
        self.bank_free = ctx.enter_context(nc.semaphore("bank_free"))
        self.step_done = ctx.enter_context(nc.semaphore("step_done"))
        self.products = 0
        self.phase_sems = []
        self.steps = 0

    def name(self, text):
        self.count += 1
        return f"{text}_{self.count}"


def scope_tools(k, ctx):
    nc = k.nc

    def sb(text, shape, dt=F32):
        return ctx.enter_context(nc.sbuf_tensor(k.name(text), shape, dt))

    def ps(text, shape):
        return ctx.enter_context(nc.psum_tensor(k.name(text), shape, F32))

    def sem(text):
        k.phase_sems.append(ctx.enter_context(nc.semaphore(k.name(text))))
        return k.phase_sems[-1]

    return sb, ps, sem


def open_phase(k, ctx):
    used, k.phase_sems = k.phase_sems, []

    def clear():
        with k.nc.Block() as block:
            @block.gpsimd
            def _(pool):
                for s in used:
                    pool.sem_clear(s)

    ctx.callback(clear)
    return ctx.enter_context(k.nc.Block())


def linear(k, pieces, evacuate, on="vector"):
    nc = k.nc
    with ExitStack() as ctx:
        sb, ps, sem = scope_tools(k, ctx)
        banks = [ps("product", [P, HALF]) for _ in range(4)]
        product_ready, bank_free = k.product_ready, k.bank_free
        base = k.products
        k.products += len(pieces)
        block = ctx.enter_context(nc.Block())

        @block.tensor
        def _(pe):
            for n, (rows, cols, pairs) in enumerate(pieces):
                if n >= 4:
                    pe.wait_ge(bank_free, base + n - 3)
                for i, (w, a) in enumerate(pairs):
                    mm = pe.matmul(banks[n % 4][0:rows, 0:cols], w, a, start=(i == 0), stop=(i == len(pairs) - 1))
                mm.then_inc(product_ready, 1)

        def take(eng):
            for n, (rows, cols, _) in enumerate(pieces):
                eng.wait_ge(product_ready, base + n + 1)
                evacuate(eng, n, banks[n % 4][0:rows, 0:cols]).then_inc(bank_free, 1)

        if on == "vector":
            @block.vector
            def _(dve):
                take(dve)
        else:
            @block.scalar
            def _(act):
                take(act)


def steps(k, on, fns):
    nc = k.nc
    with ExitStack() as ctx:
        _, _, sem = scope_tools(k, ctx)
        step_done = k.step_done
        base = k.steps
        k.steps += len(fns)
        block = ctx.enter_context(nc.Block())

        def chain(eng):
            for n, f in enumerate(fns):
                if n:
                    eng.wait_ge(step_done, base + n)
                f(eng).then_inc(step_done, 1)

        if on == "vector":
            @block.vector
            def _(dve):
                chain(dve)
        else:
            @block.scalar
            def _(act):
                chain(act)


def halves(out_rows, w, a):
    return [(out_rows, HALF, [(w, a[:, c * HALF:(c + 1) * HALF])]) for c in range(2)]


def cols(a, n, w=HALF):
    return a[:, n * w:(n + 1) * w]


def inverse_root(k, var, out, eps):
    steps(k, "scalar", [lambda e: e.activation(out, var, ACT.Sqrt, bias=eps)])
    steps(k, "vector", [lambda e: e.reciprocal(out, out)])


def rms_norm(k, x, w, out, tmp, tmp2, n=N):
    width = min(n, HALF)
    steps(k, "vector", [lambda e: e.tensor_tensor(tmp, x, x, ALU.mult)])
    linear(k, [(P, width, [(k.mean_w[:], cols(tmp, c, width))]) for c in range(n // width)],
           lambda e, i, b: e.tensor_copy(cols(tmp2, i, width), b))
    inverse_root(k, tmp2, tmp, k.eps[:, 0:1])
    steps(k, "vector", [lambda e: e.scalar_tensor_tensor(out=out, in0=x, scalar=w, in1=tmp, op0=ALU.mult, op1=ALU.mult)])


def layer_norm(k, x, g, b, out, tmp, tmp2):
    linear(k, halves(P, k.mean_w[:], x),
           lambda e, i, bank: e.tensor_tensor(cols(tmp, i), cols(x, i), bank, ALU.subtract))
    steps(k, "vector", [lambda e: e.tensor_tensor(tmp2, tmp, tmp, ALU.mult)])
    linear(k, halves(P, k.mean_w[:], tmp2),
           lambda e, i, bank: e.activation(cols(out, i), bank, ACT.Sqrt, bias=k.eps[:, 1:2]), on="scalar")
    steps(k, "vector", [
        lambda e: e.reciprocal(tmp2, out),
        lambda e: e.tensor_tensor(tmp, tmp, tmp2, ALU.mult),
        lambda e: e.tensor_scalar(out, tmp, g, b, ALU.mult, ALU.add)])


def load_everything(k, d):
    nc = k.nc
    sb, _, _ = scope_tools(k, k.ctx)
    k.x = sb("x", [P, N])
    k.ctx_t = sb("context", [P, MP])
    k.vecs = sb("vectors", [P, len(VECS)])
    k.squares = sb("squares", [P, len(SQUARES), P])
    k.mean_w = sb("mean_w", [P, P])
    k.ident = sb("ident", [P, P])
    k.ident_b = sb("ident_b", [P, P], BF16)
    k.eps = sb("eps", [P, 2])
    k.last_rows = sb("last_rows", [P, 1])
    k.v = {n: k.vecs[:, i:i + 1] for i, n in enumerate(VECS)}
    k.w = {n: k.squares[:, i, :] for i, n in enumerate(SQUARES)}
    with ExitStack() as ctx:
        _, _, sem = scope_tools(k, ctx)
        loaded = [sem("loaded") for _ in range(6)]
        constant = sem("constant")
        block = open_phase(k, ctx)

        @block.sync
        def _(sp):
            for i, (dst, src) in enumerate([(k.x[:], d["x_t"]), (k.vecs[:], d["vecs"]), (k.ident[:], d["ident"]),
                                            (k.squares[:], d["squares"].rearrange("w p n -> p w n")),
                                            (k.last_rows[:], d["last_rows"]), (k.ctx_t[:], d["ctx_t"])]):
                sp.dma_start(dst, src).then_inc(loaded[i], 16)
            for s in loaded:
                sp.wait_ge(s, 16)

        @block.vector
        def _(dve):
            dve.memset(k.mean_w[:], 1.0 / C)
            dve.memset(k.eps[:, 0:1], RMS_EPS)
            dve.memset(k.eps[:, 1:2], LN_EPS)
            dve.wait_ge(loaded[2], 16)
            dve.tensor_copy(k.ident_b[:], k.ident[:]).then_inc(constant, 1)
            dve.wait_ge(constant, 1)


def windowed_layer(k, d):
    nc = k.nc
    with ExitStack() as lctx:
        sb, _, _ = scope_tools(k, lctx)
        mask = sb("window_mask", [P, WK])
        qp = sb("q_pairs", [P, H // 2, N])
        kp = sb("k_pairs", [P, H // 2, NEX + N])
        v_tok = sb("v_tokens", [P, QT, H * DH])
        v_ext = sb("v_extra", [NEX, H * DH])
        windowed_projections(k, d, mask, qp, kp, v_tok, v_ext)
        windowed_attention(k, qp, kp, v_tok, v_ext, mask)
        gated_ffn(k, d, qp)


def windowed_projections(k, d, mask, qp, kp, v_tok, v_ext):
    nc = k.nc
    with ExitStack() as lctx:
        sb, _, _ = scope_tools(k, lctx)
        w_qkv = sb("w_qkv", [P, 3 * H * DH])
        w_swap = sb("w_swap", [P, 2 * H * DH])
        cos = sb("cos", [P, N])
        sin = sb("sin", [P, N])
        xn = sb("x_normed", [P, N])
        t1 = sb("t1", [P, N])
        t2 = sb("t2", [P, N])
        pool = sb("pooled", [P, 4])
        mem_tok = sb("mem_token", [P, 16])
        with ExitStack() as ctx:
            _, _, sem = scope_tools(k, ctx)
            loaded = [sem("loaded") for _ in range(7)]
            block = open_phase(k, ctx)

            @block.sync
            def _(sp):
                for i, (dst, src) in enumerate([
                        (w_qkv[:], d["w_qkv"]), (w_swap[:], d["w_swap"]), (cos[:], d["cos"]), (sin[:], d["sin"]),
                        (mask[:], d["window_mask"]), (kp[:, :, 16:NEX], d["persist_k"]),
                        (v_ext[16:NEX, :], d["persist_v"])]):
                    sp.dma_start(dst, src).then_inc(loaded[i], 16)
                for s in loaded:
                    sp.wait_ge(s, 16)

        steps(k, "vector", [
            lambda e: e.reduce_sum(pool[:, 0:1], k.ctx_t[:, 0:M], AX.X),
            lambda e: e.tensor_scalar(pool[:, 1:2], pool[:, 0:1], 1.0 / M, None, ALU.mult)])
        rms_norm(k, pool[:, 1:2], k.v["L0_xattn_mem_pool_norm_w"], pool[:, 0:1], pool[:, 2:3], pool[:, 3:4], n=1)
        linear(k, [(P, 1, [(k.w["L0_xattn_to_mem_tokens_w"], pool[:, 0:1])])],
               lambda e, n, b: e.tensor_copy(mem_tok[:], b.to_broadcast([P, 16])))
        rms_norm(k, k.x[:], k.v["L0_xattn_attn_norm_w"], xn[:], t1[:], t2[:])

        linear(k, [(P, 16, [(w_qkv[:, H * DH + P * p:H * DH + P * (p + 1)], mem_tok[:])]) for p in range(H // 2)],
               lambda e, n, b: e.tensor_copy(kp[:, n, 0:16], b))
        linear(k, [(16, HALF, [(mem_tok[:], w_qkv[:, 2 * H * DH + HALF * c:2 * H * DH + HALF * (c + 1)])])
                   for c in range(2)],
               lambda e, n, b: e.tensor_copy(v_ext[0:16, HALF * n:HALF * (n + 1)], b))
        linear(k, [(P, HALF, [(xn[:, P * t:P * (t + 1)],
                               w_qkv[:, 2 * H * DH + HALF * c:2 * H * DH + HALF * (c + 1)])])
                   for t in range(QT) for c in range(2)],
               lambda e, n, b: e.activation(v_tok[:, n // 2, HALF * (n % 2):HALF * (n % 2 + 1)], b, ACT.Copy),
               on="scalar")
        project_rotary(k, w_qkv, w_swap, xn, cos, sin, qp, kp)


def project_rotary(k, w_qkv, w_swap, xn, cos, sin, qp, kp):
    nc = k.nc
    jobs = [(kind, p, c) for p in range(H // 2) for kind in range(2) for c in range(2)]
    with ExitStack() as ctx:
        sb, ps, sem = scope_tools(k, ctx)
        plain = [ps("plain", [P, HALF]) for _ in range(2)]
        swapped = [ps("swapped", [P, HALF]) for _ in range(2)]
        by_cos = sb("by_cos", [P, 2, HALF])
        by_sin = sb("by_sin", [P, 2, HALF])
        projected = sem("projected")
        turned = sem("turned")
        summed = sem("summed")
        block = open_phase(k, ctx)

        @block.tensor
        def _(pe):
            for n, (kind, p, c) in enumerate(jobs):
                if n >= 2:
                    pe.wait_ge(turned, 2 * (n - 1))
                o = kind * H * DH + P * p
                pe.matmul(plain[n % 2][:], w_qkv[:, o:o + P], cols(xn, c), start=True, stop=True)
                pe.matmul(swapped[n % 2][:], w_swap[:, o:o + P], cols(xn, c), start=True, stop=True)\
                    .then_inc(projected, 1)

        @block.vector
        def _(dve):
            for n, (kind, p, c) in enumerate(jobs):
                dve.wait_ge(projected, n + 1)
                if n >= 2:
                    dve.wait_ge(summed, n - 1)
                dve.tensor_tensor(by_cos[:, n % 2, :], plain[n % 2][:], cols(cos, c), ALU.mult).then_inc(turned, 1)
                dve.tensor_tensor(by_sin[:, n % 2, :], swapped[n % 2][:], cols(sin, c), ALU.mult).then_inc(turned, 1)

        @block.gpsimd
        def _(pool):
            for n, (kind, p, c) in enumerate(jobs):
                pool.wait_ge(turned, 2 * (n + 1))
                out = qp[:, p, HALF * c:HALF * (c + 1)] if kind == 0 else kp[:, p, NEX + HALF * c:NEX + HALF * (c + 1)]
                pool.tensor_tensor(out, by_cos[:, n % 2, :], by_sin[:, n % 2, :], ALU.add).then_inc(summed, 1)


def windowed_attention(k, qp, kp, v_tok, v_ext, mask):
    nc = k.nc
    with ExitStack() as ctx:
        sb, ps, sem = scope_tools(k, ctx)
        score = ps("score", [P, QT, 256])
        pt_tok = ps("pt_tokens", [P, HALF])
        pt_ext = ps("pt_extra", [P, HALF])
        o_bank = [ps("o", [P, HALF]) for _ in range(2)]
        sm = sb("masked", [P, 2, QT, WK])
        pr = sb("probs", [P, QT, WK])
        pn = sb("probs_normed", [P, 2, QT, WK])
        nmax = sb("neg_max", [P, 2, QT])
        tot = sb("total", [P, 2, QT])
        inv = sb("inverse", [P, 2, QT])
        ptt = sb("pt_tokens_s", [P, 2, HALF])
        pte = sb("pt_extra_s", [NEX, 2, HALF])
        scores_ready = sem("scores_ready")
        masked_ready = sem("masked_ready")
        max_ready = sem("max_ready")
        exp_ready = sem("exp_ready")
        inv_ready = sem("inv_ready")
        probs_ready = sem("probs_ready")
        turned = sem("turned")
        turned_copied = sem("turned_copied")
        o_ready = sem("o_ready")
        o_copied = sem("o_copied")
        block = open_phase(k, ctx)

        @block.tensor
        def _(pe):
            def scores(h):
                r = slice(DH * (h % 2), DH * (h % 2 + 1))
                if h >= 1:
                    pe.wait_ge(masked_ready, h)
                for t in range(QT):
                    q = qp[r, h // 2, P * t:P * (t + 1)]
                    pe.matmul(score[:, t, 0:NEX], q, kp[r, h // 2, 0:NEX], start=True, stop=True)
                    mm = pe.matmul(score[:, t, NEX:WK], q, kp[r, h // 2, NEX + P * t:NEX + P * (t + 1)],
                                   start=True, stop=True)
                mm.then_inc(scores_ready, 1)

            def values(h):
                rows = slice(DH * (h % 2), DH * (h % 2 + 1))
                for c in range(2):
                    n = 2 * h + c
                    if n == 0 or c == 0:
                        pe.wait_ge(probs_ready, h + 1)
                    if n >= 1:
                        pe.wait_ge(turned_copied, 2 * n)
                    for t in range(4):
                        pe.transpose(pt_tok[:, P * t:P * (t + 1)], pn[:, h % 2, 4 * c + t, NEX:WK], k.ident[:])
                        mm = pe.transpose(pt_ext[0:NEX, P * t:P * (t + 1)], pn[:, h % 2, 4 * c + t, 0:NEX], k.ident[:])
                    mm.then_inc(turned, 1)
                    pe.wait_ge(turned_copied, 2 * (n + 1))
                    if h >= 2 and h % 2 == 0 and c == 0:
                        pe.wait_ge(o_copied, h // 2)
                    for t in range(4):
                        out = o_bank[c][rows, P * t:P * (t + 1)]
                        pe.matmul(out, v_tok[:, 4 * c + t, DH * h:DH * (h + 1)], ptt[:, n % 2, P * t:P * (t + 1)],
                                  start=True, stop=False)
                        mm = pe.matmul(out, v_ext[:, DH * h:DH * (h + 1)], pte[:, n % 2, P * t:P * (t + 1)],
                                       start=False, stop=True)
                    mm.then_inc(o_ready, 1)

            scores(0)
            for h in range(H):
                if h + 1 < H:
                    scores(h + 1)
                values(h)

        @block.vector
        def _(dve):
            m3 = mask[:].unsqueeze(1).to_broadcast([P, QT, WK])

            def finish(h):
                dve.wait_ge(exp_ready, QT * (h + 1))
                dve.reciprocal(inv[:, h % 2, :], tot[:, h % 2, :]).then_inc(inv_ready, 1)
                dve.wait_ge(inv_ready, h + 1)
                if h >= 2:
                    dve.wait_ge(turned, 2 * (h - 1))
                dve.tensor_tensor(pn[:, h % 2, :, :], pr[:], inv[:, h % 2, :].unsqueeze(2).to_broadcast([P, QT, WK]),
                                  ALU.mult).then_inc(probs_ready, 1)
                if h >= 2 and h % 2 == 0:
                    pair_out(h // 2 - 1)

            def pair_out(p):
                dve.wait_ge(o_ready, 4 * (p + 1))
                dve.tensor_copy(qp[:, p, 0:HALF], o_bank[0][:])
                dve.tensor_copy(qp[:, p, HALF:N], o_bank[1][:]).then_inc(o_copied, 1)

            for h in range(H):
                dve.wait_ge(scores_ready, h + 1)
                dve.scalar_tensor_tensor(out=sm[:, h % 2, :, :], in0=score[:, :, 0:WK], scalar=float(DH) ** -0.5,
                                         in1=m3, op0=ALU.mult, op1=ALU.add).then_inc(masked_ready, 1)
                dve.wait_ge(masked_ready, h + 1)
                dve.tensor_reduce(nmax[:, h % 2, :], sm[:, h % 2, :, :], AX.X, ALU.max, negate=True)\
                   .then_inc(max_ready, 1)
                if h >= 1:
                    finish(h - 1)
            finish(H - 1)
            pair_out(H // 2 - 1)

        @block.scalar
        def _(act):
            def exps(h):
                act.wait_ge(max_ready, h + 1)
                if h >= 1:
                    act.wait_ge(probs_ready, h)
                for t in range(QT):
                    act.activation(pr[:, t, :], sm[:, h % 2, t, :], ACT.Exp, bias=nmax[:, h % 2, t:t + 1],
                                   accum_out=tot[:, h % 2, t:t + 1]).then_inc(exp_ready, 1)

            def copies(h):
                for c in range(2):
                    n = 2 * h + c
                    act.wait_ge(turned, n + 1)
                    if n >= 2:
                        act.wait_ge(o_ready, n - 1)
                    act.activation(ptt[:, n % 2, :], pt_tok[:], ACT.Copy).then_inc(turned_copied, 1)
                    act.activation(pte[:, n % 2, :], pt_ext[0:NEX, :], ACT.Copy).then_inc(turned_copied, 1)

            for h in range(H):
                exps(h)
                if h >= 1:
                    copies(h - 1)
            copies(H - 1)


def gated_ffn(k, d, o_pairs):
    nc = k.nc
    with ExitStack() as lctx:
        sb, _, _ = scope_tools(k, lctx)
        w_o = sb("w_o", [P, H * DH // P, C])
        w1 = sb("w1", [P, 2 * DFF])
        w2 = sb("w2", [P, 3, C])
        b1 = sb("b1", [P, 6])
        t1, t2, xn = sb("t1", [P, N]), sb("t2", [P, N]), sb("x_normed", [P, N])
        gate = sb("gate", [P, 3, N])
        sig = sb("sigmoid", [P, 3, N])
        with ExitStack() as ctx:
            _, _, sem = scope_tools(k, ctx)
            loaded = [sem("loaded") for _ in range(4)]
            block = open_phase(k, ctx)

            @block.sync
            def _(sp):
                for i, (dst, src) in enumerate([
                        (w_o[:], d["w_out0"].rearrange("(p r) n -> r p n", r=P)), (w1[:], d["ff_w1_0"]),
                        (w2[:], d["ff_w2_0"].rearrange("(g r) n -> r g n", r=P)), (b1[:], d["ff_b1_0"])]):
                    sp.dma_start(dst, src).then_inc(loaded[i], 16)
                for s in loaded:
                    sp.wait_ge(s, 16)

        linear(k, [(P, HALF, [(w_o[:, p, :], o_pairs[:, p, HALF * c:HALF * (c + 1)]) for p in range(H // 2)])
                   for c in range(2)],
               lambda e, n, b: e.tensor_tensor(cols(k.x, n), b, cols(k.x, n), ALU.add))
        rms_norm(k, k.x[:], k.v["L0_xattn_ff_norm_w"], xn[:], t1[:], t2[:])
        jobs = [(g, c) for g in range(3) for c in range(2)]
        linear(k, [(FFT[g][1], HALF, [(w1[:, DFF + FFT[g][0]:DFF + FFT[g][0] + FFT[g][1]], cols(xn, c))])
                   for g, c in jobs],
               lambda e, n, b: e.tensor_scalar(gate[0:b.shape[0], jobs[n][0], HALF * jobs[n][1]:HALF * (jobs[n][1] + 1)],
                                               b, b1[0:b.shape[0], 3 + jobs[n][0]:4 + jobs[n][0]], None, ALU.add))
        for g in range(3):
            r = FFT[g][1]
            steps(k, "scalar", [lambda e: e.activation(sig[0:r, g, :], gate[0:r, g, :], ACT.Exp, scale=-1.0)])
        for g in range(3):
            r = FFT[g][1]
            steps(k, "vector", [
                lambda e: e.tensor_scalar(sig[0:r, g, :], sig[0:r, g, :], 1.0, None, ALU.add),
                lambda e: e.reciprocal(sig[0:r, g, :], sig[0:r, g, :]),
                lambda e: e.tensor_tensor(gate[0:r, g, :], gate[0:r, g, :], sig[0:r, g, :], ALU.mult)])
        linear(k, [(FFT[g][1], HALF, [(w1[:, FFT[g][0]:FFT[g][0] + FFT[g][1]], cols(xn, c))]) for g, c in jobs],
               lambda e, n, b: e.scalar_tensor_tensor(
                   out=sig[0:b.shape[0], jobs[n][0], HALF * jobs[n][1]:HALF * (jobs[n][1] + 1)], in0=b,
                   scalar=b1[0:b.shape[0], jobs[n][0]:jobs[n][0] + 1],
                   in1=gate[0:b.shape[0], jobs[n][0], HALF * jobs[n][1]:HALF * (jobs[n][1] + 1)],
                   op0=ALU.add, op1=ALU.mult))
        linear(k, [(P, HALF, [(w2[0:FFT[g][1], g, :], sig[0:FFT[g][1], g, HALF * c:HALF * (c + 1)]) for g in range(3)])
                   for c in range(2)],
               lambda e, n, b: e.scalar_tensor_tensor(out=cols(k.x, n), in0=b, scalar=k.v["L0_xattn_ff_b2"],
                                                      in1=cols(k.x, n), op0=ALU.add, op1=ALU.add))


def query_terms(k, src, w, bias, qb, q_terms):
    nc = k.nc
    with ExitStack() as lctx:
        sb, _, _ = scope_tools(k, lctx)
        qf = sb("q", [P, N])
        rest = sb("q_rest", [P, N])
        part = [sb("q_part", [P, N], BF16) for _ in range(3)]
        if bias is None:
            linear(k, halves(P, w, src), lambda e, n, b: e.tensor_scalar(cols(qf, n), b, float(SCALE), None, ALU.mult))
        else:
            linear(k, halves(P, w, src),
                   lambda e, n, b: e.tensor_scalar(cols(qf, n), b, bias, float(SCALE), ALU.add, ALU.mult))
        steps(k, "vector", [
            lambda e: e.memset(qb[32:NR + 1, :], 0.0),
            lambda e: e.tensor_copy(part[0][:], qf[:]),
            lambda e: e.tensor_tensor(rest[:], qf[:], part[0][:], ALU.subtract),
            lambda e: e.tensor_copy(part[1][:], rest[:]),
            lambda e: e.tensor_tensor(part[2][:], rest[:], part[1][:], ALU.subtract)])
        with ExitStack() as ctx:
            _, _, sem = scope_tools(k, ctx)
            stored = [sem("stored") for _ in range(NTERM)]
            fetched = sem("fetched")
            block = open_phase(k, ctx)

            @block.sync
            def _(sp):
                for t in range(NTERM):
                    sp.dma_start(q_terms[:, t].rearrange("h d n -> h d n"),
                                 part[Q_PARTS[t]][:]).then_inc(stored[t], 16)
                for t in range(NTERM):
                    sp.wait_ge(stored[t], 16)
                sp.dma_start(qb[0:NR, :].rearrange("r (h n) -> r h n", h=H),
                             q_terms.rearrange("h t d n -> (t d) h n")).then_inc(fetched, 16)
                sp.wait_ge(fetched, 16)


def key_value_terms(k, src, tk, ni, wk, bk, wv, bv_row, k_terms, vb, pad):
    nc = k.nc
    cw = TPI * tk
    with ExitStack() as ctx:
        sb, ps, sem = scope_tools(k, ctx)
        kps = [ps("k_product", [P, HALF]) for _ in range(2)]
        vps = [ps("v_product", [P, HALF]) for _ in range(2)]
        kf = sb("k", [P, 2, HALF])
        kr = sb("k_rest", [P, 2, HALF])
        kpart = sb("k_part", [P, 3, 2, HALF], BF16)
        vf = sb("v", [P, 2, HALF])
        vr = sb("v_rest", [P, 2, HALF])
        vbias = sb("v_bias", [P, TPI, C])
        k_product = sem("k_product")
        v_product = sem("v_product")
        k_out = sem("k_out")
        k_high = sem("k_high")
        k_rest = sem("k_rest")
        k_mid = sem("k_mid")
        k_low = sem("k_low")
        v_out = sem("v_out")
        v_high = sem("v_high")
        v_rest = sem("v_rest")
        v_mid = sem("v_mid")
        v_low = sem("v_low")
        ones = sem("ones")
        bias_loaded = sem("bias_loaded")
        stored = [sem("stored") for _ in range(NTERM)]
        block = open_phase(k, ctx)
        kd = [k_terms[:, t].rearrange("h d n -> h d n") for t in range(NTERM)]

        def v_slot(c, lo):
            return vb[0:tk, :, TPI * c:TPI * (c + 1), lo:lo + HD].rearrange("p h t d -> p t h d")

        def split4(a):
            return a.rearrange("p (t h d) -> p t h d", t=TPI, h=H)

        @block.sync
        def _(sp):
            if bv_row is not None:
                for t in range(TPI):
                    sp.dma_start(vbias[:, t, :], bv_row.partition_broadcast(P)).then_inc(bias_loaded, 16)
            for c in range(ni):
                for t in range(NTERM):
                    part = K_PARTS[t]
                    sp.wait_ge((k_high, k_mid, k_low)[part], c + 1)
                    if c >= 1:
                        sp.wait_ge(stored[t], 16 * c)
                    sp.dma_start(kd[t][:, :, cw * c:cw * (c + 1)], kpart[:, part, c % 2, 0:cw])\
                      .then_inc(stored[t], 16)
            for t in range(NTERM):
                sp.wait_ge(stored[t], 16 * ni)

        @block.tensor
        def _(pe):
            for c in range(ni):
                if c >= 2:
                    pe.wait_ge(k_out, c - 1)
                    pe.wait_ge(v_out, c - 1)
                pe.matmul(kps[c % 2][:, 0:cw], wk, src[:, cw * c:cw * (c + 1)], start=True, stop=True)\
                  .then_inc(k_product, 1)
                for t in range(TPI):
                    o = cw * c + tk * t
                    mm = pe.matmul(vps[c % 2][0:tk, C * t:C * (t + 1)], src[:, o:o + tk], wv, start=True, stop=True)
                mm.then_inc(v_product, 1)

        @block.scalar
        def _(act):
            for c in range(ni):
                b = c % 2
                act.wait_ge(k_product, c + 1)
                if c >= 2:
                    act.wait_ge(k_rest, c - 1)
                if bk is None:
                    act.activation(kf[:, b, 0:cw], kps[b][:, 0:cw], ACT.Copy).then_inc(k_out, 1)
                else:
                    act.activation(kf[:, b, 0:cw], kps[b][:, 0:cw], ACT.Identity, bias=bk).then_inc(k_out, 1)
                act.wait_ge(v_out, c + 1)
                act.activation(v_slot(c, 0), split4(vf[0:tk, b, :]), ACT.Copy).then_inc(v_high, 1)
                act.wait_ge(v_rest, c + 1)
                act.activation(v_slot(c, HD + 1), split4(vr[0:tk, b, :]), ACT.Copy).then_inc(v_mid, 1)

        @block.vector
        def _(dve):
            dve.memset(vb[0:tk, :, 0:TPI * ni, HD:HD + 1], 1.0).then_inc(ones, 1)
            if bv_row is None:
                dve.memset(vbias[:], 0.0).then_inc(ones, 1)
                dve.wait_ge(ones, 2)
            else:
                dve.wait_ge(bias_loaded, 16 * TPI)
            for c in range(ni):
                b = c % 2
                dve.wait_ge(v_product, c + 1)
                if c >= 2:
                    dve.wait_ge(v_rest, c - 1)
                    dve.wait_ge(v_high, c - 1)
                dve.tensor_tensor(vf[0:tk, b, :], vps[b][0:tk, :], vbias[0:tk].rearrange("p t n -> p (t n)"), ALU.add)\
                   .then_inc(v_out, 1)
                dve.wait_ge(k_out, c + 1)
                if c >= 2:
                    for t in range(NTERM):
                        dve.wait_ge(stored[t], 16 * (c - 1))
                dve.tensor_copy(kpart[:, 0, b, 0:cw], kf[:, b, 0:cw]).then_inc(k_high, 1)
                dve.wait_ge(k_high, c + 1)
                dve.tensor_tensor(kr[:, b, 0:cw], kf[:, b, 0:cw], kpart[:, 0, b, 0:cw], ALU.subtract).then_inc(k_rest, 1)
                dve.wait_ge(k_rest, c + 1)
                dve.tensor_copy(kpart[:, 1, b, 0:cw], kr[:, b, 0:cw]).then_inc(k_mid, 1)
                dve.wait_ge(k_mid, c + 1)
                dve.tensor_tensor(kpart[:, 2, b, 0:cw], kr[:, b, 0:cw], kpart[:, 1, b, 0:cw], ALU.subtract)\
                   .then_inc(k_low, 1)

        @block.gpsimd
        def _(pool):
            for c in range(ni):
                b = c % 2
                pool.wait_ge(v_high, c + 1)
                if c >= 2:
                    pool.wait_ge(v_low, c - 1)
                pool.tensor_tensor(split4(vr[0:tk, b, :]), split4(vf[0:tk, b, :]), v_slot(c, 0), ALU.subtract)\
                    .then_inc(v_rest, 1)
                pool.wait_ge(v_mid, c + 1)
                pool.tensor_tensor(v_slot(c, 2 * HD + 1), split4(vr[0:tk, b, :]), v_slot(c, HD + 1), ALU.subtract)\
                    .then_inc(v_low, 1)

    if pad:
        last = vb[0:tk, :, TPI * ni - 1, :]
        steps(k, "vector", [lambda e: e.tensor_scalar(last, last, k.last_rows[0:tk, :], None, ALU.mult)])


def wide_attention(k, tk, ni, kb, qb, vb, k_terms, o_raw, mask=None):
    nc = k.nc
    cw = TPI * tk
    nk = cw * ni
    with ExitStack() as ctx:
        sb, ps, sem = scope_tools(k, ctx)
        sc_bank = [ps("scores", [P, HALF]) for _ in range(2)]
        mx_bank = [ps("max_scores", [P, 2, HALF]) for _ in range(2)]
        acc = ps("values_sum", [P, HALF])
        small = ps("small", [P, HALF])
        pr = sb("probs", [P, 2 * TPI, HALF])
        pr_low = sb("probs_low", [P, 2 * TPI, HALF], BF16)
        mx = sb("chunk_max", [P, 2 * ni * QT])
        nmax = sb("neg_max", [P, QT])
        nmax_t = sb("neg_max_rows", [QT, P], BF16)

        keys_loaded = sem("keys_loaded")
        scores_ready = sem("scores_ready")
        exp_ready = sem("exp_ready")
        low_pool = sem("low_pool")
        low_dve = sem("low_dve")
        tile_used = sem("tile_used")
        max_scores = sem("max_scores")
        max_taken = sem("max_taken")
        head_max = sem("head_max")
        max_turned = sem("max_turned")
        max_rows = sem("max_rows")
        max_in_q = sem("max_in_q")
        acc_ready = sem("acc_ready")
        acc_taken = sem("acc_taken")
        block = open_phase(k, ctx)

        pr_words = pr[:].bitcast(BF16).rearrange("p s (n two) -> p s n two", two=2)

        def high(slot, a, b):
            return pr_words[0:tk, slot, a:b, 1]

        def phases(h, last_head):
            return [(0, True, ni == 1, False)] + ([("loop", False, False, True)] if ni > 2 else []) + \
                [(ni - 1, False, True, False)]

        def run(eng, body):
            def head(h, **kw):
                for i, first, last, looped in phases(h, False):
                    if looped:
                        with eng.Fori(1, ni - 1) as i:
                            body(h, i, first, last, **kw)
                    else:
                        body(h, i, first, last, **kw)
            head(0, ahead=True)
            with eng.Fori(1, H - 2) as h:
                head(h, ahead=True)
            head(H - 2, ahead=True)
            head(H - 1, ahead=False)

        def ends(h):
            return isinstance(h, int) and h == H - 2

        @block.sync
        def _(sp):
            def values_of(h):
                keep = (lambda x: x) if isinstance(h, int) else sp.snap
                return keep(h + 1), [keep(h * N + t * P) for t in range(QT)]

            def load(h, at):
                sp.dma_start(kb[0:NR, bass.ds(at, nk)],
                             k_terms[bass.ds(h, 1)].rearrange("o t d n -> (o t d) n")).then_inc(keys_loaded, 16)

            def max_row(rows_wanted, at):
                sp.wait_ge(max_rows, rows_wanted)
                for t in range(QT):
                    sp.dma_start(qb[NR:NR + 1, bass.ds(at[t], P)], nmax_t[t:t + 1, :]).then_inc(max_in_q, 16)

            for h in range(KRING):
                load(h, h * MP)
                sp.wait_ge(keys_loaded, 16 * (h + 1))
            max_row(*values_of(0))
            max_row(*values_of(1))
            with sp.Fori(KRING, H) as h:
                at = sp.snap((h % KRING) * MP)
                scored = sp.snap((h - KRING + 1) * (2 * TPI * ni))
                row = values_of(h - 1)
                sp.wait_ge(scores_ready, scored)
                load(h, at)
                max_row(*row)
            max_row(*values_of(H - 1))
            sp.wait_ge(max_in_q, ROW_DMAS * H)

        @block.tensor
        def _(pe):
            def max_chunk(h, i, n0, units):
                kof = pe.snap((h % KRING) * MP + i * cw)
                qof = pe.snap(h * N)
                for u in units:
                    n = n0 + u
                    if not (isinstance(n, int) and n < 2):
                        pe.wait_ge(max_taken, n - 1)
                    for v in range(2):
                        t = 2 * u + v
                        out = mx_bank[u % 2][:, v, 0:cw]
                        mm = pe.matmul(out, qb[:, bass.ds(qof + t * P, P)], kb[:, bass.ds(kof, cw)],
                                       start=True, stop=mask is None)
                        if mask is not None:
                            mm = pe.matmul(out, k.ident_b[:], mask[0][:, bass.ds(i * cw + t * nk, cw)],
                                           start=False, stop=True)
                    mm.then_inc(max_scores, 1)

            def values(g, h_last, first_tile, last_tile, j):
                pe.wait_ge(low_pool, g + 1)
                pe.wait_ge(low_dve, g + 1)
                vof = pe.snap(g * VC)
                for t in range(QT):
                    slot = 2 * j + t // 4
                    a = P * (t % 4)
                    out = acc[:, VC * t:VC * (t + 1)]
                    v = vb[0:tk].rearrange("p h t c -> p (h t c)")[:, bass.ds(vof, VC)]
                    pe.matmul(out, high(slot, a, a + P), v, start=(first_tile and t == 0), stop=False,
                              skip_group_check=True)
                    mm = pe.matmul(out, pr_low[0:tk, slot, a:a + P], v, start=False, stop=last_tile,
                                   skip_group_check=True)
                mm.then_inc(tile_used, 1)
                return mm

            def body(h, i, first, last, ahead):
                g = pe.snap(h * ni + i) if not (isinstance(h, int) and isinstance(i, int)) else h * ni + i
                kof = pe.snap((h % KRING) * MP + i * cw)
                qof = pe.snap(h * N)
                if first:
                    pe.wait_ge(max_in_q, h * ROW_DMAS + ROW_DMAS)
                for j in range(TPI):
                    for c in range(2):
                        n = 2 * TPI * g + 2 * j + c
                        if not (isinstance(n, int) and n < 2):
                            pe.wait_ge(exp_ready, n - 1)
                        mm = pe.matmul(sc_bank[c][0:tk, :], kb[:, bass.ds(kof + j * tk, tk)],
                                       qb[:, bass.ds(qof + c * HALF, HALF)], start=True, stop=mask is None)
                        if mask is not None:
                            mm = pe.matmul(sc_bank[c][0:tk, :], k.ident_b[:],
                                           mask[1][:, bass.ds((i * TPI + j) * N + c * HALF, HALF)],
                                           start=False, stop=True)
                        mm.then_inc(scores_ready, 1)
                    if ahead and not (last and ends(h)):
                        if last:
                            if j == 0:
                                pe.wait_ge(keys_loaded, 16 * (h + 3))
                            max_chunk(h + 2, 0, TPI * (g + ni + 1), [j])
                        else:
                            max_chunk(h + 1, i + 1, TPI * (g + ni + 1), [j])
                    if last and ahead and j == 2:
                        turn_max(h + 1)
                    if j >= 1:
                        if first and j == 1 and not (isinstance(h, int) and h == 0):
                            pe.wait_ge(acc_taken, h)
                        values(TPI * g + j - 1, h, first and j == 1, False, j - 1)
                    elif not (first and isinstance(h, int) and h == 0):
                        mm = values(TPI * g - 1, h, False, first, TPI - 1)
                        if first:
                            tail_signal(pe)

            def turn_max(h):
                pe.wait_ge(head_max, h + 1)
                pe.transpose(small[0:QT, 0:P], nmax[:], k.ident[:]).then_inc(max_turned, 1)

            def tail_signal(pe):
                pe.matmul(small[0:QT, 256:257], k.ident_b[:, 0:QT], k.ident_b[:, 0:1], start=True, stop=True)\
                  .then_inc(acc_ready, 1)

            for h, i in [(0, i) for i in range(ni)] + [(1, 0)]:
                if i == 0:
                    pe.wait_ge(keys_loaded, 16 * (h + 1))
                max_chunk(h, i, TPI * (h * ni + i), range(TPI))
            turn_max(0)
            run(pe, body)
            values(TPI * ni * H - 1, H - 1, False, True, TPI - 1)
            tail_signal(pe)

        @block.scalar
        def _(act):
            def body(h, i, first, last, ahead):
                g = h * ni + i
                g = g if isinstance(g, int) else act.snap(g)
                for j in range(TPI):
                    tile = TPI * g + j
                    for c in range(2):
                        act.wait_ge(scores_ready, 2 * TPI * g + 2 * j + c + 1)
                        if c == 0 and not (isinstance(tile, int) and tile < TPI):
                            act.wait_ge(tile_used, tile - TPI + 1)
                        act.activation(pr[0:tk, 2 * j + c, :], sc_bank[c][0:tk, :], ACT.Exp).then_inc(exp_ready, 1)
            run(act, body)

        @block.gpsimd
        def _(pool):
            def body(h, i, first, last, ahead):
                g = h * ni + i
                g = g if isinstance(g, int) else pool.snap(g)
                for j in range(TPI):
                    pool.wait_ge(exp_ready, 2 * TPI * g + 2 * j + 1)
                    pool.tensor_tensor(pr_low[0:tk, 2 * j, :], pr[0:tk, 2 * j, :], high(2 * j, 0, HALF), ALU.subtract)\
                        .then_inc(low_pool, 1)
            run(pool, body)

        @block.vector
        def _(dve):
            def take_max(n, slot, i, u):
                dve.wait_ge(max_scores, n + 1)
                dve.tensor_reduce(mx[:, bass.ds(slot * (ni * QT) + i * QT + 2 * u, 2)], mx_bank[u % 2][:, :, 0:cw],
                                  AX.X, ALU.max).then_inc(max_taken, 1)

            def head_maximum(h, taken):
                dve.wait_ge(max_taken, taken)
                if not (isinstance(h, int) and h == 0):
                    dve.wait_ge(max_turned, h)
                slot = h % 2 if isinstance(h, int) else dve.snap(h % 2)
                dve.tensor_reduce(nmax[:], mx[:, bass.ds(slot * (ni * QT), ni * QT)].rearrange("p (i t) -> p t i", t=QT),
                                  AX.X, ALU.max, negate=True).then_inc(head_max, 1)

            def max_to_rows(h):
                dve.wait_ge(max_turned, h + 1)
                if not (isinstance(h, int) and h == 0):
                    dve.wait_ge(max_in_q, h * ROW_DMAS)
                dve.tensor_copy(nmax_t[:], small[0:QT, 0:P]).then_inc(max_rows, 1)

            def take_acc(h):
                dve.wait_ge(acc_ready, h + 1)
                dve.tensor_copy(o_raw[:, bass.ds(h * (QT * VC), QT * VC)], acc[:, 0:QT * VC]).then_inc(acc_taken, 1)

            def body(h, i, first, last, ahead):
                g = h * ni + i
                g = g if isinstance(g, int) else dve.snap(g)
                if last and ahead:
                    head_maximum(h + 1, TPI * (g + ni + 1))
                for j in range(TPI):
                    if ahead and not (last and ends(h)):
                        hm, im = (h + 2, 0) if last else (h + 1, i + 1)
                        slot = hm % 2 if isinstance(hm, int) else dve.snap(hm % 2)
                        take_max(TPI * (g + ni + 1) + j, slot, im, j)
                    if first and j == 1 and not (isinstance(h, int) and h == 0):
                        take_acc(h - 1)
                    if last and ahead and j == 3:
                        max_to_rows(h + 1)
                    dve.wait_ge(exp_ready, 2 * TPI * g + 2 * j + 2)
                    dve.tensor_tensor(pr_low[0:tk, 2 * j + 1, :], pr[0:tk, 2 * j + 1, :], high(2 * j + 1, 0, HALF),
                                      ALU.subtract).then_inc(low_dve, 1)

            for h, i in [(0, i) for i in range(ni)] + [(1, 0)]:
                for u in range(TPI):
                    take_max(TPI * (h * ni + i) + u, h, i, u)
            head_maximum(0, TPI * ni)
            max_to_rows(0)
            run(dve, body)
            take_acc(H - 1)


def normalised_output(k, o_raw, out_t, any_key=None):
    nc = k.nc
    with ExitStack() as lctx:
        sb, _, _ = scope_tools(k, lctx)
        o = sb("o", [P, H, QT, HD])
        oq = sb("o_query_major", [P, QT, C])
        inv = sb("inverse", [P, H, QT])
        v = o_raw[:].rearrange("p (h t c) -> p h t c", h=H, t=QT)
        total = v[:, :, :, HD]
        fns = []
        if any_key is not None:
            seen = any_key[:].unsqueeze(1).to_broadcast([P, H, QT])
            fns.append(lambda e: e.tensor_tensor(total, total, seen, ALU.mult))
        fns.append(lambda e: e.reciprocal(inv[:], total))
        if any_key is not None:
            fns.append(lambda e: e.tensor_tensor(inv[:], inv[:], seen, ALU.mult))
        fns += [
            lambda e: e.tensor_tensor(o[:], v[:, :, :, HD + 1:2 * HD + 1], v[:, :, :, 2 * HD + 1:VC], ALU.add),
            lambda e: e.tensor_tensor(o[:], o[:], v[:, :, :, 0:HD], ALU.add),
            lambda e: e.tensor_tensor(oq[:].rearrange("p t (h d) -> p h t d", h=H), o[:],
                                      inv[:].unsqueeze(3).to_broadcast([P, H, QT, HD]), ALU.mult)]
        steps(k, "vector", fns)
        with ExitStack() as ctx:
            _, ps, sem = scope_tools(k, ctx)
            bank = [ps("turned", [P, HALF]) for _ in range(2)]
            turned = sem("turned")
            copied = sem("copied")
            block = open_phase(k, ctx)

            @block.tensor
            def _(pe):
                for t in range(QT):
                    pe.transpose(bank[t // 4][:, P * (t % 4):P * (t % 4 + 1)], oq[:, t, :], k.ident[:])\
                      .then_inc(turned, 1)

            @block.scalar
            def _(act):
                for c in range(2):
                    act.wait_ge(turned, 4 * (c + 1))
                    act.activation(out_t[:, HALF * c:HALF * (c + 1)], bank[c][:], ACT.Copy).then_inc(copied, 1)


def ffn(k, x_in, w1_d, b1_d, w2_d, b2, gelu):
    nc = k.nc
    with ExitStack() as lctx:
        sb, _, _ = scope_tools(k, lctx)
        w1 = sb("w1", [P, FF])
        w2 = sb("w2", [P, FF // P, C])
        b1 = sb("b1", [P, FF // P])
        hid = sb("hidden", [P, FF // P, N])
        with ExitStack() as ctx:
            _, _, sem = scope_tools(k, ctx)
            loaded = [sem("loaded") for _ in range(3)]
            block = open_phase(k, ctx)

            @block.sync
            def _(sp):
                for i, (dst, src) in enumerate([(w1[:], w1_d), (w2[:], w2_d.rearrange("(g r) n -> r g n", r=P)),
                                                (b1[:], b1_d)]):
                    sp.dma_start(dst, src).then_inc(loaded[i], 16)
                for s in loaded:
                    sp.wait_ge(s, 16)

        jobs = [(g, c) for c in range(2) for g in range(FF // P)]
        fn = ACT.Gelu_apprx_tanh if gelu else ACT.Relu
        linear(k, [(P, HALF, [(w1[:, P * g:P * (g + 1)], cols(x_in, c))]) for g, c in jobs],
               lambda e, n, b: e.activation(hid[:, jobs[n][0], HALF * jobs[n][1]:HALF * (jobs[n][1] + 1)], b, fn,
                                            bias=b1[:, jobs[n][0]:jobs[n][0] + 1]), on="scalar")
        linear(k, [(P, HALF, [(w2[:, g, :], hid[:, g, HALF * c:HALF * (c + 1)]) for g in range(FF // P)])
                   for c in range(2)],
               lambda e, n, b: e.scalar_tensor_tensor(out=cols(k.x, n), in0=b, scalar=b2, in1=cols(k.x, n),
                                                      op0=ALU.add, op1=ALU.add))


def project_residual(k, o_t, w, b):
    linear(k, halves(P, w, o_t), lambda e, n, bank: e.scalar_tensor_tensor(
        out=cols(k.x, n), in0=bank, scalar=b, in1=cols(k.x, n), op0=ALU.add, op1=ALU.add))


def program(nc, d, out):
    with ExitStack() as ctx:
        k = Core(nc, ctx)
        q_terms = nc.dram_tensor("q_terms", [H, NTERM, HD, N], BF16).ap()
        k_terms = nc.dram_tensor("k_terms", [H, NTERM, HD, MP], BF16).ap()
        k_self = nc.dram_tensor("k_self", [H, NTERM, HD, N], BF16).ap()
        load_everything(k, d)
        windowed_layer(k, d)

        sb, _, _ = scope_tools(k, ctx)
        kb = sb("key_ring", [P, KRING * MP], BF16)
        qb = sb("queries", [P, H * N], BF16)
        o_raw = sb("o_raw", [P, H * QT * VC])
        o_t = sb("o_t", [P, N])
        hn = sb("normed", [P, N])
        steps(k, "vector", [lambda e: e.memset(kb[:], 0.0), lambda e: e.memset(kb[32:NR + 1, :], 1.0),
                            lambda e: e.memset(qb[:], 0.0)])

        def attend(prefix, src, w, bq, bk, bv_row):
            with ExitStack() as c2:
                vb = scope_tools(k, c2)[0]("values", [P, H, NT, VC], BF16)
                query_terms(k, src, k.w[prefix + w[0]], bq, qb, q_terms)
                key_value_terms(k, k.ctx_t, TK, NI, k.w[prefix + w[1]], bk, k.w[prefix + w[2]], bv_row,
                                k_terms, vb, pad=True)
                wide_attention(k, TK, NI, kb, qb, vb, k_terms, o_raw)
            normalised_output(k, o_raw, o_t)

        v = k.v
        attend("L1_xattn_", k.x, ("Wq", "Wk", "Wv"), v["L1_xattn_bq"], v["L1_xattn_bk"], d["bv1"])
        project_residual(k, o_t, k.w["L1_xattn_Wo"], v["L1_xattn_bo"])
        ffn(k, k.x, d["ff_w1_1"], d["ff_b1_1"], d["ff_w2_1"], v["L1_xattn_b2"], gelu=True)

        attend("L2_xattn_", k.x, ("Wq", "Wk", "Wv"), None, None, None)
        project_residual(k, o_t, k.w["L2_xattn_Wo"], v["L2_xattn_bo"])
        with ExitStack() as c2:
            s2 = scope_tools(k, c2)[0]
            t1, t2 = s2("t1", [P, N]), s2("t2", [P, N])
            layer_norm(k, k.x[:], v["L2_xattn_ln_gamma"], v["L2_xattn_ln_beta"], hn[:], t1[:], t2[:])
            steps(k, "vector", [lambda e: e.tensor_copy(k.x[:], hn[:])])
            layer_norm(k, k.x[:], v["L3_xattn_ln1_g"], v["L3_xattn_ln1_b"], hn[:], t1[:], t2[:])

        with ExitStack() as c2:
            s2 = scope_tools(k, c2)[0]
            m_qk = s2("mask_query_key", [P, QT * N], BF16)
            m_kq = s2("mask_key_query", [P, QT * N], BF16)
            any_key = s2("any_key", [P, QT])
            with ExitStack() as c3:
                sbm, _, sem = scope_tools(k, c3)
                raw = sbm("mask_bytes", [P, 2, QT, N], U8)
                loaded = [sem("loaded") for _ in range(2)]
                turned = sem("turned")
                block = open_phase(k, c3)

                @block.sync
                def _(sp):
                    sp.dma_start(raw[:, 0], d["mask_qk"].rearrange("(t p) n -> p t n", p=P)).then_inc(loaded[0], 16)
                    sp.dma_start(raw[:, 1], d["mask_kq"].rearrange("(t p) n -> p t n", p=P)).then_inc(loaded[1], 16)

                @block.vector
                def _(dve):
                    for i, m in enumerate((m_qk, m_kq)):
                        dve.wait_ge(loaded[i], 16)
                        dve.tensor_scalar(m[:].rearrange("p (t n) -> p t n", t=QT), raw[:, i], -1.0, BIG,
                                          ALU.add, ALU.mult).then_inc(turned, 1)
                    dve.tensor_reduce(any_key[:], raw[:, 0], AX.X, ALU.max).then_inc(turned, 1)
            vb = s2("values", [P, H, QT, VC], BF16)
            query_terms(k, hn, k.w["L3_xattn_sa_wq"], v["L3_xattn_sa_bq"], qb, q_terms)
            key_value_terms(k, hn, P, 2, k.w["L3_xattn_sa_wk"], v["L3_xattn_sa_bk"], k.w["L3_xattn_sa_wv"],
                            d["bv_sa"], k_self, vb, pad=False)
            wide_attention(k, P, 2, kb, qb, vb, k_self, o_raw, mask=(m_qk, m_kq))
            normalised_output(k, o_raw, o_t, any_key)
        project_residual(k, o_t, k.w["L3_xattn_sa_wo"], v["L3_xattn_sa_bo"])
        with ExitStack() as c2:
            s2 = scope_tools(k, c2)[0]
            t1, t2 = s2("t1", [P, N]), s2("t2", [P, N])
            layer_norm(k, k.x[:], v["L3_xattn_ln2_g"], v["L3_xattn_ln2_b"], hn[:], t1[:], t2[:])
        attend("L3_xattn_", hn, ("ca_wq", "ca_wk", "ca_wv"), v["L3_xattn_ca_bq"], v["L3_xattn_ca_bk"], d["bv_ca"])
        project_residual(k, o_t, k.w["L3_xattn_ca_wo"], v["L3_xattn_ca_bo"])
        with ExitStack() as c2:
            s2 = scope_tools(k, c2)[0]
            t1, t2 = s2("t1", [P, N]), s2("t2", [P, N])
            layer_norm(k, k.x[:], v["L3_xattn_ln3_g"], v["L3_xattn_ln3_b"], hn[:], t1[:], t2[:])
        ffn(k, hn, d["ff_w1_3"], d["ff_b1_3"], d["ff_w2_3"], v["L3_xattn_ff_b2"], gelu=False)

        with ExitStack() as c3:
            _, _, sem = scope_tools(k, c3)
            written = sem("written")
            block = open_phase(k, c3)

            @block.sync
            def _(sp):
                sp.dma_start(out, k.x[:]).then_inc(written, 16)
                sp.wait_ge(written, 16)


def host_layout(inp):
    c = np.ascontiguousarray
    ctx = inp["ctx_1024"][0]
    qkv = inp["L0_xattn_to_qkv_w"]
    swap = np.arange(2 * H * DH) ^ 1
    inv = (1.0 / 10000.0 ** (np.arange(0, DH, 2, dtype=np.float32) / np.float32(DH))).astype(np.float32)
    ang = np.repeat(np.arange(N, dtype=np.float32)[:, None] * inv[None, :], 2, axis=1)
    sign = np.where(np.arange(DH) % 2 == 0, -1.0, 1.0).astype(np.float32)
    qi, ki = np.arange(P)[:, None], np.arange(P)[None, :]
    window = np.where((qi >= ki) & (qi // SEG == ki // SEG), 0.0, -BIG).astype(np.float32)
    pm = inp["L0_xattn_persist_mem"]
    mask = inp["mask_1x1xSxS_bk0"][0, 0]
    pad_rows = lambda a, n: np.concatenate([a, np.zeros((n - a.shape[0],) + a.shape[1:], a.dtype)])
    b1 = inp["L0_xattn_ff_b1"]
    b1_tiles = np.zeros((P, 6), np.float32)
    for s in range(2):
        for g, (o, w) in enumerate(FFT):
            b1_tiles[0:w, 3 * s + g] = b1[s * DFF + o:s * DFF + o + w]
    w2 = np.zeros((3 * P, C), np.float32)
    w2[0:DFF] = inp["L0_xattn_ff_w2"]
    turned = ("L2_xattn_Wq", "L2_xattn_Wk", "L2_xattn_Wv", "L2_xattn_Wo")
    return {
        "x_t": c(inp["x"][0].T), "ctx_t": c(np.concatenate([ctx, ctx[0:MP - M]]).T),
        "vecs": c(np.stack([inp[n] for n in VECS], axis=1)),
        "squares": c(np.stack([inp[n].T if n in turned else inp[n] for n in SQUARES])),
        "ident": np.eye(P, dtype=np.float32),
        "last_rows": (np.arange(P) < LAST_VALID).astype(np.float32)[:, None],
        "w_qkv": c(qkv), "w_swap": c(qkv[:, 0:2 * H * DH][:, swap]),
        "cos": c(np.tile(np.cos(ang).T, (2, 1)).astype(np.float32)),
        "sin": c(np.tile((np.sin(ang) * sign).T, (2, 1)).astype(np.float32)),
        "window_mask": c(np.concatenate([np.zeros((P, NEX), np.float32), window], axis=1)),
        "persist_k": c(pm.reshape(H // 2, 2, 16, DH).transpose(1, 3, 0, 2).reshape(P, H // 2, 16)),
        "persist_v": c(pm.transpose(1, 0, 2).reshape(16, H * DH)),
        "w_out0": c(inp["L0_xattn_to_out_w"]), "ff_w1_0": c(inp["L0_xattn_ff_w1"]), "ff_w2_0": w2,
        "ff_b1_0": b1_tiles,
        "bv1": c(inp["L1_xattn_bv"]), "bv_sa": c(inp["L3_xattn_sa_bv"]), "bv_ca": c(inp["L3_xattn_ca_bv"]),
        "ff_w1_1": c(inp["L1_xattn_W1"]), "ff_b1_1": c(inp["L1_xattn_b1"].reshape(FF // P, P).T),
        "ff_w2_1": c(inp["L1_xattn_W2"]),
        "ff_w1_3": c(inp["L3_xattn_ff_w1"]), "ff_b1_3": c(inp["L3_xattn_ff_b1"].reshape(FF // P, P).T),
        "ff_w2_3": c(inp["L3_xattn_ff_w2"]),
        "mask_qk": c(mask), "mask_kq": c(mask.T),
    }


def kernel(**inputs):
    import concourse.bacc as bacc
    from concourse.bass_utils import run_bass_kernel_spmd

    nc = bacc.Bacc("TRN2", target_bir_lowering=False, num_devices=1)
    arrays = host_layout({n: np.asarray(a) for n, a in inputs.items()})
    d = {n: nc.dram_tensor(f"in_{n}", a.shape, mybir.dt.from_np(a.dtype), kind="ExternalInput").ap()
         for n, a in arrays.items()}
    out = nc.dram_tensor("out_t", (C, N), F32, kind="ExternalOutput").ap()
    program(nc, d, out)
    r = run_bass_kernel_spmd(nc, [{f"in_{n}": a for n, a in arrays.items()}], core_ids=[0])
    return np.ascontiguousarray(r.results[0]["out_t"].T)[None]
```

```python
from contextlib import ExitStack

import numpy as np

import concourse.bass as bass
from concourse import mybir

F32 = mybir.dt.float32
BF16 = mybir.dt.bfloat16
U8 = mybir.dt.uint8
ACT = mybir.ActivationFunctionType
ALU = mybir.AluOpType
AX = mybir.AxisListType

P = 128
N = 1024
C = 128
H = 16
HD = C // H
M = 6404
TPI = 4
TK = 124
CW = TPI * TK
NI = -(-M // CW)
MP = NI * CW
NT = MP // TK
LAST_VALID = M - (NT - 1) * TK
NPART = 3
K_RUNS = (3, 2, 1)
NTERM = sum(K_RUNS)
RUN_ROW = [1 + HD * sum(K_RUNS[:p]) for p in range(NPART)]
NR = 1 + NTERM * HD
VC = 3 * HD + 1
QT = N // P
HALF = 512
KRING = 3
KEY_DMAS = 16 * NPART
WHOLE = 2
WV = HD + 1
LAG = 2
BIG = 1.0e30
PAIR_OF_ONES = float(np.uint32(0x3F803F80).view(np.float32))
SCALE = 1.0 / np.sqrt(np.float32(HD))

DH = 64
SEG = 64
NEX = 32
WK = NEX + P
DFF = 341
FFT = [(0, 128), (128, 128), (256, 85)]
FF = 512
RMS_EPS = 1.1920929e-07
LN_EPS = 1e-05

VECS = ["L0_xattn_attn_norm_w", "L0_xattn_mem_pool_norm_w", "L0_xattn_ff_norm_w", "L0_xattn_ff_b2",
        "L1_xattn_bq", "L1_xattn_bk", "L1_xattn_bo", "L1_xattn_b2", "L2_xattn_bo", "L2_xattn_ln_gamma",
        "L2_xattn_ln_beta", "L3_xattn_sa_bq", "L3_xattn_sa_bk", "L3_xattn_sa_bo", "L3_xattn_ca_bq",
        "L3_xattn_ca_bk", "L3_xattn_ca_bo", "L3_xattn_ff_b2", "L3_xattn_ln1_g", "L3_xattn_ln1_b",
        "L3_xattn_ln2_g", "L3_xattn_ln2_b", "L3_xattn_ln3_g", "L3_xattn_ln3_b"]
SQUARES = ["L0_xattn_to_mem_tokens_w", "L1_xattn_Wq", "L1_xattn_Wk", "L1_xattn_Wv", "L1_xattn_Wo",
           "L2_xattn_Wq", "L2_xattn_Wk", "L2_xattn_Wv", "L2_xattn_Wo", "L3_xattn_sa_wq", "L3_xattn_sa_wk",
           "L3_xattn_sa_wv", "L3_xattn_sa_wo", "L3_xattn_ca_wq", "L3_xattn_ca_wk", "L3_xattn_ca_wv",
           "L3_xattn_ca_wo"]


class Core:

    def __init__(self, nc, ctx):
        self.nc = nc
        self.ctx = ctx
        self.count = 0
        self.product_ready = ctx.enter_context(nc.semaphore("product_ready"))
        self.bank_free = ctx.enter_context(nc.semaphore("bank_free"))
        self.step_done = ctx.enter_context(nc.semaphore("step_done"))
        self.products = 0
        self.phase_sems = []
        self.steps = 0

    def name(self, text):
        self.count += 1
        return f"{text}_{self.count}"


def scope_tools(k, ctx):
    nc = k.nc

    def sb(text, shape, dt=F32):
        return ctx.enter_context(nc.sbuf_tensor(k.name(text), shape, dt))

    def ps(text, shape):
        return ctx.enter_context(nc.psum_tensor(k.name(text), shape, F32))

    def sem(text):
        k.phase_sems.append(ctx.enter_context(nc.semaphore(k.name(text))))
        return k.phase_sems[-1]

    return sb, ps, sem


def open_phase(k, ctx):
    used, k.phase_sems = k.phase_sems, []

    def clear():
        with k.nc.Block() as block:
            @block.gpsimd
            def _(pool):
                for s in used:
                    pool.sem_clear(s)

    ctx.callback(clear)
    return ctx.enter_context(k.nc.Block())


def linear(k, pieces, evacuate, on="vector", beside=None):
    nc = k.nc
    with ExitStack() as ctx:
        sb, ps, sem = scope_tools(k, ctx)
        banks = [ps("product", [P, HALF]) for _ in range(4)]
        product_ready, bank_free = k.product_ready, k.bank_free
        base = k.products
        k.products += len(pieces)
        block = ctx.enter_context(nc.Block())

        @block.tensor
        def _(pe):
            for n, (rows, cols, pairs) in enumerate(pieces):
                if n >= 4:
                    pe.wait_ge(bank_free, base + n - 3)
                for i, (w, a) in enumerate(pairs):
                    mm = pe.matmul(banks[n % 4][0:rows, 0:cols], w, a, start=(i == 0), stop=(i == len(pairs) - 1))
                mm.then_inc(product_ready, 1)

        def take(eng):
            for n, (rows, cols, _) in enumerate(pieces):
                eng.wait_ge(product_ready, base + n + 1)
                evacuate(eng, n, banks[n % 4][0:rows, 0:cols]).then_inc(bank_free, 1)

        if beside is not None:
            @block.gpsimd
            def _(pool):
                beside(pool)

        if on == "vector":
            @block.vector
            def _(dve):
                take(dve)
        else:
            @block.scalar
            def _(act):
                take(act)


def steps(k, on, fns):
    nc = k.nc
    with ExitStack() as ctx:
        _, _, sem = scope_tools(k, ctx)
        step_done = k.step_done
        base = k.steps
        k.steps += len(fns)
        block = ctx.enter_context(nc.Block())

        def chain(eng):
            for n, f in enumerate(fns):
                if n:
                    eng.wait_ge(step_done, base + n)
                f(eng).then_inc(step_done, 1)

        if on == "vector":
            @block.vector
            def _(dve):
                chain(dve)
        else:
            @block.scalar
            def _(act):
                chain(act)


def halves(out_rows, w, a):
    return [(out_rows, HALF, [(w, a[:, c * HALF:(c + 1) * HALF])]) for c in range(2)]


def cols(a, n, w=HALF):
    return a[:, n * w:(n + 1) * w]


def inverse_root(k, var, out, eps):
    steps(k, "scalar", [lambda e: e.activation(out, var, ACT.Sqrt, bias=eps)])
    steps(k, "vector", [lambda e: e.reciprocal(out, out)])


def rms_norm(k, x, w, out, tmp, tmp2, n=N):
    width = min(n, HALF)
    steps(k, "vector", [lambda e: e.tensor_tensor(tmp, x, x, ALU.mult)])
    linear(k, [(P, width, [(k.mean_w[:], cols(tmp, c, width))]) for c in range(n // width)],
           lambda e, i, b: e.tensor_copy(cols(tmp2, i, width), b))
    inverse_root(k, tmp2, tmp, k.eps[:, 0:1])
    steps(k, "vector", [lambda e: e.scalar_tensor_tensor(out=out, in0=x, scalar=w, in1=tmp, op0=ALU.mult, op1=ALU.mult)])


def layer_norm(k, x, g, b, out, tmp, tmp2):
    linear(k, halves(P, k.mean_w[:], x),
           lambda e, i, bank: e.tensor_tensor(cols(tmp, i), cols(x, i), bank, ALU.subtract))
    steps(k, "vector", [lambda e: e.tensor_tensor(tmp2, tmp, tmp, ALU.mult)])
    linear(k, halves(P, k.mean_w[:], tmp2),
           lambda e, i, bank: e.activation(cols(out, i), bank, ACT.Sqrt, bias=k.eps[:, 1:2]), on="scalar")
    steps(k, "vector", [
        lambda e: e.reciprocal(tmp2, out),
        lambda e: e.tensor_tensor(tmp, tmp, tmp2, ALU.mult),
        lambda e: e.tensor_scalar(out, tmp, g, b, ALU.mult, ALU.add)])


def load_everything(k, d):
    nc = k.nc
    sb, _, _ = scope_tools(k, k.ctx)
    k.x = sb("x", [P, N])
    k.ctx_t = sb("context", [P, MP])
    k.vecs = sb("vectors", [P, len(VECS)])
    k.squares = sb("squares", [P, len(SQUARES), P])
    k.mean_w = sb("mean_w", [P, P])
    k.ident = sb("ident", [P, P])
    k.ident_b = sb("ident_b", [P, P], BF16)
    k.eps = sb("eps", [P, 2])
    k.last_rows = sb("last_rows", [P, 1])
    k.queries = sb("queries", [P, H * N], BF16)
    k.v = {n: k.vecs[:, i:i + 1] for i, n in enumerate(VECS)}
    k.w = {n: k.squares[:, i, :] for i, n in enumerate(SQUARES)}
    with ExitStack() as ctx:
        _, _, sem = scope_tools(k, ctx)
        loaded = [sem("loaded") for _ in range(6)]
        constant = sem("constant")
        block = open_phase(k, ctx)

        @block.sync
        def _(sp):
            for i, (dst, src) in enumerate([(k.x[:], d["x_t"]), (k.vecs[:], d["vecs"]), (k.ident[:], d["ident"]),
                                            (k.squares[:], d["squares"].rearrange("w p n -> p w n")),
                                            (k.last_rows[:], d["last_rows"]), (k.ctx_t[:], d["ctx_t"])]):
                sp.dma_start(dst, src).then_inc(loaded[i], 16)
            for s in loaded:
                sp.wait_ge(s, 16)

        @block.vector
        def _(dve):
            dve.memset(k.mean_w[:], 1.0 / C)
            dve.memset(k.eps[:, 0:1], RMS_EPS)
            dve.memset(k.eps[:, 1:2], LN_EPS)
            dve.wait_ge(loaded[2], 16)
            dve.tensor_copy(k.ident_b[:], k.ident[:]).then_inc(constant, 1)
            dve.wait_ge(constant, 1)


def windowed_layer(k, d):
    qp = k.queries[:].bitcast(F32).rearrange("p (h n) -> p h n", n=N)
    with ExitStack() as lctx:
        sb, _, _ = scope_tools(k, lctx)
        mask = sb("window_mask", [P, WK])
        kp = sb("k_pairs", [P, H // 2, NEX + N])
        v_tok = sb("v_tokens", [P, QT, H * DH])
        v_ext = sb("v_extra", [NEX, H * DH])
        windowed_projections(k, d, mask, qp, kp, v_tok, v_ext)
        windowed_attention(k, qp, kp, v_tok, v_ext, mask)
    k.key_ring = scope_tools(k, k.ctx)[0]("key_ring", [P, KRING * MP], BF16)
    gated_ffn(k, d, qp)


def windowed_projections(k, d, mask, qp, kp, v_tok, v_ext):
    nc = k.nc
    with ExitStack() as lctx:
        sb, _, _ = scope_tools(k, lctx)
        w_qkv = sb("w_qkv", [P, 3 * H * DH])
        w_swap = sb("w_swap", [P, 2 * H * DH])
        cos = sb("cos", [P, N])
        sin = sb("sin", [P, N])
        xn = sb("x_normed", [P, N])
        t1 = sb("t1", [P, N])
        t2 = sb("t2", [P, N])
        pool = sb("pooled", [P, 4])
        mem_tok = sb("mem_token", [P, 16])
        with ExitStack() as ctx:
            _, _, sem = scope_tools(k, ctx)
            loaded = [sem("loaded") for _ in range(7)]
            block = open_phase(k, ctx)

            @block.sync
            def _(sp):
                for i, (dst, src) in enumerate([
                        (w_qkv[:], d["w_qkv"]), (w_swap[:], d["w_swap"]), (cos[:], d["cos"]), (sin[:], d["sin"]),
                        (mask[:], d["window_mask"]), (kp[:, :, 16:NEX], d["persist_k"]),
                        (v_ext[16:NEX, :], d["persist_v"])]):
                    sp.dma_start(dst, src).then_inc(loaded[i], 16)
                for s in loaded:
                    sp.wait_ge(s, 16)

        steps(k, "vector", [
            lambda e: e.reduce_sum(pool[:, 0:1], k.ctx_t[:, 0:M], AX.X),
            lambda e: e.tensor_scalar(pool[:, 1:2], pool[:, 0:1], 1.0 / M, None, ALU.mult)])
        rms_norm(k, pool[:, 1:2], k.v["L0_xattn_mem_pool_norm_w"], pool[:, 0:1], pool[:, 2:3], pool[:, 3:4], n=1)
        linear(k, [(P, 1, [(k.w["L0_xattn_to_mem_tokens_w"], pool[:, 0:1])])],
               lambda e, n, b: e.tensor_copy(mem_tok[:], b.to_broadcast([P, 16])))
        rms_norm(k, k.x[:], k.v["L0_xattn_attn_norm_w"], xn[:], t1[:], t2[:])

        linear(k, [(P, 16, [(w_qkv[:, H * DH + P * p:H * DH + P * (p + 1)], mem_tok[:])]) for p in range(H // 2)],
               lambda e, n, b: e.tensor_copy(kp[:, n, 0:16], b))
        linear(k, [(16, HALF, [(mem_tok[:], w_qkv[:, 2 * H * DH + HALF * c:2 * H * DH + HALF * (c + 1)])])
                   for c in range(2)],
               lambda e, n, b: e.tensor_copy(v_ext[0:16, HALF * n:HALF * (n + 1)], b))
        linear(k, [(P, HALF, [(xn[:, P * t:P * (t + 1)],
                               w_qkv[:, 2 * H * DH + HALF * c:2 * H * DH + HALF * (c + 1)])])
                   for t in range(QT) for c in range(2)],
               lambda e, n, b: e.activation(v_tok[:, n // 2, HALF * (n % 2):HALF * (n % 2 + 1)], b, ACT.Copy),
               on="scalar")
        project_rotary(k, w_qkv, w_swap, xn, cos, sin, qp, kp)


def project_rotary(k, w_qkv, w_swap, xn, cos, sin, qp, kp):
    nc = k.nc
    jobs = [(kind, p, c) for p in range(H // 2) for kind in range(2) for c in range(2)]
    with ExitStack() as ctx:
        sb, ps, sem = scope_tools(k, ctx)
        plain = [ps("plain", [P, HALF]) for _ in range(2)]
        swapped = [ps("swapped", [P, HALF]) for _ in range(2)]
        by_cos = sb("by_cos", [P, 2, HALF])
        by_sin = sb("by_sin", [P, 2, HALF])
        projected = sem("projected")
        turned = sem("turned")
        summed = sem("summed")
        block = open_phase(k, ctx)

        @block.tensor
        def _(pe):
            for n, (kind, p, c) in enumerate(jobs):
                if n >= 2:
                    pe.wait_ge(turned, 2 * (n - 1))
                o = kind * H * DH + P * p
                pe.matmul(plain[n % 2][:], w_qkv[:, o:o + P], cols(xn, c), start=True, stop=True)
                pe.matmul(swapped[n % 2][:], w_swap[:, o:o + P], cols(xn, c), start=True, stop=True)\
                    .then_inc(projected, 1)

        @block.vector
        def _(dve):
            for n, (kind, p, c) in enumerate(jobs):
                dve.wait_ge(projected, n + 1)
                if n >= 2:
                    dve.wait_ge(summed, n - 1)
                dve.tensor_tensor(by_cos[:, n % 2, :], plain[n % 2][:], cols(cos, c), ALU.mult).then_inc(turned, 1)
                dve.tensor_tensor(by_sin[:, n % 2, :], swapped[n % 2][:], cols(sin, c), ALU.mult).then_inc(turned, 1)

        @block.gpsimd
        def _(pool):
            for n, (kind, p, c) in enumerate(jobs):
                pool.wait_ge(turned, 2 * (n + 1))
                out = qp[:, p, HALF * c:HALF * (c + 1)] if kind == 0 else kp[:, p, NEX + HALF * c:NEX + HALF * (c + 1)]
                pool.tensor_tensor(out, by_cos[:, n % 2, :], by_sin[:, n % 2, :], ALU.add).then_inc(summed, 1)


def windowed_attention(k, qp, kp, v_tok, v_ext, mask):
    nc = k.nc
    with ExitStack() as ctx:
        sb, ps, sem = scope_tools(k, ctx)
        score = ps("score", [P, QT, 256])
        pt_tok = ps("pt_tokens", [P, HALF])
        pt_ext = ps("pt_extra", [P, HALF])
        o_bank = [ps("o", [P, HALF]) for _ in range(2)]
        sm = sb("masked", [P, 2, QT, WK])
        pr = sb("probs", [P, QT, WK])
        pn = sb("probs_normed", [P, 2, QT, WK])
        nmax = sb("neg_max", [P, 2, QT])
        tot = sb("total", [P, 2, QT])
        inv = sb("inverse", [P, 2, QT])
        ptt = sb("pt_tokens_s", [P, 2, HALF])
        pte = sb("pt_extra_s", [NEX, 2, HALF])
        scores_ready = sem("scores_ready")
        masked_ready = sem("masked_ready")
        max_ready = sem("max_ready")
        exp_ready = sem("exp_ready")
        inv_ready = sem("inv_ready")
        probs_ready = sem("probs_ready")
        turned = sem("turned")
        turned_copied = sem("turned_copied")
        o_ready = sem("o_ready")
        o_copied = sem("o_copied")
        block = open_phase(k, ctx)

        @block.tensor
        def _(pe):
            def scores(h):
                r = slice(DH * (h % 2), DH * (h % 2 + 1))
                if h >= 1:
                    pe.wait_ge(masked_ready, h)
                for t in range(QT):
                    q = qp[r, h // 2, P * t:P * (t + 1)]
                    pe.matmul(score[:, t, 0:NEX], q, kp[r, h // 2, 0:NEX], start=True, stop=True)
                    mm = pe.matmul(score[:, t, NEX:WK], q, kp[r, h // 2, NEX + P * t:NEX + P * (t + 1)],
                                   start=True, stop=True)
                mm.then_inc(scores_ready, 1)

            def turn(h, c):
                n = 2 * h + c
                pe.wait_ge(probs_ready, h + 1)
                if n >= 1:
                    pe.wait_ge(turned_copied, 2 * n)
                for t in range(4):
                    pe.transpose(pt_tok[:, P * t:P * (t + 1)], pn[:, h % 2, 4 * c + t, NEX:WK], k.ident[:])
                    mm = pe.transpose(pt_ext[0:NEX, P * t:P * (t + 1)], pn[:, h % 2, 4 * c + t, 0:NEX], k.ident[:])
                mm.then_inc(turned, 1)

            def values(h, c):
                rows = slice(DH * (h % 2), DH * (h % 2 + 1))
                n = 2 * h + c
                pe.wait_ge(turned_copied, 2 * (n + 1))
                if h >= 2 and h % 2 == 0 and c == 0:
                    pe.wait_ge(o_copied, h // 2)
                for t in range(4):
                    out = o_bank[c][rows, P * t:P * (t + 1)]
                    pe.matmul(out, v_tok[:, 4 * c + t, DH * h:DH * (h + 1)], ptt[:, n % 2, P * t:P * (t + 1)],
                              start=True, stop=False)
                    mm = pe.matmul(out, v_ext[:, DH * h:DH * (h + 1)], pte[:, n % 2, P * t:P * (t + 1)],
                                   start=False, stop=True)
                mm.then_inc(o_ready, 1)

            for s in range(H + 2):
                if s >= 2:
                    turn(s - 2, 0)
                if s < H:
                    scores(s)
                if s >= 2:
                    values(s - 2, 0)
                    turn(s - 2, 1)
                    values(s - 2, 1)

        @block.vector
        def _(dve):
            m3 = mask[:].unsqueeze(1).to_broadcast([P, QT, WK])

            def mask_and_maximum(h):
                dve.wait_ge(scores_ready, h + 1)
                if h >= 2:
                    dve.wait_ge(exp_ready, QT * (h - 1))
                dve.scalar_tensor_tensor(out=sm[:, h % 2, :, :], in0=score[:, :, 0:WK], scalar=float(DH) ** -0.5,
                                         in1=m3, op0=ALU.mult, op1=ALU.add).then_inc(masked_ready, 1)
                dve.wait_ge(masked_ready, h + 1)
                dve.tensor_reduce(nmax[:, h % 2, :], sm[:, h % 2, :, :], AX.X, ALU.max, negate=True)\
                   .then_inc(max_ready, 1)

            def normalise(h):
                dve.wait_ge(exp_ready, QT * (h + 1))
                dve.reciprocal(inv[:, h % 2, :], tot[:, h % 2, :]).then_inc(inv_ready, 1)
                dve.wait_ge(inv_ready, h + 1)
                if h >= 2:
                    dve.wait_ge(turned, 2 * (h - 1))
                dve.tensor_tensor(pn[:, h % 2, :, :], pr[:], inv[:, h % 2, :].unsqueeze(2).to_broadcast([P, QT, WK]),
                                  ALU.mult).then_inc(probs_ready, 1)

            def pair_out(p):
                dve.wait_ge(o_ready, 4 * (p + 1))
                dve.tensor_copy(qp[:, p, 0:HALF], o_bank[0][:])
                dve.tensor_copy(qp[:, p, HALF:N], o_bank[1][:]).then_inc(o_copied, 1)

            for s in range(H + 3):
                if s >= 4 and s % 2 == 0:
                    pair_out((s - 4) // 2)
                if s < H:
                    mask_and_maximum(s)
                if 1 <= s <= H:
                    normalise(s - 1)

        @block.scalar
        def _(act):
            def exps(h):
                act.wait_ge(max_ready, h + 1)
                if h >= 1:
                    act.wait_ge(probs_ready, h)
                for t in range(QT):
                    act.activation(pr[:, t, :], sm[:, h % 2, t, :], ACT.Exp, bias=nmax[:, h % 2, t:t + 1],
                                   accum_out=tot[:, h % 2, t:t + 1]).then_inc(exp_ready, 1)

            def copies(h, c):
                n = 2 * h + c
                act.wait_ge(turned, n + 1)
                if n >= 2:
                    act.wait_ge(o_ready, n - 1)
                act.activation(ptt[:, n % 2, :], pt_tok[:], ACT.Copy).then_inc(turned_copied, 1)
                act.activation(pte[:, n % 2, :], pt_ext[0:NEX, :], ACT.Copy).then_inc(turned_copied, 1)

            for s in range(1, H + 2):
                if s >= 2:
                    copies(s - 2, 0)
                if s <= H:
                    exps(s - 1)
                if s >= 2:
                    copies(s - 2, 1)


def gated_ffn(k, d, o_pairs):
    nc = k.nc
    with ExitStack() as lctx:
        sb, _, _ = scope_tools(k, lctx)
        w_o = sb("w_o", [P, H * DH // P, C])
        w1 = sb("w1", [P, 2 * DFF])
        w2 = sb("w2", [P, 3, C])
        b1 = sb("b1", [P, 6])
        t1, t2, xn = sb("t1", [P, N]), sb("t2", [P, N]), sb("x_normed", [P, N])
        gate = sb("gate", [P, 3, N])
        sig = sb("sigmoid", [P, 3, N])
        with ExitStack() as ctx:
            _, _, sem = scope_tools(k, ctx)
            loaded = [sem("loaded") for _ in range(4)]
            block = open_phase(k, ctx)

            @block.sync
            def _(sp):
                for i, (dst, src) in enumerate([
                        (w_o[:], d["w_out0"].rearrange("(p r) n -> r p n", r=P)), (w1[:], d["ff_w1_0"]),
                        (w2[:], d["ff_w2_0"].rearrange("(g r) n -> r g n", r=P)), (b1[:], d["ff_b1_0"])]):
                    sp.dma_start(dst, src).then_inc(loaded[i], 16)
                for s in loaded:
                    sp.wait_ge(s, 16)

        linear(k, [(P, HALF, [(w_o[:, p, :], o_pairs[:, p, HALF * c:HALF * (c + 1)]) for p in range(H // 2)])
                   for c in range(2)],
               lambda e, n, b: e.tensor_tensor(cols(k.x, n), b, cols(k.x, n), ALU.add),
               beside=lambda pool: pool.memset(k.key_ring[:].bitcast(F32), 0.0))
        rms_norm(k, k.x[:], k.v["L0_xattn_ff_norm_w"], xn[:], t1[:], t2[:])
        jobs = [(g, c) for g in range(3) for c in range(2)]
        linear(k, [(FFT[g][1], HALF, [(w1[:, DFF + FFT[g][0]:DFF + FFT[g][0] + FFT[g][1]], cols(xn, c))])
                   for g, c in jobs],
               lambda e, n, b: e.tensor_scalar(gate[0:b.shape[0], jobs[n][0], HALF * jobs[n][1]:HALF * (jobs[n][1] + 1)],
                                               b, b1[0:b.shape[0], 3 + jobs[n][0]:4 + jobs[n][0]], None, ALU.add),
               beside=lambda pool: pool.memset(k.queries[:].bitcast(F32), 0.0))
        for g in range(3):
            r = FFT[g][1]
            steps(k, "scalar", [lambda e: e.activation(sig[0:r, g, :], gate[0:r, g, :], ACT.Exp, scale=-1.0)])
        for g in range(3):
            r = FFT[g][1]
            steps(k, "vector", [
                lambda e: e.tensor_scalar(sig[0:r, g, :], sig[0:r, g, :], 1.0, None, ALU.add),
                lambda e: e.reciprocal(sig[0:r, g, :], sig[0:r, g, :]),
                lambda e: e.tensor_tensor(gate[0:r, g, :], gate[0:r, g, :], sig[0:r, g, :], ALU.mult)])
        linear(k, [(FFT[g][1], HALF, [(w1[:, FFT[g][0]:FFT[g][0] + FFT[g][1]], cols(xn, c))]) for g, c in jobs],
               lambda e, n, b: e.scalar_tensor_tensor(
                   out=sig[0:b.shape[0], jobs[n][0], HALF * jobs[n][1]:HALF * (jobs[n][1] + 1)], in0=b,
                   scalar=b1[0:b.shape[0], jobs[n][0]:jobs[n][0] + 1],
                   in1=gate[0:b.shape[0], jobs[n][0], HALF * jobs[n][1]:HALF * (jobs[n][1] + 1)],
                   op0=ALU.add, op1=ALU.mult),
               beside=lambda pool: pool.memset(k.key_ring[0:1, :].bitcast(F32), PAIR_OF_ONES))
        linear(k, [(P, HALF, [(w2[0:FFT[g][1], g, :], sig[0:FFT[g][1], g, HALF * c:HALF * (c + 1)]) for g in range(3)])
                   for c in range(2)],
               lambda e, n, b: e.scalar_tensor_tensor(out=cols(k.x, n), in0=b, scalar=k.v["L0_xattn_ff_b2"],
                                                      in1=cols(k.x, n), op0=ALU.add, op1=ALU.add))


def query_terms(k, src, w, bias, qb, q_parts, zero_row):
    nc = k.nc
    with ExitStack() as ctx:
        sb, ps, sem = scope_tools(k, ctx)
        bank = [ps("q_product", [P, HALF]) for _ in range(2)]
        qf = sb("q", [P, N])
        rest = sb("q_rest", [P, N])
        part = [sb("q_part", [P, N], BF16) for _ in range(NPART)]
        projected = sem("projected")
        scaled = sem("scaled")
        high = sem("high")
        rest_ready = sem("rest_ready")
        middle = sem("middle")
        low = sem("low")
        stored = [sem("stored") for _ in range(NPART)]
        fetched = sem("fetched")
        block = open_phase(k, ctx)

        @block.tensor
        def _(pe):
            for c in range(2):
                pe.matmul(bank[c][:], w, cols(src, c), start=True, stop=True).then_inc(projected, 1)

        @block.scalar
        def _(act):
            for c in range(2):
                act.wait_ge(scaled, c + 1)
                act.activation(cols(part[0], c), cols(qf, c), ACT.Copy).then_inc(high, 1)
            for c in range(2):
                act.wait_ge(rest_ready, c + 1)
                act.activation(cols(part[1], c), cols(rest, c), ACT.Copy).then_inc(middle, 1)

        @block.vector
        def _(dve):
            for c in range(2):
                dve.wait_ge(projected, c + 1)
                if bias is None:
                    dve.tensor_scalar(cols(qf, c), bank[c][:], float(SCALE), None, ALU.mult).then_inc(scaled, 1)
                else:
                    dve.tensor_scalar(cols(qf, c), bank[c][:], bias, float(SCALE), ALU.add, ALU.mult)\
                       .then_inc(scaled, 1)
            for c in range(2):
                dve.wait_ge(high, c + 1)
                dve.tensor_tensor(cols(rest, c), cols(qf, c), cols(part[0], c), ALU.subtract).then_inc(rest_ready, 1)
            for c in range(2):
                dve.wait_ge(middle, c + 1)
                dve.tensor_tensor(cols(part[2], c), cols(rest, c), cols(part[1], c), ALU.subtract).then_inc(low, 1)

        @block.sync
        def _(sp):
            sp.dma_start(qb[0:1, :], zero_row).then_inc(fetched, 16)
            for p, ready in enumerate((high, middle, low)):
                sp.wait_ge(ready, 2)
                sp.dma_start(q_parts[:, p].rearrange("h d n -> h d n"), part[p][:]).then_inc(stored[p], 16)
            for p in range(NPART):
                sp.wait_ge(stored[p], 16)
                for r in range(K_RUNS[p]):
                    row = RUN_ROW[p] + HD * r
                    sp.dma_start(qb[row:row + HD, :].rearrange("r (h n) -> r h n", h=H),
                                 q_parts[:, p].rearrange("h d n -> d h n")).then_inc(fetched, 16)
            sp.wait_ge(fetched, 16 * (1 + NTERM))


def key_value_terms(k, src, tk, ni, wk, bk, wv, bv_row, k_parts, vb, pad):
    nc = k.nc
    cw = TPI * tk
    with ExitStack() as ctx:
        sb, ps, sem = scope_tools(k, ctx)
        kps = [ps("k_product", [P, HALF]) for _ in range(2)]
        vps = [ps("v_product", [P, HALF]) for _ in range(2)]
        kf = sb("k", [P, 2, HALF])
        kr = sb("k_rest", [P, 2, HALF])
        kpart = sb("k_part", [P, 3, 2, HALF], BF16)
        vf = sb("v", [P, 2, HALF])
        vr = sb("v_rest", [P, 2, HALF])
        vbias = sb("v_bias", [P, TPI, C])
        k_product = sem("k_product")
        v_product = sem("v_product")
        k_out = sem("k_out")
        k_high = sem("k_high")
        k_rest = sem("k_rest")
        k_mid = sem("k_mid")
        k_low = sem("k_low")
        v_out = sem("v_out")
        v_high = sem("v_high")
        v_rest = sem("v_rest")
        v_mid = sem("v_mid")
        v_low = sem("v_low")
        ones = sem("ones")
        bias_loaded = sem("bias_loaded")
        stored = [sem("stored") for _ in range(NPART)]
        block = open_phase(k, ctx)
        kd = [k_parts[:, t].rearrange("h d n -> h d n") for t in range(NPART)]

        def v_slot(c, lo):
            return vb[0:tk, :, TPI * c:TPI * (c + 1), lo:lo + HD].rearrange("p h t d -> p t h d")

        def split4(a):
            return a.rearrange("p (t h d) -> p t h d", t=TPI, h=H)

        @block.sync
        def _(sp):
            if bv_row is not None:
                for t in range(TPI):
                    sp.dma_start(vbias[:, t, :], bv_row.partition_broadcast(P)).then_inc(bias_loaded, 16)
            for c in range(ni):
                for t in range(NPART):
                    sp.wait_ge((k_high, k_mid, k_low)[t], c + 1)
                    if c >= 1:
                        sp.wait_ge(stored[t], 16 * c)
                    sp.dma_start(kd[t][:, :, cw * c:cw * (c + 1)], kpart[:, t, c % 2, 0:cw])\
                      .then_inc(stored[t], 16)
            for t in range(NPART):
                sp.wait_ge(stored[t], 16 * ni)

        @block.tensor
        def _(pe):
            for c in range(ni):
                if c >= 2:
                    pe.wait_ge(k_out, c - 1)
                    pe.wait_ge(v_out, c - 1)
                pe.matmul(kps[c % 2][:, 0:cw], wk, src[:, cw * c:cw * (c + 1)], start=True, stop=True)\
                  .then_inc(k_product, 1)
                for t in range(TPI):
                    o = cw * c + tk * t
                    mm = pe.matmul(vps[c % 2][0:tk, C * t:C * (t + 1)], src[:, o:o + tk], wv, start=True, stop=True)
                mm.then_inc(v_product, 1)

        @block.scalar
        def _(act):
            def middle_values(c):
                act.wait_ge(v_rest, c + 1)
                act.activation(v_slot(c, HD + 1), split4(vr[0:tk, c % 2, :]), ACT.Copy).then_inc(v_mid, 1)

            for c in range(ni):
                b = c % 2
                act.wait_ge(k_product, c + 1)
                if c >= 2:
                    act.wait_ge(k_rest, c - 1)
                if bk is None:
                    act.activation(kf[:, b, 0:cw], kps[b][:, 0:cw], ACT.Copy).then_inc(k_out, 1)
                else:
                    act.activation(kf[:, b, 0:cw], kps[b][:, 0:cw], ACT.Identity, bias=bk).then_inc(k_out, 1)
                act.wait_ge(k_out, c + 1)
                if c >= 2:
                    act.wait_ge(stored[0], 16 * (c - 1))
                act.activation(kpart[:, 0, b, 0:cw], kf[:, b, 0:cw], ACT.Copy).then_inc(k_high, 1)
                act.wait_ge(v_out, c + 1)
                act.activation(v_slot(c, 0), split4(vf[0:tk, b, :]), ACT.Copy).then_inc(v_high, 1)
                if c >= 1:
                    middle_values(c - 1)
            middle_values(ni - 1)

        @block.vector
        def _(dve):
            dve.memset(vb[0:tk, :, 0:TPI * ni, HD:HD + 1], 1.0).then_inc(ones, 1)
            if bv_row is None:
                dve.memset(vbias[:], 0.0).then_inc(ones, 1)
                dve.wait_ge(ones, 2)
            else:
                dve.wait_ge(bias_loaded, 16 * TPI)
            for c in range(ni):
                b = c % 2
                dve.wait_ge(v_product, c + 1)
                if c >= 2:
                    dve.wait_ge(v_rest, c - 1)
                    dve.wait_ge(v_high, c - 1)
                dve.tensor_tensor(vf[0:tk, b, :], vps[b][0:tk, :], vbias[0:tk].rearrange("p t n -> p (t n)"), ALU.add)\
                   .then_inc(v_out, 1)
                if c >= 2:
                    for t in range(1, NPART):
                        dve.wait_ge(stored[t], 16 * (c - 1))
                dve.wait_ge(k_high, c + 1)
                dve.tensor_tensor(kr[:, b, 0:cw], kf[:, b, 0:cw], kpart[:, 0, b, 0:cw], ALU.subtract).then_inc(k_rest, 1)
                dve.wait_ge(k_rest, c + 1)
                dve.tensor_copy(kpart[:, 1, b, 0:cw], kr[:, b, 0:cw]).then_inc(k_mid, 1)
                dve.wait_ge(k_mid, c + 1)
                dve.tensor_tensor(kpart[:, 2, b, 0:cw], kr[:, b, 0:cw], kpart[:, 1, b, 0:cw], ALU.subtract)\
                   .then_inc(k_low, 1)

        @block.gpsimd
        def _(pool):
            def low_values(c):
                pool.wait_ge(v_mid, c + 1)
                pool.tensor_tensor(v_slot(c, 2 * HD + 1), split4(vr[0:tk, c % 2, :]), v_slot(c, HD + 1), ALU.subtract)\
                    .then_inc(v_low, 1)

            for c in range(ni):
                b = c % 2
                pool.wait_ge(v_high, c + 1)
                if c >= 2:
                    pool.wait_ge(v_low, c - 1)
                pool.tensor_tensor(split4(vr[0:tk, b, :]), split4(vf[0:tk, b, :]), v_slot(c, 0), ALU.subtract)\
                    .then_inc(v_rest, 1)
                if c >= 1:
                    low_values(c - 1)
            low_values(ni - 1)

    if pad:
        last = vb[0:tk, :, TPI * ni - 1, :]
        steps(k, "vector", [lambda e: e.tensor_scalar(last, last, k.last_rows[0:tk, :], None, ALU.mult)])


def wide_attention(k, tk, ni, kb, qb, vb, k_parts, o_raw, o_whole=None, mask=None):
    nc = k.nc
    split_tiles = QT if o_whole is None else QT - WHOLE
    dve_cols = HALF - (QT - split_tiles) * P
    cw = TPI * tk
    nk = cw * ni
    with ExitStack() as ctx:
        sb, ps, sem = scope_tools(k, ctx)
        sc_bank = [ps("scores", [P, HALF]) for _ in range(2)]
        mx_bank = [ps("max_scores", [P, 2, HALF]) for _ in range(2)]
        acc = ps("values_sum", [P, HALF])
        small = ps("small", [P, HALF])
        pr = sb("probs", [P, 2 * TPI, HALF])
        pr_low = sb("probs_low", [P, 2 * TPI, HALF], BF16)
        mx = sb("chunk_max", [P, 2 * ni * QT])
        nmax = sb("neg_max", [P, QT], BF16)
        if o_whole is not None:
            v_whole = sb("values_whole", [P, 2, TPI * ni, WV])
            v_now = sb("values_now", [P, TPI, WV])
            whole_s = sb("whole_sum", [P, WHOLE * P])
            v_middle = sem("v_middle")
            v_ready = sem("v_ready")
            v_placed = sem("v_placed")
            whole_stored = sem("whole_stored")

        keys_loaded = sem("keys_loaded")
        scores_ready = sem("scores_ready")
        exp_ready = sem("exp_ready")
        low_pool = sem("low_pool")
        low_dve = sem("low_dve")
        tile_used = sem("tile_used")
        max_scores = sem("max_scores")
        max_taken = sem("max_taken")
        head_max = sem("head_max")
        max_turned = sem("max_turned")
        max_in_q = sem("max_in_q")
        acc_taken = sem("acc_taken")
        block = open_phase(k, ctx)

        pr_words = pr[:].bitcast(BF16).rearrange("p s (n two) -> p s n two", two=2)

        def high(slot, a, b):
            return pr_words[0:tk, slot, a:b, 1]

        def phases(h, last_head):
            return [(0, True, ni == 1, False)] + ([("loop", False, False, True)] if ni > 2 else []) + \
                [(ni - 1, False, True, False)]

        def run(eng, body):
            def head(h, **kw):
                for i, first, last, looped in phases(h, False):
                    if looped:
                        with eng.Fori(1, ni - 1) as i:
                            body(h, i, first, last, **kw)
                    else:
                        body(h, i, first, last, **kw)
            head(0, ahead=True)
            with eng.Fori(1, H - 2) as h:
                head(h, ahead=True)
            head(H - 2, ahead=True)
            head(H - 1, ahead=False)

        def ends(h):
            return isinstance(h, int) and h == H - 2

        @block.sync
        def _(sp):
            def load(h, at):
                for p, run_length in enumerate(K_RUNS):
                    rows = RUN_ROW[p]
                    sp.dma_start(kb[rows:rows + HD * run_length, bass.ds(at, nk)],
                                 k_parts[bass.ds(h, 1), 0:run_length].rearrange("o p d n -> (o p d) n"))\
                      .then_inc(keys_loaded, 16)

            def store_whole(h, taken):
                sp.wait_ge(acc_taken, taken)
                sp.dma_start(o_whole[bass.ds(h, 1)].rearrange("o v n -> (o v) n"), whole_s[32:32 + WV, :])\
                  .then_inc(whole_stored, 16)

            for h in range(KRING):
                load(h, h * MP)
                sp.wait_ge(keys_loaded, KEY_DMAS * (h + 1))
            with sp.Fori(KRING, H) as h:
                done = sp.snap(h - KRING)
                taken = sp.snap(h - KRING + 1)
                at = sp.snap((h % KRING) * MP)
                scored = sp.snap((h - KRING + 1) * (2 * TPI * ni))
                sp.wait_ge(scores_ready, scored)
                load(h, at)
                if o_whole is not None:
                    store_whole(done, taken)
            sp.wait_ge(keys_loaded, KEY_DMAS * H)
            if o_whole is not None:
                for h in range(H - KRING, H):
                    store_whole(h, h + 1)
                sp.wait_ge(whole_stored, 16 * H)

        @block.tensor
        def _(pe):
            def max_chunk(h, i, n0, units):
                kof = pe.snap((h % KRING) * MP + i * cw)
                qof = pe.snap(h * N)
                for u in units:
                    n = n0 + u
                    if not (isinstance(n, int) and n < 2):
                        pe.wait_ge(max_taken, n - 1)
                    for v in range(2):
                        t = 2 * u + v
                        out = mx_bank[u % 2][:, v, 0:cw]
                        mm = pe.matmul(out, qb[:, bass.ds(qof + t * P, P)], kb[:, bass.ds(kof, cw)],
                                       start=True, stop=mask is None)
                        if mask is not None:
                            mm = pe.matmul(out, k.ident_b[:], mask[0][:, bass.ds(i * cw + t * nk, cw)],
                                           start=False, stop=True)
                    mm.then_inc(max_scores, 1)

            def values(tile, slot, placed, first_tile=False, last_tile=False):
                pe.wait_ge(low_pool, tile + 1)
                pe.wait_ge(low_dve, tile + 1)
                vof = pe.snap(tile * VC)
                v = vb[0:tk].rearrange("p h t c -> p (h t c)")[:, bass.ds(vof, VC)]
                if o_whole is not None:
                    pe.wait_ge(v_placed, placed)
                    pe.matmul(small[32:32 + WV, 0:WHOLE * P], v_now[0:tk, slot, :],
                              pr[0:tk, 2 * slot + 1, dve_cols:HALF], start=first_tile, stop=last_tile)
                for t in range(split_tiles):
                    half = 2 * slot + t // 4
                    a = P * (t % 4)
                    out = acc[:, VC * t:VC * (t + 1)]
                    pe.matmul(out, high(half, a, a + P), v, start=(first_tile and t == 0), stop=False,
                              skip_group_check=True)
                    mm = pe.matmul(out, pr_low[0:tk, half, a:a + P], v, start=False, stop=last_tile,
                                   skip_group_check=True)
                mm.then_inc(tile_used, 1)

            def turn_max(h, part):
                pe.wait_ge(head_max, h + 1)
                if not (isinstance(h, int) and h == 0 and part == 0):
                    pe.wait_ge(max_in_q, 2 * h + part)
                for t in range(4):
                    mm = pe.matmul(small[0:1, P * t:P * (t + 1)], nmax[:, 4 * part + t:4 * part + t + 1], k.ident_b[:],
                                   start=True, stop=True)
                mm.then_inc(max_turned, 1)

            def body(h, i, first, last, ahead):
                g = pe.snap(h * ni + i) if not (isinstance(h, int) and isinstance(i, int)) else h * ni + i
                kof = pe.snap((h % KRING) * MP + i * cw)
                qof = pe.snap(h * N)
                if first:
                    pe.wait_ge(max_in_q, 2 * h + 2)
                for j in range(TPI):
                    for c in range(2):
                        n = 2 * TPI * g + 2 * j + c
                        if not (isinstance(n, int) and n < 2):
                            pe.wait_ge(exp_ready, n - 1)
                        mm = pe.matmul(sc_bank[c][0:tk, :], kb[:, bass.ds(kof + j * tk, tk)],
                                       qb[:, bass.ds(qof + c * HALF, HALF)], start=True, stop=mask is None)
                        if mask is not None:
                            mm = pe.matmul(sc_bank[c][0:tk, :], k.ident_b[:],
                                           mask[1][:, bass.ds((i * TPI + j) * N + c * HALF, HALF)],
                                           start=False, stop=True)
                        mm.then_inc(scores_ready, 1)
                    if ahead and not (last and ends(h)):
                        if last:
                            if j == 0:
                                pe.wait_ge(keys_loaded, KEY_DMAS * (h + 3))
                            max_chunk(h + 2, 0, TPI * (g + ni + 1), [j])
                        else:
                            max_chunk(h + 1, i + 1, TPI * (g + ni + 1), [j])
                    if j >= LAG:
                        if first and j == LAG and not (isinstance(h, int) and h == 0):
                            pe.wait_ge(acc_taken, h)
                        values(TPI * g + j - LAG, j - LAG, 2 * g + 1, first_tile=first and j == LAG)
                    elif not (first and isinstance(h, int) and h == 0):
                        values(TPI * g + j - LAG, TPI + j - LAG, 2 * g, last_tile=first and j == LAG - 1)
                    if last and ahead and j in (1, 2):
                        turn_max(h + 1, j - 1)

            for h, i in [(0, i) for i in range(ni)] + [(1, 0)]:
                if i == 0:
                    pe.wait_ge(keys_loaded, KEY_DMAS * (h + 1))
                max_chunk(h, i, TPI * (h * ni + i), range(TPI))
            for part in range(2):
                turn_max(0, part)
            run(pe, body)
            for j in range(LAG):
                values(TPI * ni * H - LAG + j, TPI - LAG + j, 2 * ni * H, last_tile=j == LAG - 1)

        @block.scalar
        def _(act):
            def max_into_queries(h, part):
                act.wait_ge(max_turned, 2 * h + part + 1)
                act.activation(qb[0:1, bass.ds(h * N + part * HALF, HALF)], small[0:1, :], ACT.Copy)\
                   .then_inc(max_in_q, 1)

            def place_values(h, i, g, pair, first):
                if first and pair == 0:
                    act.wait_ge(v_ready, h + 2)
                if not (isinstance(g, int) and g == 0):
                    act.wait_ge(tile_used, TPI * g - 2 + 2 * pair)
                slot = h % 2 if isinstance(h, int) else act.snap(h % 2)
                at = slot * (TPI * ni * WV) + (TPI * i + 2 * pair) * WV
                act.activation(v_now[0:tk, 2 * pair:2 * pair + 2, :].rearrange("p t c -> p (t c)"),
                               v_whole[0:tk].rearrange("p s t c -> p (s t c)")[:, bass.ds(at, 2 * WV)], ACT.Copy)\
                   .then_inc(v_placed, 1)

            def body(h, i, first, last, ahead):
                g = h * ni + i
                g = g if isinstance(g, int) else act.snap(g)
                for j in range(TPI):
                    if o_whole is not None and j % 2 == 0:
                        place_values(h, i, g, j // 2, first)
                    tile = TPI * g + j
                    for c in range(2):
                        act.wait_ge(scores_ready, 2 * TPI * g + 2 * j + c + 1)
                        if c == 0 and not (isinstance(tile, int) and tile < TPI):
                            act.wait_ge(tile_used, tile - TPI + 1)
                        act.activation(pr[0:tk, 2 * j + c, :], sc_bank[c][0:tk, :], ACT.Exp).then_inc(exp_ready, 1)
                    if last and ahead and j in (1, 2):
                        max_into_queries(h + 1, j - 1)

            for part in range(2):
                max_into_queries(0, part)
            run(act, body)

        @block.gpsimd
        def _(pool):
            def whole_values(h):
                if isinstance(h, int):
                    slot = h % 2
                    if h >= 2:
                        pool.wait_ge(v_placed, 2 * ni * (h - 1))
                else:
                    slot = pool.snap(h % 2)
                    pool.wait_ge(v_placed, (h - 1) * (2 * ni))
                v = vb[0:tk].rearrange("p h t c -> p (h t) c")[:, bass.ds(h * (TPI * ni), TPI * ni), :]
                w = v_whole[0:tk].rearrange("p s t c -> p (s t) c")[:, bass.ds(slot * (TPI * ni), TPI * ni), 0:HD]
                pool.tensor_tensor(w, v[:, :, HD + 1:2 * HD + 1], v[:, :, 2 * HD + 1:VC], ALU.add).then_inc(v_middle, 1)
                pool.wait_ge(v_middle, h + 1)
                pool.tensor_tensor(w, w, v[:, :, 0:HD], ALU.add).then_inc(v_ready, 1)

            if o_whole is not None:
                pool.memset(v_whole[0:tk, :, 0:TPI * ni - 1, HD:WV], 1.0)
                pool.tensor_copy(v_whole[0:tk, :, TPI * ni - 1, HD:WV],
                                 k.last_rows[0:tk].unsqueeze(1).to_broadcast([tk, 2, 1])).then_inc(v_ready, 1)
                whole_values(0)

            def body(h, i, first, last, ahead):
                g = h * ni + i
                g = g if isinstance(g, int) else pool.snap(g)
                if o_whole is not None and last and ahead:
                    whole_values(h + 1)
                for j in range(TPI):
                    pool.wait_ge(exp_ready, 2 * TPI * g + 2 * j + 1)
                    pool.tensor_tensor(pr_low[0:tk, 2 * j, :], pr[0:tk, 2 * j, :], high(2 * j, 0, HALF), ALU.subtract)\
                        .then_inc(low_pool, 1)
            run(pool, body)

        @block.vector
        def _(dve):
            def take_max(n, slot, i, u):
                dve.wait_ge(max_scores, n + 1)
                dve.tensor_reduce(mx[:, bass.ds(slot * (ni * QT) + i * QT + 2 * u, 2)], mx_bank[u % 2][:, :, 0:cw],
                                  AX.X, ALU.max).then_inc(max_taken, 1)

            def head_maximum(h, taken):
                dve.wait_ge(max_taken, taken)
                if not (isinstance(h, int) and h == 0):
                    dve.wait_ge(max_turned, 2 * h)
                slot = h % 2 if isinstance(h, int) else dve.snap(h % 2)
                dve.tensor_reduce(nmax[:], mx[:, bass.ds(slot * (ni * QT), ni * QT)].rearrange("p (i t) -> p t i", t=QT),
                                  AX.X, ALU.max, negate=True).then_inc(head_max, 1)

            def take_acc(h):
                dve.wait_ge(tile_used, (h + 1) * (TPI * ni))
                copy = dve.tensor_copy(o_raw[:, bass.ds(h * (QT * VC), split_tiles * VC)], acc[:, 0:split_tiles * VC])
                if o_whole is not None:
                    if not (isinstance(h, int) and h == 0):
                        dve.wait_ge(whole_stored, h * 16)
                    copy = dve.tensor_copy(whole_s[32:32 + WV, :], small[32:32 + WV, 0:WHOLE * P])
                copy.then_inc(acc_taken, 1)

            def low_part(tiles_before, slot):
                dve.wait_ge(exp_ready, 2 * tiles_before + 2)
                half = 2 * slot + 1
                dve.tensor_tensor(pr_low[0:tk, half, 0:dve_cols], pr[0:tk, half, 0:dve_cols], high(half, 0, dve_cols),
                                  ALU.subtract).then_inc(low_dve, 1)

            def body(h, i, first, last, ahead):
                g = h * ni + i
                g = g if isinstance(g, int) else dve.snap(g)
                if last and ahead:
                    head_maximum(h + 1, TPI * (g + ni + 1))
                for j in range(TPI):
                    if first and j == LAG and not (isinstance(h, int) and h == 0):
                        take_acc(h - 1)
                    if not (first and j == 0 and isinstance(h, int) and h == 0):
                        low_part(TPI * g + j - 1, (j - 1) % TPI)
                    if ahead and not (last and ends(h)):
                        hm, im = (h + 2, 0) if last else (h + 1, i + 1)
                        slot = hm % 2 if isinstance(hm, int) else dve.snap(hm % 2)
                        take_max(TPI * (g + ni + 1) + j, slot, im, j)

            for h, i in [(0, i) for i in range(ni)] + [(1, 0)]:
                for u in range(TPI):
                    take_max(TPI * (h * ni + i) + u, h, i, u)
            head_maximum(0, TPI * ni)
            run(dve, body)
            low_part(TPI * ni * H - 1, TPI - 1)
            take_acc(H - 1)


def normalised_output(k, o_raw, out_t, o_whole=None, any_key=None):
    nc = k.nc
    split_tiles = QT if o_whole is None else QT - WHOLE
    with ExitStack() as lctx:
        sb, _, _ = scope_tools(k, lctx)
        o = sb("o", [P, H, split_tiles, HD])
        oq = sb("o_query_major", [P, split_tiles, C])
        inv = sb("inverse", [P, H, split_tiles])
        v = o_raw[:].rearrange("p (h t c) -> p h t c", h=H, t=QT)[:, :, 0:split_tiles, :]
        if o_whole is not None:
            sums = sb("whole_sums", [P, WHOLE * P])
            totals = sb("whole_totals", [P, WHOLE * P])
        total = v[:, :, :, HD]
        fns = []
        if any_key is not None:
            seen = any_key[:].unsqueeze(1).to_broadcast([P, H, QT])
            fns.append(lambda e: e.tensor_tensor(total, total, seen, ALU.mult))
        fns.append(lambda e: e.reciprocal(inv[:], total))
        if any_key is not None:
            fns.append(lambda e: e.tensor_tensor(inv[:], inv[:], seen, ALU.mult))
        fns += [
            lambda e: e.tensor_tensor(o[:], v[:, :, :, HD + 1:2 * HD + 1], v[:, :, :, 2 * HD + 1:VC], ALU.add),
            lambda e: e.tensor_tensor(o[:], o[:], v[:, :, :, 0:HD], ALU.add),
            lambda e: e.tensor_tensor(oq[:].rearrange("p t (h d) -> p h t d", h=H), o[:],
                                      inv[:].unsqueeze(3).to_broadcast([P, H, split_tiles, HD]), ALU.mult)]
        steps(k, "vector", fns)
        with ExitStack() as ctx:
            _, ps, sem = scope_tools(k, ctx)
            bank = [ps("turned", [P, HALF]) for _ in range(2)]
            turned = sem("turned")
            copied = sem("copied")
            fetched = sem("fetched")
            inverted = sem("inverted")
            block = open_phase(k, ctx)

            if o_whole is not None:
                @block.sync
                def _(sp):
                    sp.dma_start(totals[:], o_whole[:, HD:WV, :].to_broadcast([H, HD, WHOLE * P]))\
                      .then_inc(fetched, 16)
                    sp.dma_start(sums[:], o_whole[:, 0:HD, :]).then_inc(fetched, 16)

                @block.vector
                def _(dve):
                    dve.wait_ge(fetched, 32)
                    dve.reciprocal(totals[:], totals[:]).then_inc(inverted, 1)
                    dve.wait_ge(inverted, 1)
                    dve.tensor_tensor(out_t[:, split_tiles * P:N], sums[:], totals[:], ALU.mult)

            @block.tensor
            def _(pe):
                for t in range(split_tiles):
                    pe.transpose(bank[t // 4][:, P * (t % 4):P * (t % 4 + 1)], oq[:, t, :], k.ident[:])\
                      .then_inc(turned, 1)

            @block.scalar
            def _(act):
                for c in range(2):
                    tiles = min(4, split_tiles - 4 * c)
                    act.wait_ge(turned, 4 * c + tiles)
                    act.activation(out_t[:, HALF * c:HALF * c + P * tiles], bank[c][:, 0:P * tiles], ACT.Copy)\
                       .then_inc(copied, 1)


def ffn(k, x_in, w1_d, b1_d, w2_d, b2, gelu):
    nc = k.nc
    with ExitStack() as lctx:
        sb, _, _ = scope_tools(k, lctx)
        w1 = sb("w1", [P, FF])
        w2 = sb("w2", [P, FF // P, C])
        b1 = sb("b1", [P, FF // P])
        hid = sb("hidden", [P, FF // P, N])
        with ExitStack() as ctx:
            _, _, sem = scope_tools(k, ctx)
            loaded = [sem("loaded") for _ in range(3)]
            block = open_phase(k, ctx)

            @block.sync
            def _(sp):
                for i, (dst, src) in enumerate([(w1[:], w1_d), (w2[:], w2_d.rearrange("(g r) n -> r g n", r=P)),
                                                (b1[:], b1_d)]):
                    sp.dma_start(dst, src).then_inc(loaded[i], 16)
                for s in loaded:
                    sp.wait_ge(s, 16)

        jobs = [(g, c) for c in range(2) for g in range(FF // P)]
        fn = ACT.Gelu_apprx_tanh if gelu else ACT.Relu
        linear(k, [(P, HALF, [(w1[:, P * g:P * (g + 1)], cols(x_in, c))]) for g, c in jobs],
               lambda e, n, b: e.activation(hid[:, jobs[n][0], HALF * jobs[n][1]:HALF * (jobs[n][1] + 1)], b, fn,
                                            bias=b1[:, jobs[n][0]:jobs[n][0] + 1]), on="scalar")
        linear(k, [(P, HALF, [(w2[:, g, :], hid[:, g, HALF * c:HALF * (c + 1)]) for g in range(FF // P)])
                   for c in range(2)],
               lambda e, n, b: e.scalar_tensor_tensor(out=cols(k.x, n), in0=b, scalar=b2, in1=cols(k.x, n),
                                                      op0=ALU.add, op1=ALU.add))


def project_residual(k, o_t, w, b):
    linear(k, halves(P, w, o_t), lambda e, n, bank: e.scalar_tensor_tensor(
        out=cols(k.x, n), in0=bank, scalar=b, in1=cols(k.x, n), op0=ALU.add, op1=ALU.add))


def program(nc, d, out):
    with ExitStack() as ctx:
        k = Core(nc, ctx)
        q_parts = nc.dram_tensor("q_parts", [H, NPART, HD, N], BF16).ap()
        k_parts = nc.dram_tensor("k_parts", [H, NPART, HD, MP], BF16).ap()
        k_self = nc.dram_tensor("k_self", [H, NPART, HD, N], BF16).ap()
        zero_row = nc.dram_tensor("zero_row", [1, H * N], BF16).ap()
        o_whole = nc.dram_tensor("o_whole", [H, WV, WHOLE * P], F32).ap()
        load_everything(k, d)
        windowed_layer(k, d)

        sb, _, _ = scope_tools(k, ctx)
        kb = k.key_ring
        qb = k.queries
        o_raw = sb("o_raw", [P, H * QT * VC])
        o_t = sb("o_t", [P, N])
        hn = sb("normed", [P, N])
        with ExitStack() as c3:
            _, _, sem = scope_tools(k, c3)
            stored = sem("stored")
            block = open_phase(k, c3)

            @block.sync
            def _(sp):
                sp.dma_start(zero_row, qb[0:1, :]).then_inc(stored, 16)
                sp.wait_ge(stored, 16)

        def attend(prefix, src, w, bq, bk, bv_row):
            with ExitStack() as c2:
                vb = scope_tools(k, c2)[0]("values", [P, H, NT, VC], BF16)
                query_terms(k, src, k.w[prefix + w[0]], bq, qb, q_parts, zero_row)
                key_value_terms(k, k.ctx_t, TK, NI, k.w[prefix + w[1]], bk, k.w[prefix + w[2]], bv_row,
                                k_parts, vb, pad=True)
                wide_attention(k, TK, NI, kb, qb, vb, k_parts, o_raw, o_whole)
            normalised_output(k, o_raw, o_t, o_whole)

        v = k.v
        attend("L1_xattn_", k.x, ("Wq", "Wk", "Wv"), v["L1_xattn_bq"], v["L1_xattn_bk"], d["bv1"])
        project_residual(k, o_t, k.w["L1_xattn_Wo"], v["L1_xattn_bo"])
        ffn(k, k.x, d["ff_w1_1"], d["ff_b1_1"], d["ff_w2_1"], v["L1_xattn_b2"], gelu=True)

        attend("L2_xattn_", k.x, ("Wq", "Wk", "Wv"), None, None, None)
        project_residual(k, o_t, k.w["L2_xattn_Wo"], v["L2_xattn_bo"])
        with ExitStack() as c2:
            s2 = scope_tools(k, c2)[0]
            t1, t2 = s2("t1", [P, N]), s2("t2", [P, N])
            layer_norm(k, k.x[:], v["L2_xattn_ln_gamma"], v["L2_xattn_ln_beta"], hn[:], t1[:], t2[:])
            steps(k, "vector", [lambda e: e.tensor_copy(k.x[:], hn[:])])
            layer_norm(k, k.x[:], v["L3_xattn_ln1_g"], v["L3_xattn_ln1_b"], hn[:], t1[:], t2[:])

        with ExitStack() as c2:
            s2 = scope_tools(k, c2)[0]
            m_qk = s2("mask_query_key", [P, QT * N], BF16)
            m_kq = s2("mask_key_query", [P, QT * N], BF16)
            any_key = s2("any_key", [P, QT])
            with ExitStack() as c3:
                sbm, _, sem = scope_tools(k, c3)
                raw = sbm("mask_bytes", [P, 2, QT, N], U8)
                loaded = [sem("loaded") for _ in range(2)]
                turned = sem("turned")
                block = open_phase(k, c3)

                @block.sync
                def _(sp):
                    sp.dma_start(raw[:, 0], d["mask_qk"].rearrange("(t p) n -> p t n", p=P)).then_inc(loaded[0], 16)
                    sp.dma_start(raw[:, 1], d["mask_kq"].rearrange("(t p) n -> p t n", p=P)).then_inc(loaded[1], 16)

                @block.vector
                def _(dve):
                    for i, m in enumerate((m_qk, m_kq)):
                        dve.wait_ge(loaded[i], 16)
                        dve.tensor_scalar(m[:].rearrange("p (t n) -> p t n", t=QT), raw[:, i], -1.0, BIG,
                                          ALU.add, ALU.mult).then_inc(turned, 1)
                    dve.tensor_reduce(any_key[:], raw[:, 0], AX.X, ALU.max).then_inc(turned, 1)
            vb = s2("values", [P, H, QT, VC], BF16)
            query_terms(k, hn, k.w["L3_xattn_sa_wq"], v["L3_xattn_sa_bq"], qb, q_parts, zero_row)
            key_value_terms(k, hn, P, 2, k.w["L3_xattn_sa_wk"], v["L3_xattn_sa_bk"], k.w["L3_xattn_sa_wv"],
                            d["bv_sa"], k_self, vb, pad=False)
            wide_attention(k, P, 2, kb, qb, vb, k_self, o_raw, mask=(m_qk, m_kq))
            normalised_output(k, o_raw, o_t, any_key=any_key)
        project_residual(k, o_t, k.w["L3_xattn_sa_wo"], v["L3_xattn_sa_bo"])
        with ExitStack() as c2:
            s2 = scope_tools(k, c2)[0]
            t1, t2 = s2("t1", [P, N]), s2("t2", [P, N])
            layer_norm(k, k.x[:], v["L3_xattn_ln2_g"], v["L3_xattn_ln2_b"], hn[:], t1[:], t2[:])
        attend("L3_xattn_", hn, ("ca_wq", "ca_wk", "ca_wv"), v["L3_xattn_ca_bq"], v["L3_xattn_ca_bk"], d["bv_ca"])
        project_residual(k, o_t, k.w["L3_xattn_ca_wo"], v["L3_xattn_ca_bo"])
        with ExitStack() as c2:
            s2 = scope_tools(k, c2)[0]
            t1, t2 = s2("t1", [P, N]), s2("t2", [P, N])
            layer_norm(k, k.x[:], v["L3_xattn_ln3_g"], v["L3_xattn_ln3_b"], hn[:], t1[:], t2[:])
        ffn(k, hn, d["ff_w1_3"], d["ff_b1_3"], d["ff_w2_3"], v["L3_xattn_ff_b2"], gelu=False)

        with ExitStack() as c3:
            _, _, sem = scope_tools(k, c3)
            written = sem("written")
            block = open_phase(k, c3)

            @block.sync
            def _(sp):
                sp.dma_start(out, k.x[:]).then_inc(written, 16)
                sp.wait_ge(written, 16)


def host_layout(inp):
    c = np.ascontiguousarray
    ctx = inp["ctx_1024"][0]
    qkv = inp["L0_xattn_to_qkv_w"]
    swap = np.arange(2 * H * DH) ^ 1
    inv = (1.0 / 10000.0 ** (np.arange(0, DH, 2, dtype=np.float32) / np.float32(DH))).astype(np.float32)
    ang = np.repeat(np.arange(N, dtype=np.float32)[:, None] * inv[None, :], 2, axis=1)
    sign = np.where(np.arange(DH) % 2 == 0, -1.0, 1.0).astype(np.float32)
    qi, ki = np.arange(P)[:, None], np.arange(P)[None, :]
    window = np.where((qi >= ki) & (qi // SEG == ki // SEG), 0.0, -BIG).astype(np.float32)
    pm = inp["L0_xattn_persist_mem"]
    mask = inp["mask_1x1xSxS_bk0"][0, 0]
    pad_rows = lambda a, n: np.concatenate([a, np.zeros((n - a.shape[0],) + a.shape[1:], a.dtype)])
    b1 = inp["L0_xattn_ff_b1"]
    b1_tiles = np.zeros((P, 6), np.float32)
    for s in range(2):
        for g, (o, w) in enumerate(FFT):
            b1_tiles[0:w, 3 * s + g] = b1[s * DFF + o:s * DFF + o + w]
    w2 = np.zeros((3 * P, C), np.float32)
    w2[0:DFF] = inp["L0_xattn_ff_w2"]
    turned = ("L2_xattn_Wq", "L2_xattn_Wk", "L2_xattn_Wv", "L2_xattn_Wo")
    return {
        "x_t": c(inp["x"][0].T), "ctx_t": c(np.concatenate([ctx, ctx[0:MP - M]]).T),
        "vecs": c(np.stack([inp[n] for n in VECS], axis=1)),
        "squares": c(np.stack([inp[n].T if n in turned else inp[n] for n in SQUARES])),
        "ident": np.eye(P, dtype=np.float32),
        "last_rows": (np.arange(P) < LAST_VALID).astype(np.float32)[:, None],
        "w_qkv": c(qkv), "w_swap": c(qkv[:, 0:2 * H * DH][:, swap]),
        "cos": c(np.tile(np.cos(ang).T, (2, 1)).astype(np.float32)),
        "sin": c(np.tile((np.sin(ang) * sign).T, (2, 1)).astype(np.float32)),
        "window_mask": c(np.concatenate([np.zeros((P, NEX), np.float32), window], axis=1)),
        "persist_k": c(pm.reshape(H // 2, 2, 16, DH).transpose(1, 3, 0, 2).reshape(P, H // 2, 16)),
        "persist_v": c(pm.transpose(1, 0, 2).reshape(16, H * DH)),
        "w_out0": c(inp["L0_xattn_to_out_w"]), "ff_w1_0": c(inp["L0_xattn_ff_w1"]), "ff_w2_0": w2,
        "ff_b1_0": b1_tiles,
        "bv1": c(inp["L1_xattn_bv"]), "bv_sa": c(inp["L3_xattn_sa_bv"]), "bv_ca": c(inp["L3_xattn_ca_bv"]),
        "ff_w1_1": c(inp["L1_xattn_W1"]), "ff_b1_1": c(inp["L1_xattn_b1"].reshape(FF // P, P).T),
        "ff_w2_1": c(inp["L1_xattn_W2"]),
        "ff_w1_3": c(inp["L3_xattn_ff_w1"]), "ff_b1_3": c(inp["L3_xattn_ff_b1"].reshape(FF // P, P).T),
        "ff_w2_3": c(inp["L3_xattn_ff_w2"]),
        "mask_qk": c(mask), "mask_kq": c(mask.T),
    }


def kernel(**inputs):
    import concourse.bacc as bacc
    from concourse.bass_utils import run_bass_kernel_spmd

    nc = bacc.Bacc("TRN2", target_bir_lowering=False, num_devices=1)
    arrays = host_layout({n: np.asarray(a) for n, a in inputs.items()})
    d = {n: nc.dram_tensor(f"in_{n}", a.shape, mybir.dt.from_np(a.dtype), kind="ExternalInput").ap()
         for n, a in arrays.items()}
    out = nc.dram_tensor("out_t", (C, N), F32, kind="ExternalOutput").ap()
    program(nc, d, out)
    r = run_bass_kernel_spmd(nc, [{f"in_{n}": a for n, a in arrays.items()}], core_ids=[0])
    return np.ascontiguousarray(r.results[0]["out_t"].T)[None]
```

```python
from contextlib import ExitStack

import numpy as np

import concourse.bass as bass
from concourse import mybir

F32 = mybir.dt.float32
BF16 = mybir.dt.bfloat16
U8 = mybir.dt.uint8
ACT = mybir.ActivationFunctionType
ALU = mybir.AluOpType
AX = mybir.AxisListType

P = 128
N = 1024
C = 128
H = 16
HD = C // H
M = 6404
TPI = 4
TK = 124
CW = TPI * TK
NI = -(-M // CW)
MP = NI * CW
NT = MP // TK
LAST_VALID = M - (NT - 1) * TK
NPART = 3
K_RUNS = (3, 2, 1)
NTERM = sum(K_RUNS)
RUN_ROW = [1 + HD * sum(K_RUNS[:p]) for p in range(NPART)]
NR = 1 + NTERM * HD
VC = 3 * HD + 1
QT = N // P
HALF = 512
KRING = 3
KEY_DMAS = 16 * NPART
WHOLE = 2
WV = HD + 1
LAG = 2
BIG = 1.0e30
PAIR_OF_ONES = float(np.uint32(0x3F803F80).view(np.float32))
SCALE = 1.0 / np.sqrt(np.float32(HD))

DH = 64
SEG = 64
NEX = 32
WK = NEX + P
DFF = 341
FFT = [(0, 128), (128, 128), (256, 85)]
FF = 512
RMS_EPS = 1.1920929e-07
LN_EPS = 1e-05

VECS = ["L0_xattn_attn_norm_w", "L0_xattn_mem_pool_norm_w", "L0_xattn_ff_norm_w", "L0_xattn_ff_b2",
        "L1_xattn_bq", "L1_xattn_bk", "L1_xattn_bo", "L1_xattn_b2", "L2_xattn_bo", "L2_xattn_ln_gamma",
        "L2_xattn_ln_beta", "L3_xattn_sa_bq", "L3_xattn_sa_bk", "L3_xattn_sa_bo", "L3_xattn_ca_bq",
        "L3_xattn_ca_bk", "L3_xattn_ca_bo", "L3_xattn_ff_b2", "L3_xattn_ln1_g", "L3_xattn_ln1_b",
        "L3_xattn_ln2_g", "L3_xattn_ln2_b", "L3_xattn_ln3_g", "L3_xattn_ln3_b"]
SQUARES = ["L0_xattn_to_mem_tokens_w", "L1_xattn_Wq", "L1_xattn_Wk", "L1_xattn_Wv", "L1_xattn_Wo",
           "L2_xattn_Wq", "L2_xattn_Wk", "L2_xattn_Wv", "L2_xattn_Wo", "L3_xattn_sa_wq", "L3_xattn_sa_wk",
           "L3_xattn_sa_wv", "L3_xattn_sa_wo", "L3_xattn_ca_wq", "L3_xattn_ca_wk", "L3_xattn_ca_wv",
           "L3_xattn_ca_wo"]


class Core:

    def __init__(self, nc, ctx):
        self.nc = nc
        self.ctx = ctx
        self.count = 0
        self.product_ready = ctx.enter_context(nc.semaphore("product_ready"))
        self.bank_free = ctx.enter_context(nc.semaphore("bank_free"))
        self.step_done = ctx.enter_context(nc.semaphore("step_done"))
        self.products = 0
        self.phase_sems = []
        self.arrived = {}
        self.steps = 0

    def name(self, text):
        self.count += 1
        return f"{text}_{self.count}"


def scope_tools(k, ctx):
    nc = k.nc

    def sb(text, shape, dt=F32):
        return ctx.enter_context(nc.sbuf_tensor(k.name(text), shape, dt))

    def ps(text, shape):
        return ctx.enter_context(nc.psum_tensor(k.name(text), shape, F32))

    def sem(text):
        k.phase_sems.append(ctx.enter_context(nc.semaphore(k.name(text))))
        return k.phase_sems[-1]

    return sb, ps, sem


def open_phase(k, ctx):
    used, k.phase_sems = k.phase_sems, []

    def clear():
        with k.nc.Block() as block:
            @block.gpsimd
            def _(pool):
                for s in used:
                    pool.sem_clear(s)

    ctx.push(lambda failed, *_: None if failed else clear())
    return ctx.enter_context(k.nc.Block())


def linear(k, pieces, evacuate, on="vector", beside=None, beside_vector=None):
    nc = k.nc
    with ExitStack() as ctx:
        sb, ps, sem = scope_tools(k, ctx)
        banks = [ps("product", [P, HALF]) for _ in range(4)]
        product_ready, bank_free = k.product_ready, k.bank_free
        base = k.products
        k.products += len(pieces)
        block = ctx.enter_context(nc.Block())

        @block.tensor
        def _(pe):
            for n, (rows, cols, pairs) in enumerate(pieces):
                if n >= 4:
                    pe.wait_ge(bank_free, base + n - 3)
                for i, (w, a) in enumerate(pairs):
                    mm = pe.matmul(banks[n % 4][0:rows, 0:cols], w, a, start=(i == 0), stop=(i == len(pairs) - 1))
                mm.then_inc(product_ready, 1)

        def take(eng):
            for n, (rows, cols, _) in enumerate(pieces):
                eng.wait_ge(product_ready, base + n + 1)
                evacuate(eng, n, banks[n % 4][0:rows, 0:cols]).then_inc(bank_free, 1)

        if beside_vector is not None:
            @block.vector
            def _(dve):
                beside_vector(dve)

        if beside is not None:
            @block.gpsimd
            def _(pool):
                beside(pool)

        if on == "vector":
            @block.vector
            def _(dve):
                take(dve)
        else:
            @block.scalar
            def _(act):
                take(act)


def steps(k, on, fns):
    nc = k.nc
    with ExitStack() as ctx:
        _, _, sem = scope_tools(k, ctx)
        step_done = k.step_done
        base = k.steps
        k.steps += len(fns)
        block = ctx.enter_context(nc.Block())

        def chain(eng):
            for n, f in enumerate(fns):
                if n:
                    eng.wait_ge(step_done, base + n)
                f(eng).then_inc(step_done, 1)

        if on == "vector":
            @block.vector
            def _(dve):
                chain(dve)
        else:
            @block.scalar
            def _(act):
                chain(act)


def halves(out_rows, w, a):
    return [(out_rows, HALF, [(w, a[:, c * HALF:(c + 1) * HALF])]) for c in range(2)]


def cols(a, n, w=HALF):
    return a[:, n * w:(n + 1) * w]


def rms_norm(k, x, w, out, squares, root, n=N):
    nc = k.nc
    width = min(n, HALF)
    parts = range(n // width)
    with ExitStack() as ctx:
        _, ps, sem = scope_tools(k, ctx)
        bank = [ps("mean", [P, HALF]) for _ in parts]
        squared = sem("squared")
        mean_ready = sem("mean_ready")
        root_ready = sem("root_ready")
        inverted = sem("inverted")
        block = open_phase(k, ctx)

        @block.tensor
        def _(pe):
            for c in parts:
                pe.wait_ge(squared, c + 1)
                pe.matmul(bank[c][:, 0:width], k.mean_w[:], cols(squares, c, width), start=True, stop=True)\
                  .then_inc(mean_ready, 1)

        @block.scalar
        def _(act):
            for c in parts:
                act.activation(cols(squares, c, width), cols(x, c, width), ACT.Square).then_inc(squared, 1)
            for c in parts:
                act.wait_ge(mean_ready, c + 1)
                act.activation(cols(root, c, width), bank[c][:, 0:width], ACT.Sqrt, bias=k.eps[:, 0:1])\
                   .then_inc(root_ready, 1)

        @block.vector
        def _(dve):
            for c in parts:
                dve.wait_ge(root_ready, c + 1)
                dve.reciprocal(cols(root, c, width), cols(root, c, width)).then_inc(inverted, 1)
                dve.wait_ge(inverted, c + 1)
                dve.scalar_tensor_tensor(out=cols(out, c, width), in0=cols(x, c, width), scalar=w,
                                         in1=cols(root, c, width), op0=ALU.mult, op1=ALU.mult)


def layer_norm(k, x, g, b, out, centred, root, beside=None):
    nc = k.nc
    with ExitStack() as ctx:
        sb, ps, sem = scope_tools(k, ctx)
        bank = [ps("mean", [P, HALF]) for _ in range(2)]
        spread = [ps("variance", [P, HALF]) for _ in range(2)]
        squares = sb("squares", [P, N])
        mean_ready = sem("mean_ready")
        centred_ready = sem("centred_ready")
        squared = sem("squared")
        variance_ready = sem("variance_ready")
        root_ready = sem("root_ready")
        inverted = sem("inverted")
        scaled = sem("scaled")
        block = open_phase(k, ctx)

        if beside is not None:
            @block.gpsimd
            def _(pool):
                beside(pool)

        @block.tensor
        def _(pe):
            for c in range(2):
                pe.matmul(bank[c][:], k.mean_w[:], cols(x, c), start=True, stop=True).then_inc(mean_ready, 1)
            for c in range(2):
                pe.wait_ge(squared, c + 1)
                pe.matmul(spread[c][:], k.mean_w[:], cols(squares, c), start=True, stop=True)\
                  .then_inc(variance_ready, 1)

        @block.scalar
        def _(act):
            for c in range(2):
                act.wait_ge(centred_ready, c + 1)
                act.activation(cols(squares, c), cols(centred, c), ACT.Square).then_inc(squared, 1)
            for c in range(2):
                act.wait_ge(variance_ready, c + 1)
                act.activation(cols(root, c), spread[c][:], ACT.Sqrt, bias=k.eps[:, 1:2]).then_inc(root_ready, 1)
            for c in range(2):
                act.wait_ge(scaled, c + 1)
                act.activation(cols(out, c), cols(centred, c), ACT.Identity, bias=b, scale=g)

        @block.vector
        def _(dve):
            for c in range(2):
                dve.wait_ge(mean_ready, c + 1)
                dve.tensor_tensor(cols(centred, c), cols(x, c), bank[c][:], ALU.subtract).then_inc(centred_ready, 1)
            for c in range(2):
                dve.wait_ge(root_ready, c + 1)
                dve.reciprocal(cols(root, c), cols(root, c)).then_inc(inverted, 1)
                dve.wait_ge(inverted, c + 1)
                dve.wait_ge(squared, c + 1)
                dve.tensor_tensor(cols(centred, c), cols(centred, c), cols(root, c), ALU.mult).then_inc(scaled, 1)


def load_everything(k, d):
    nc = k.nc
    sb, _, _ = scope_tools(k, k.ctx)
    k.x = sb("x", [P, N])
    k.ctx_t = sb("context", [P, MP])
    k.vecs = sb("vectors", [P, len(VECS)])
    k.squares = sb("squares", [P, len(SQUARES), P])
    k.mean_w = sb("mean_w", [P, P])
    k.ident = sb("ident", [P, P])
    k.ident_b = sb("ident_b", [P, P], BF16)
    k.eps = sb("eps", [P, 2])
    k.last_rows = sb("last_rows", [P, 1])
    k.queries = sb("queries", [P, H * N], BF16)
    k.v = {n: k.vecs[:, i:i + 1] for i, n in enumerate(VECS)}
    k.w = {n: k.squares[:, i, :] for i, n in enumerate(SQUARES)}
    with ExitStack() as ctx:
        _, _, sem = scope_tools(k, ctx)
        loaded = [sem("loaded") for _ in range(4)]
        constant = sem("constant")
        block = open_phase(k, ctx)

        @block.sync
        def _(sp):
            for i, (dst, src) in enumerate([(k.x[:], d["x_t"]), (k.vecs[:], d["vecs"]), (k.ident[:], d["ident"]),
                                            (k.last_rows[:], d["last_rows"])]):
                sp.dma_start(dst, src).then_inc(loaded[i], 16)
            for s in loaded:
                sp.wait_ge(s, 16)

        @block.vector
        def _(dve):
            dve.memset(k.mean_w[:], 1.0 / C)
            dve.memset(k.eps[:, 0:1], RMS_EPS)
            dve.memset(k.eps[:, 1:2], LN_EPS)
            dve.wait_ge(loaded[2], 16)
            dve.tensor_copy(k.ident_b[:], k.ident[:]).then_inc(constant, 1)
            dve.wait_ge(constant, 1)


def start_loads(k, named):
    with ExitStack() as ctx:
        for name, _, _ in named:
            k.arrived[name] = k.ctx.enter_context(k.nc.semaphore(k.name("arrived_" + name)))
        block = ctx.enter_context(k.nc.Block())

        @block.sync
        def _(sp):
            for name, dst, src in named:
                sp.dma_start(dst, src).then_inc(k.arrived[name], 16)


def await_loads(k, *names):
    with ExitStack() as ctx:
        block = ctx.enter_context(k.nc.Block())

        @block.sync
        def _(sp):
            for name in names:
                sp.wait_ge(k.arrived[name], 16)


def windowed_layer(k, d):
    sb, _, _ = scope_tools(k, k.ctx)
    ff0 = {"w_o": sb("w_o", [P, H * DH // P, C]), "w1": sb("w1", [P, 2 * DFF]), "w2": sb("w2", [P, 3, C]),
           "b1": sb("b1", [P, 6])}
    qp = k.queries[:].bitcast(F32).rearrange("p (h n) -> p h n", n=N)
    with ExitStack() as lctx:
        sb, _, _ = scope_tools(k, lctx)
        mask = sb("window_mask", [P, WK])
        kp = sb("k_pairs", [P, H // 2, QT, WK])
        v_tok = sb("v_tokens", [P, QT, H * DH])
        v_ext = sb("v_extra", [NEX, H * DH])
        windowed_projections(k, d, ff0, mask, qp, kp, v_tok, v_ext)
        windowed_attention(k, qp, kp, v_tok, v_ext, mask)
    k.key_ring = scope_tools(k, k.ctx)[0]("key_ring", [P, KRING * MP], BF16)
    gated_ffn(k, ff0, qp)


def windowed_projections(k, d, ff0, mask, qp, kp, v_tok, v_ext):
    nc = k.nc
    with ExitStack() as lctx:
        sb, _, _ = scope_tools(k, lctx)
        w_qkv = sb("w_qkv", [P, 3 * H * DH])
        w_swap = sb("w_swap", [P, 2 * H * DH])
        cos = sb("cos", [P, N])
        sin = sb("sin", [P, N])
        xn = sb("x_normed", [P, N])
        t1 = sb("t1", [P, N])
        t2 = sb("t2", [P, N])
        pool = sb("pooled", [P, 4])
        mem_tok = sb("mem_token", [P, NEX])
        persist_k = sb("persist_k", [P, H // 2, 16])
        start_loads(k, [
            ("w_qkv", w_qkv[:], d["w_qkv"]), ("w_swap", w_swap[:], d["w_swap"]), ("cos", cos[:], d["cos"]),
            ("sin", sin[:], d["sin"]), ("context", k.ctx_t[:], d["ctx_t"]),
            ("squares", k.squares[:], d["squares"].rearrange("w p n -> p w n")),
            ("mask", mask[:], d["window_mask"]), ("persist_k", persist_k[:], d["persist_k"]),
            ("persist_v", v_ext[:], d["persist_v"]),
            ("w_o", ff0["w_o"][:], d["w_out0"].rearrange("(p r) n -> r p n", r=P)), ("w1", ff0["w1"][:], d["ff_w1_0"]),
            ("w2", ff0["w2"][:], d["ff_w2_0"].rearrange("(g r) n -> r g n", r=P)), ("b1", ff0["b1"][:], d["ff_b1_0"])])
        rms_norm(k, k.x[:], k.v["L0_xattn_attn_norm_w"], xn[:], t1[:], t2[:])
        await_loads(k, "w_qkv", "w_swap", "cos", "sin")
        project_rotary(k, w_qkv, w_swap, xn, cos, sin, qp, kp)
        await_loads(k, "context", "squares", "mask", "persist_k", "persist_v")
        linear(k, [(P, HALF, [(xn[:, P * t:P * (t + 1)],
                               w_qkv[:, 2 * H * DH + HALF * c:2 * H * DH + HALF * (c + 1)])])
                   for t in range(QT) for c in range(2)],
               lambda e, n, b: e.activation(v_tok[:, n // 2, HALF * (n % 2):HALF * (n % 2 + 1)], b, ACT.Copy),
               on="scalar", beside_vector=lambda dve: dve.reduce_sum(pool[:, 0:1], k.ctx_t[:, 0:M], AX.X))
        steps(k, "vector", [lambda e: e.tensor_scalar(pool[:, 1:2], pool[:, 0:1], 1.0 / M, None, ALU.mult)])
        rms_norm(k, pool[:, 1:2], k.v["L0_xattn_mem_pool_norm_w"], pool[:, 0:1], pool[:, 2:3], pool[:, 3:4], n=1)
        linear(k, [(P, 1, [(k.w["L0_xattn_to_mem_tokens_w"], pool[:, 0:1])])],
               lambda e, n, b: e.tensor_copy(mem_tok[:, 0:16], b.to_broadcast([P, 16])),
               beside=lambda g: g.memset(mem_tok[:, 16:NEX], 0.0))
        linear(k, [(P, 16, [(w_qkv[:, H * DH + P * p:H * DH + P * (p + 1)], mem_tok[:, 0:16])])
                   for p in range(H // 2)],
               lambda e, n, b: e.tensor_copy(kp[:, n, :, 0:16], b.unsqueeze(1).to_broadcast([P, QT, 16])),
               beside=lambda g: g.tensor_copy(kp[:, :, :, 16:NEX],
                                              persist_k[:].unsqueeze(2).to_broadcast([P, H // 2, QT, 16])))
        linear(k, [(NEX, HALF, [(mem_tok[:], w_qkv[:, 2 * H * DH + HALF * c:2 * H * DH + HALF * (c + 1)])])
                   for c in range(2)],
               lambda e, n, b: e.tensor_tensor(cols(v_ext, n), b, cols(v_ext, n), ALU.add))


def project_rotary(k, w_qkv, w_swap, xn, cos, sin, qp, kp):
    nc = k.nc
    jobs = [(kind, p, c) for p in range(H // 2) for kind in range(2) for c in range(2)]
    with ExitStack() as ctx:
        sb, ps, sem = scope_tools(k, ctx)
        plain = [ps("plain", [P, HALF]) for _ in range(2)]
        swapped = [ps("swapped", [P, HALF]) for _ in range(2)]
        by_cos = sb("by_cos", [P, 2, HALF])
        by_sin = sb("by_sin", [P, 2, HALF])
        projected = sem("projected")
        turned = sem("turned")
        summed = sem("summed")
        block = open_phase(k, ctx)

        @block.tensor
        def _(pe):
            for n, (kind, p, c) in enumerate(jobs):
                if n >= 2:
                    pe.wait_ge(turned, 2 * (n - 1))
                o = kind * H * DH + P * p
                pe.matmul(plain[n % 2][:], w_qkv[:, o:o + P], cols(xn, c), start=True, stop=True)
                pe.matmul(swapped[n % 2][:], w_swap[:, o:o + P], cols(xn, c), start=True, stop=True)\
                    .then_inc(projected, 1)

        @block.vector
        def _(dve):
            for n, (kind, p, c) in enumerate(jobs):
                dve.wait_ge(projected, n + 1)
                if n >= 2:
                    dve.wait_ge(summed, n - 1)
                dve.tensor_tensor(by_cos[:, n % 2, :], plain[n % 2][:], cols(cos, c), ALU.mult).then_inc(turned, 1)
                dve.tensor_tensor(by_sin[:, n % 2, :], swapped[n % 2][:], cols(sin, c), ALU.mult).then_inc(turned, 1)

        @block.gpsimd
        def _(pool):
            for n, (kind, p, c) in enumerate(jobs):
                pool.wait_ge(turned, 2 * (n + 1))
                if kind == 0:
                    out, parts = cols(qp[:, p, :], c), (by_cos[:, n % 2, :], by_sin[:, n % 2, :])
                else:
                    out = kp[:, p, 4 * c:4 * (c + 1), NEX:WK]
                    parts = [x[:, n % 2, :].rearrange("p (t n) -> p t n", n=P) for x in (by_cos, by_sin)]
                pool.tensor_tensor(out, parts[0], parts[1], ALU.add).then_inc(summed, 1)


def windowed_attention(k, qp, kp, v_tok, v_ext, mask):
    nc = k.nc
    with ExitStack() as ctx:
        sb, ps, sem = scope_tools(k, ctx)
        score = ps("score", [P, QT, 256])
        pt_tok = ps("pt_tokens", [P, HALF])
        pt_ext = ps("pt_extra", [P, HALF])
        o_bank = [ps("o", [P, HALF]) for _ in range(2)]
        sm = sb("masked", [P, 2, QT, WK])
        pr = sb("probs", [P, QT, WK])
        pn = sb("probs_normed", [P, 2, QT, WK])
        nmax = sb("neg_max", [P, 2, QT])
        tot = sb("total", [P, 2, QT])
        inv = sb("inverse", [P, 2, QT])
        ptt = sb("pt_tokens_s", [P, 2, HALF])
        pte = sb("pt_extra_s", [NEX, 2, HALF])
        scores_ready = sem("scores_ready")
        masked_ready = sem("masked_ready")
        max_ready = sem("max_ready")
        exp_ready = sem("exp_ready")
        inv_ready = sem("inv_ready")
        probs_ready = sem("probs_ready")
        turned = sem("turned")
        turned_copied = sem("turned_copied")
        o_ready = sem("o_ready")
        o_copied = sem("o_copied")
        block = open_phase(k, ctx)

        @block.tensor
        def _(pe):
            def scores(h):
                r = slice(DH * (h % 2), DH * (h % 2 + 1))
                if h >= 1:
                    pe.wait_ge(masked_ready, h)
                for t in range(QT):
                    q = qp[r, h // 2, P * t:P * (t + 1)]
                    mm = pe.matmul(score[:, t, 0:WK], q, kp[r, h // 2, t, :], start=True, stop=True)
                mm.then_inc(scores_ready, 1)

            def turn(h, c):
                n = 2 * h + c
                pe.wait_ge(probs_ready, h + 1)
                if n >= 1:
                    pe.wait_ge(turned_copied, 2 * n)
                for t in range(4):
                    pe.transpose(pt_tok[:, P * t:P * (t + 1)], pn[:, h % 2, 4 * c + t, NEX:WK], k.ident[:])
                    mm = pe.transpose(pt_ext[0:NEX, P * t:P * (t + 1)], pn[:, h % 2, 4 * c + t, 0:NEX], k.ident[:])
                mm.then_inc(turned, 1)

            def values(h, c):
                rows = slice(DH * (h % 2), DH * (h % 2 + 1))
                n = 2 * h + c
                pe.wait_ge(turned_copied, 2 * (n + 1))
                if h >= 2 and h % 2 == 0 and c == 0:
                    pe.wait_ge(o_copied, h // 2)
                for t in range(4):
                    pe.matmul(o_bank[c][rows, P * t:P * (t + 1)], v_tok[:, 4 * c + t, DH * h:DH * (h + 1)],
                              ptt[:, n % 2, P * t:P * (t + 1)], start=(t == 0), stop=False, skip_group_check=True)
                pe.matmul(o_bank[c][rows, :], v_ext[:, DH * h:DH * (h + 1)], pte[:, n % 2, :],
                          start=False, stop=True, skip_group_check=True).then_inc(o_ready, 1)

            for s in range(H + 2):
                if s >= 2:
                    turn(s - 2, 0)
                if s < H:
                    scores(s)
                if s >= 2:
                    values(s - 2, 0)
                    turn(s - 2, 1)
                    values(s - 2, 1)

        @block.vector
        def _(dve):
            m3 = mask[:].unsqueeze(1).to_broadcast([P, QT, WK])

            def mask_and_maximum(h):
                dve.wait_ge(scores_ready, h + 1)
                if h >= 2:
                    dve.wait_ge(exp_ready, QT * (h - 1))
                dve.scalar_tensor_tensor(out=sm[:, h % 2, :, :], in0=score[:, :, 0:WK], scalar=float(DH) ** -0.5,
                                         in1=m3, op0=ALU.mult, op1=ALU.add).then_inc(masked_ready, 1)
                dve.wait_ge(masked_ready, h + 1)
                dve.tensor_reduce(nmax[:, h % 2, :], sm[:, h % 2, :, :], AX.X, ALU.max, negate=True)\
                   .then_inc(max_ready, 1)

            def normalise(h):
                dve.wait_ge(exp_ready, QT * (h + 1))
                dve.reciprocal(inv[:, h % 2, :], tot[:, h % 2, :]).then_inc(inv_ready, 1)
                dve.wait_ge(inv_ready, h + 1)
                if h >= 2:
                    dve.wait_ge(turned, 2 * (h - 1))
                dve.tensor_tensor(pn[:, h % 2, :, :], pr[:], inv[:, h % 2, :].unsqueeze(2).to_broadcast([P, QT, WK]),
                                  ALU.mult).then_inc(probs_ready, 1)

            def pair_out(p):
                dve.wait_ge(o_ready, 4 * (p + 1))
                dve.tensor_copy(qp[:, p, 0:HALF], o_bank[0][:])
                dve.tensor_copy(qp[:, p, HALF:N], o_bank[1][:]).then_inc(o_copied, 1)

            for s in range(H + 3):
                if s >= 4 and s % 2 == 0:
                    pair_out((s - 4) // 2)
                if 1 <= s <= H:
                    normalise(s - 1)
                if s < H:
                    mask_and_maximum(s)

        @block.scalar
        def _(act):
            def exps(h):
                act.wait_ge(max_ready, h + 1)
                if h >= 1:
                    act.wait_ge(probs_ready, h)
                for t in range(QT):
                    act.activation(pr[:, t, :], sm[:, h % 2, t, :], ACT.Exp, bias=nmax[:, h % 2, t:t + 1],
                                   accum_out=tot[:, h % 2, t:t + 1]).then_inc(exp_ready, 1)

            def copies(h, c):
                n = 2 * h + c
                act.wait_ge(turned, n + 1)
                if n >= 2:
                    act.wait_ge(o_ready, n - 1)
                act.activation(ptt[:, n % 2, :], pt_tok[:], ACT.Copy).then_inc(turned_copied, 1)
                act.activation(pte[:, n % 2, :], pt_ext[0:NEX, :], ACT.Copy).then_inc(turned_copied, 1)

            for s in range(1, H + 2):
                if s >= 2:
                    copies(s - 2, 0)
                if s <= H:
                    exps(s - 1)
                if s >= 2:
                    copies(s - 2, 1)


def gated_ffn(k, ff0, o_pairs):
    nc = k.nc
    with ExitStack() as lctx:
        sb, _, _ = scope_tools(k, lctx)
        w_o, w1, w2, b1 = (ff0[n] for n in ("w_o", "w1", "w2", "b1"))
        t1, t2, xn = sb("t1", [P, N]), sb("t2", [P, N]), sb("x_normed", [P, N])
        gate = sb("gate", [P, 3, N])
        gated = sb("gated", [P, 3, N])
        await_loads(k, "w_o", "w1", "w2", "b1")
        linear(k, [(P, HALF, [(w_o[:, p, :], o_pairs[:, p, HALF * c:HALF * (c + 1)]) for p in range(H // 2)])
                   for c in range(2)],
               lambda e, n, b: e.tensor_tensor(cols(k.x, n), b, cols(k.x, n), ALU.add),
               beside=lambda pool: pool.memset(k.key_ring[:].bitcast(F32), 0.0))
        rms_norm(k, k.x[:], k.v["L0_xattn_ff_norm_w"], xn[:], t1[:], t2[:])
        jobs = [(g, c) for g in range(3) for c in range(2)]
        linear(k, [(FFT[g][1], HALF, [(w1[:, DFF + FFT[g][0]:DFF + FFT[g][0] + FFT[g][1]], cols(xn, c))])
                   for g, c in jobs],
               lambda e, n, b: e.activation(gate[0:b.shape[0], jobs[n][0], HALF * jobs[n][1]:HALF * (jobs[n][1] + 1)],
                                            b, ACT.Silu, bias=b1[0:b.shape[0], 3 + jobs[n][0]:4 + jobs[n][0]]),
               on="scalar", beside=lambda pool: pool.memset(k.queries[:].bitcast(F32), 0.0))
        linear(k, [(FFT[g][1], HALF, [(w1[:, FFT[g][0]:FFT[g][0] + FFT[g][1]], cols(xn, c))]) for g, c in jobs],
               lambda e, n, b: e.scalar_tensor_tensor(
                   out=gated[0:b.shape[0], jobs[n][0], HALF * jobs[n][1]:HALF * (jobs[n][1] + 1)], in0=b,
                   scalar=b1[0:b.shape[0], jobs[n][0]:jobs[n][0] + 1],
                   in1=gate[0:b.shape[0], jobs[n][0], HALF * jobs[n][1]:HALF * (jobs[n][1] + 1)],
                   op0=ALU.add, op1=ALU.mult),
               beside=lambda pool: pool.memset(k.key_ring[0:1, :].bitcast(F32), PAIR_OF_ONES))
        linear(k, [(P, HALF, [(w2[0:FFT[g][1], g, :], gated[0:FFT[g][1], g, HALF * c:HALF * (c + 1)]) for g in range(3)])
                   for c in range(2)],
               lambda e, n, b: e.scalar_tensor_tensor(out=cols(k.x, n), in0=b, scalar=k.v["L0_xattn_ff_b2"],
                                                      in1=cols(k.x, n), op0=ALU.add, op1=ALU.add))


def query_terms(k, src, w, bias, q_parts):
    nc = k.nc
    with ExitStack() as ctx:
        sb, ps, sem = scope_tools(k, ctx)
        bank = [ps("q_product", [P, HALF]) for _ in range(2)]
        qf = sb("q", [P, N])
        rest = sb("q_rest", [P, N])
        part = [sb("q_part", [P, N], BF16) for _ in range(NPART)]
        projected = sem("projected")
        scaled = sem("scaled")
        high = sem("high")
        rest_ready = sem("rest_ready")
        middle = sem("middle")
        low = sem("low")
        stored = [sem("stored") for _ in range(NPART)]
        block = open_phase(k, ctx)

        @block.tensor
        def _(pe):
            for c in range(2):
                pe.matmul(bank[c][:], w, cols(src, c), start=True, stop=True).then_inc(projected, 1)

        @block.scalar
        def _(act):
            for c in range(2):
                act.wait_ge(scaled, c + 1)
                act.activation(cols(part[0], c), cols(qf, c), ACT.Copy).then_inc(high, 1)
            for c in range(2):
                act.wait_ge(rest_ready, c + 1)
                act.activation(cols(part[1], c), cols(rest, c), ACT.Copy).then_inc(middle, 1)

        @block.vector
        def _(dve):
            for c in range(2):
                dve.wait_ge(projected, c + 1)
                if bias is None:
                    dve.tensor_scalar(cols(qf, c), bank[c][:], float(SCALE), None, ALU.mult).then_inc(scaled, 1)
                else:
                    dve.tensor_scalar(cols(qf, c), bank[c][:], bias, float(SCALE), ALU.add, ALU.mult)\
                       .then_inc(scaled, 1)
            for c in range(2):
                dve.wait_ge(high, c + 1)
                dve.tensor_tensor(cols(rest, c), cols(qf, c), cols(part[0], c), ALU.subtract).then_inc(rest_ready, 1)
            for c in range(2):
                dve.wait_ge(middle, c + 1)
                dve.tensor_tensor(cols(part[2], c), cols(rest, c), cols(part[1], c), ALU.subtract).then_inc(low, 1)

        @block.sync
        def _(sp):
            for p, ready in enumerate((high, middle, low)):
                sp.wait_ge(ready, 2)
                sp.dma_start(q_parts[:, p], part[p][:]).then_inc(stored[p], 16)
            for p in range(NPART):
                sp.wait_ge(stored[p], 16)


def key_value_terms(k, src, tk, ni, wk, bk, wv, bv_row, k_parts, vb, pad, qb, q_parts, zero_row,
                    beside_vector=None):
    nc = k.nc
    cw = TPI * tk
    with ExitStack() as ctx:
        sb, ps, sem = scope_tools(k, ctx)
        kps = [ps("k_product", [P, HALF]) for _ in range(2)]
        vps = [ps("v_product", [P, HALF]) for _ in range(2)]
        kf = sb("k", [P, 2, HALF])
        kr = sb("k_rest", [P, 2, HALF])
        kpart = sb("k_part", [P, 3, 2, HALF], BF16)
        vf = sb("v", [P, 2, HALF])
        vr = sb("v_rest", [P, 2, HALF])
        vbias = sb("v_bias", [P, TPI, C])
        k_product = sem("k_product")
        v_product = sem("v_product")
        k_out = sem("k_out")
        k_high = sem("k_high")
        k_rest = sem("k_rest")
        k_mid = sem("k_mid")
        k_low = sem("k_low")
        v_out = sem("v_out")
        v_high = sem("v_high")
        v_rest = sem("v_rest")
        v_mid = sem("v_mid")
        v_low = sem("v_low")
        ones = sem("ones")
        bias_loaded = sem("bias_loaded")
        fetched = sem("fetched")
        stored = [sem("stored") for _ in range(NPART)]
        block = open_phase(k, ctx)
        kd = [k_parts[:, t] for t in range(NPART)]

        def v_slot(c, lo):
            return vb[0:tk, :, TPI * c:TPI * (c + 1), lo:lo + HD].rearrange("p h t d -> p t h d")

        def split4(a):
            return a.rearrange("p (t h d) -> p t h d", t=TPI, h=H)

        @block.sync
        def _(sp):
            if bv_row is not None:
                for t in range(TPI):
                    sp.dma_start(vbias[:, t, :], bv_row.partition_broadcast(P)).then_inc(bias_loaded, 16)
            sp.dma_start(qb[0:1, :], zero_row).then_inc(fetched, 16)
            for p in range(NPART):
                for r in range(K_RUNS[p]):
                    row = RUN_ROW[p] + HD * r
                    sp.dma_start(qb[row:row + HD, :].rearrange("r (h n) -> r h n", h=H),
                                 q_parts[:, p].rearrange("h d n -> d h n")).then_inc(fetched, 16)
            for c in range(ni):
                for t in range(NPART):
                    sp.wait_ge((k_high, k_mid, k_low)[t], c + 1)
                    if c >= 1:
                        sp.wait_ge(stored[t], 16 * c)
                    sp.dma_start(kd[t][:, :, cw * c:cw * (c + 1)], kpart[:, t, c % 2, 0:cw])\
                      .then_inc(stored[t], 16)
            for t in range(NPART):
                sp.wait_ge(stored[t], 16 * ni)
            sp.wait_ge(fetched, 16 * (1 + NTERM))

        @block.tensor
        def _(pe):
            for c in range(ni):
                if c >= 2:
                    pe.wait_ge(k_out, c - 1)
                    pe.wait_ge(v_out, c - 1)
                pe.matmul(kps[c % 2][:, 0:cw], wk, src[:, cw * c:cw * (c + 1)], start=True, stop=True)\
                  .then_inc(k_product, 1)
                for t in range(TPI):
                    o = cw * c + tk * t
                    mm = pe.matmul(vps[c % 2][0:tk, C * t:C * (t + 1)], src[:, o:o + tk], wv, start=True, stop=True)
                mm.then_inc(v_product, 1)

        @block.scalar
        def _(act):
            def middle_values(c):
                act.wait_ge(v_rest, c + 1)
                act.activation(v_slot(c, HD + 1), split4(vr[0:tk, c % 2, :]), ACT.Copy).then_inc(v_mid, 1)

            for c in range(ni):
                b = c % 2
                act.wait_ge(k_product, c + 1)
                if c >= 2:
                    act.wait_ge(k_rest, c - 1)
                if bk is None:
                    act.activation(kf[:, b, 0:cw], kps[b][:, 0:cw], ACT.Copy).then_inc(k_out, 1)
                else:
                    act.activation(kf[:, b, 0:cw], kps[b][:, 0:cw], ACT.Identity, bias=bk).then_inc(k_out, 1)
                act.wait_ge(k_out, c + 1)
                if c >= 2:
                    act.wait_ge(stored[0], 16 * (c - 1))
                act.activation(kpart[:, 0, b, 0:cw], kf[:, b, 0:cw], ACT.Copy).then_inc(k_high, 1)
                act.wait_ge(v_out, c + 1)
                act.activation(v_slot(c, 0), split4(vf[0:tk, b, :]), ACT.Copy).then_inc(v_high, 1)
                if c >= 1:
                    middle_values(c - 1)
            middle_values(ni - 1)

        @block.vector
        def _(dve):
            dve.memset(vb[0:tk, :, 0:TPI * ni, HD:HD + 1], 1.0).then_inc(ones, 1)
            if bv_row is None:
                dve.memset(vbias[:], 0.0).then_inc(ones, 1)
                dve.wait_ge(ones, 2)
            else:
                dve.wait_ge(bias_loaded, 16 * TPI)
            for c in range(ni):
                b = c % 2
                dve.wait_ge(v_product, c + 1)
                if c >= 2:
                    dve.wait_ge(v_rest, c - 1)
                    dve.wait_ge(v_high, c - 1)
                dve.tensor_tensor(vf[0:tk, b, :], vps[b][0:tk, :], vbias[0:tk].rearrange("p t n -> p (t n)"), ALU.add)\
                   .then_inc(v_out, 1)
                if c >= 2:
                    for t in range(1, NPART):
                        dve.wait_ge(stored[t], 16 * (c - 1))
                dve.wait_ge(k_high, c + 1)
                dve.tensor_tensor(kr[:, b, 0:cw], kf[:, b, 0:cw], kpart[:, 0, b, 0:cw], ALU.subtract).then_inc(k_rest, 1)
                dve.wait_ge(k_rest, c + 1)
                dve.tensor_copy(kpart[:, 1, b, 0:cw], kr[:, b, 0:cw]).then_inc(k_mid, 1)
                dve.wait_ge(k_mid, c + 1)
                dve.tensor_tensor(kpart[:, 2, b, 0:cw], kr[:, b, 0:cw], kpart[:, 1, b, 0:cw], ALU.subtract)\
                   .then_inc(k_low, 1)
            if beside_vector is not None:
                beside_vector(dve)

        @block.gpsimd
        def _(pool):
            def low_values(c):
                pool.wait_ge(v_mid, c + 1)
                pool.tensor_tensor(v_slot(c, 2 * HD + 1), split4(vr[0:tk, c % 2, :]), v_slot(c, HD + 1), ALU.subtract)\
                    .then_inc(v_low, 1)

            for c in range(ni):
                b = c % 2
                pool.wait_ge(v_high, c + 1)
                if c >= 2:
                    pool.wait_ge(v_low, c - 1)
                pool.tensor_tensor(split4(vr[0:tk, b, :]), split4(vf[0:tk, b, :]), v_slot(c, 0), ALU.subtract)\
                    .then_inc(v_rest, 1)
                if c >= 1:
                    low_values(c - 1)
            low_values(ni - 1)

    if pad:
        last = vb[0:tk, :, TPI * ni - 1, :]
        steps(k, "vector", [lambda e: e.tensor_scalar(last, last, k.last_rows[0:tk, :], None, ALU.mult)])


def wide_attention(k, tk, ni, kb, qb, vb, k_parts, o_raw, o_whole=None, mask=None):
    nc = k.nc
    split_tiles = QT if o_whole is None else QT - WHOLE
    dve_cols = HALF - (QT - split_tiles) * P
    helped = ni > 2
    units0 = TPI // 2 if helped else TPI
    skipped = (TPI - units0) * ni
    cw = TPI * tk
    nk = cw * ni
    with ExitStack() as ctx:
        sb, ps, sem = scope_tools(k, ctx)
        sc_bank = [ps("scores", [P, HALF]) for _ in range(2)]
        mx_bank = [ps("max_scores", [P, 2, HALF]) for _ in range(2)]
        acc = ps("values_sum", [P, HALF])
        small = ps("small", [P, HALF])
        pr = sb("probs", [P, 2 * TPI, HALF])
        pr_low = sb("probs_low", [P, 2 * TPI, HALF], BF16)
        mx = sb("chunk_max", [P, 2 * ni * QT])
        nmax = sb("neg_max", [P, QT], BF16)
        if o_whole is not None:
            v_whole = sb("values_whole", [P, 2, TPI * ni, WV])
            v_now = sb("values_now", [P, TPI, WV])
            whole_s = sb("whole_sum", [P, WHOLE * P])
            v_middle = sem("v_middle")
            v_ready = sem("v_ready")
            v_placed = sem("v_placed")
            whole_stored = sem("whole_stored")

        keys_loaded = sem("keys_loaded")
        scores_ready = sem("scores_ready")
        exp_ready = sem("exp_ready")
        low_pool = sem("low_pool")
        low_dve = sem("low_dve")
        tile_used = sem("tile_used")
        max_scores = sem("max_scores")
        max_taken = sem("max_taken")
        head_max = sem("head_max")
        max_turned = sem("max_turned")
        max_in_q = sem("max_in_q")
        acc_taken = sem("acc_taken")
        help_scores = sem("help_scores")
        help_copied = sem("help_copied")
        help_taken = sem("help_taken")
        block = open_phase(k, ctx)

        pr_words = pr[:].bitcast(BF16).rearrange("p s (n two) -> p s n two", two=2)

        def high(slot, a, b):
            return pr_words[0:tk, slot, a:b, 1]

        def phases(h, last_head):
            return [(0, True, ni == 1, False)] + ([("loop", False, False, True)] if ni > 2 else []) + \
                [(ni - 1, False, True, False)]

        def run(eng, body):
            def head(h, **kw):
                for i, first, last, looped in phases(h, False):
                    if looped:
                        with eng.Fori(1, ni - 1) as i:
                            body(h, i, first, last, **kw)
                    else:
                        body(h, i, first, last, **kw)
            head(0, ahead=True)
            with eng.Fori(1, H - 2) as h:
                head(h, ahead=True)
            head(H - 2, ahead=True)
            head(H - 1, ahead=False)

        def ends(h):
            return isinstance(h, int) and h == H - 2

        @block.sync
        def _(sp):
            def load(h, at):
                for p, run_length in enumerate(K_RUNS):
                    rows = RUN_ROW[p]
                    sp.dma_start(kb[rows:rows + HD * run_length, bass.ds(at, nk)],
                                 k_parts[bass.ds(h, 1), 0:run_length].rearrange("o p d n -> (o p d) n"))\
                      .then_inc(keys_loaded, 16)

            def store_whole(h, taken):
                sp.wait_ge(acc_taken, taken)
                sp.dma_start(o_whole[bass.ds(h, 1)].rearrange("o v n -> (o v) n"), whole_s[32:32 + WV, :])\
                  .then_inc(whole_stored, 16)

            for h in range(KRING):
                load(h, h * MP)
                sp.wait_ge(keys_loaded, KEY_DMAS * (h + 1))
            with sp.Fori(KRING, H) as h:
                done = sp.snap(h - KRING)
                taken = sp.snap(h - KRING + 1)
                at = sp.snap((h % KRING) * MP)
                scored = sp.snap((h - KRING + 1) * (2 * TPI * ni))
                sp.wait_ge(scores_ready, scored)
                load(h, at)
                if o_whole is not None:
                    store_whole(done, taken)
            sp.wait_ge(keys_loaded, KEY_DMAS * H)
            if o_whole is not None:
                for h in range(H - KRING, H):
                    store_whole(h, h + 1)
                sp.wait_ge(whole_stored, 16 * H)

        @block.tensor
        def _(pe):
            def max_chunk(h, i, n0, units):
                kof = pe.snap((h % KRING) * MP + i * cw)
                qof = pe.snap(h * N)
                for u in units:
                    n = n0 + u
                    if not (isinstance(n, int) and n < 2):
                        pe.wait_ge(max_taken, n - 1)
                    for v in range(2):
                        t = 2 * u + v
                        out = mx_bank[u % 2][:, v, 0:cw]
                        mm = pe.matmul(out, qb[:, bass.ds(qof + t * P, P)], kb[:, bass.ds(kof, cw)],
                                       start=True, stop=mask is None)
                        if mask is not None:
                            mm = pe.matmul(out, k.ident_b[:], mask[0][:, bass.ds(i * cw + t * nk, cw)],
                                           start=False, stop=True)
                    mm.then_inc(max_scores, 1)

            def help_unit(i, w):
                before = 2 * i + w
                for v in range(2):
                    if before >= 1:
                        pe.wait_ge(help_copied, 2 * before - 1 + v)
                    t = 2 * (units0 + w) + v
                    pe.matmul(sc_bank[v][:, 0:cw], qb[:, t * P:(t + 1) * P], kb[:, i * cw:(i + 1) * cw],
                              start=True, stop=True).then_inc(help_scores, 1)

            def values(tile, slot, placed, first_tile=False, last_tile=False):
                pe.wait_ge(low_pool, tile + 1)
                pe.wait_ge(low_dve, tile + 1)
                vof = pe.snap(tile * VC)
                v = vb[0:tk].rearrange("p h t c -> p (h t c)")[:, bass.ds(vof, VC)]
                if o_whole is not None:
                    pe.wait_ge(v_placed, placed)
                    pe.matmul(small[32:32 + WV, 0:WHOLE * P], v_now[0:tk, slot, :],
                              pr[0:tk, 2 * slot + 1, dve_cols:HALF], start=first_tile, stop=last_tile)
                for t in range(split_tiles):
                    half = 2 * slot + t // 4
                    a = P * (t % 4)
                    out = acc[:, VC * t:VC * (t + 1)]
                    pe.matmul(out, high(half, a, a + P), v, start=(first_tile and t == 0), stop=False,
                              skip_group_check=True)
                    mm = pe.matmul(out, pr_low[0:tk, half, a:a + P], v, start=False, stop=last_tile,
                                   skip_group_check=True)
                mm.then_inc(tile_used, 1)

            def turn_max(h, part):
                pe.wait_ge(head_max, h + 1)
                if not (isinstance(h, int) and h == 0 and part == 0):
                    pe.wait_ge(max_in_q, 2 * h + part)
                for t in range(4):
                    mm = pe.matmul(small[0:1, P * t:P * (t + 1)], nmax[:, 4 * part + t:4 * part + t + 1], k.ident_b[:],
                                   start=True, stop=True)
                mm.then_inc(max_turned, 1)

            def body(h, i, first, last, ahead):
                g = pe.snap(h * ni + i) if not (isinstance(h, int) and isinstance(i, int)) else h * ni + i
                kof = pe.snap((h % KRING) * MP + i * cw)
                qof = pe.snap(h * N)
                if first:
                    pe.wait_ge(max_in_q, 2 * h + 2)
                for j in range(TPI):
                    for c in range(2):
                        n = 2 * TPI * g + 2 * j + c
                        if not (isinstance(n, int) and n < 2):
                            pe.wait_ge(exp_ready, n - 1)
                        mm = pe.matmul(sc_bank[c][0:tk, :], kb[:, bass.ds(kof + j * tk, tk)],
                                       qb[:, bass.ds(qof + c * HALF, HALF)], start=True, stop=mask is None)
                        if mask is not None:
                            mm = pe.matmul(sc_bank[c][0:tk, :], k.ident_b[:],
                                           mask[1][:, bass.ds((i * TPI + j) * N + c * HALF, HALF)],
                                           start=False, stop=True)
                        mm.then_inc(scores_ready, 1)
                    if ahead and not (last and ends(h)):
                        if last:
                            if j == 0:
                                pe.wait_ge(keys_loaded, KEY_DMAS * (h + 3))
                            max_chunk(h + 2, 0, TPI * (g + ni + 1) - skipped, [j])
                        else:
                            max_chunk(h + 1, i + 1, TPI * (g + ni + 1) - skipped, [j])
                    if j >= LAG:
                        if first and j == LAG and not (isinstance(h, int) and h == 0):
                            pe.wait_ge(acc_taken, h)
                        values(TPI * g + j - LAG, j - LAG, 2 * g + 1, first_tile=first and j == LAG)
                    elif not (first and isinstance(h, int) and h == 0):
                        values(TPI * g + j - LAG, TPI + j - LAG, 2 * g, last_tile=first and j == LAG - 1)
                    if last and ahead and j in (1, 2):
                        turn_max(h + 1, j - 1)

            pe.wait_ge(keys_loaded, KEY_DMAS)
            for i in range(ni):
                for u in range(units0):
                    max_chunk(0, i, units0 * i, [u])
                    if helped:
                        help_unit(i, u)
            pe.wait_ge(keys_loaded, KEY_DMAS * 2)
            max_chunk(1, 0, units0 * ni, range(TPI))
            if helped:
                pe.wait_ge(help_copied, 4 * ni)
            for part in range(2):
                turn_max(0, part)
            run(pe, body)
            for j in range(LAG):
                values(TPI * ni * H - LAG + j, TPI - LAG + j, 2 * ni * H, last_tile=j == LAG - 1)

        @block.scalar
        def _(act):
            def max_into_queries(h, part):
                act.wait_ge(max_turned, 2 * h + part + 1)
                act.activation(qb[0:1, bass.ds(h * N + part * HALF, HALF)], small[0:1, :], ACT.Copy)\
                   .then_inc(max_in_q, 1)

            def place_values(h, i, g, pair, first):
                if first and pair == 0:
                    act.wait_ge(v_ready, h + 2)
                if not (isinstance(g, int) and g == 0):
                    act.wait_ge(tile_used, TPI * g - 2 + 2 * pair)
                slot = h % 2 if isinstance(h, int) else act.snap(h % 2)
                at = slot * (TPI * ni * WV) + (TPI * i + 2 * pair) * WV
                act.activation(v_now[0:tk, 2 * pair:2 * pair + 2, :].rearrange("p t c -> p (t c)"),
                               v_whole[0:tk].rearrange("p s t c -> p (s t c)")[:, bass.ds(at, 2 * WV)], ACT.Copy)\
                   .then_inc(v_placed, 1)

            def body(h, i, first, last, ahead):
                g = h * ni + i
                g = g if isinstance(g, int) else act.snap(g)
                for j in range(TPI):
                    if o_whole is not None and j % 2 == 0:
                        place_values(h, i, g, j // 2, first)
                    tile = TPI * g + j
                    for c in range(2):
                        act.wait_ge(scores_ready, 2 * TPI * g + 2 * j + c + 1)
                        if c == 0 and not (isinstance(tile, int) and tile < TPI):
                            act.wait_ge(tile_used, tile - TPI + 1)
                        act.activation(pr[0:tk, 2 * j + c, :], sc_bank[c][0:tk, :], ACT.Exp).then_inc(exp_ready, 1)
                    if last and ahead and j in (1, 2):
                        max_into_queries(h + 1, j - 1)

            if helped:
                for i in range(ni):
                    for w in range(2):
                        if i >= 2:
                            act.wait_ge(help_taken, 2 * (i - 2) + w + 1)
                        for v in range(2):
                            act.wait_ge(help_scores, 2 * (2 * i + w) + v + 1)
                            slot = (4 if i == 0 else 0) + 2 * w + v
                            act.activation(pr_low[:, slot, 0:cw], sc_bank[v][:, 0:cw], ACT.Copy)\
                               .then_inc(help_copied, 1)
            for part in range(2):
                max_into_queries(0, part)
            run(act, body)

        @block.gpsimd
        def _(pool):
            def whole_values(h):
                if isinstance(h, int):
                    slot = h % 2
                    if h >= 2:
                        pool.wait_ge(v_placed, 2 * ni * (h - 1))
                else:
                    slot = pool.snap(h % 2)
                    pool.wait_ge(v_placed, (h - 1) * (2 * ni))
                v = vb[0:tk].rearrange("p h t c -> p (h t) c")[:, bass.ds(h * (TPI * ni), TPI * ni), :]
                w = v_whole[0:tk].rearrange("p s t c -> p (s t) c")[:, bass.ds(slot * (TPI * ni), TPI * ni), 0:HD]
                pool.tensor_tensor(w, v[:, :, HD + 1:2 * HD + 1], v[:, :, 2 * HD + 1:VC], ALU.add).then_inc(v_middle, 1)
                pool.wait_ge(v_middle, h + 1)
                pool.tensor_tensor(w, w, v[:, :, 0:HD], ALU.add).then_inc(v_ready, 1)

            if o_whole is not None:
                pool.memset(v_whole[0:tk, :, 0:TPI * ni - 1, HD:WV], 1.0)
                pool.tensor_copy(v_whole[0:tk, :, TPI * ni - 1, HD:WV],
                                 k.last_rows[0:tk].unsqueeze(1).to_broadcast([tk, 2, 1])).then_inc(v_ready, 1)
                whole_values(0)
            def body(h, i, first, last, ahead):
                g = h * ni + i
                g = g if isinstance(g, int) else pool.snap(g)
                if o_whole is not None and last and ahead:
                    whole_values(h + 1)
                mine = HALF if ahead else HALF // 2
                for j in range(TPI):
                    pool.wait_ge(exp_ready, 2 * TPI * g + 2 * j + 1)
                    pool.tensor_tensor(pr_low[0:tk, 2 * j, 0:mine], pr[0:tk, 2 * j, 0:mine], high(2 * j, 0, mine),
                                       ALU.subtract).then_inc(low_pool, 1)
            run(pool, body)

        @block.vector
        def _(dve):
            def take_max(n, slot, i, u):
                dve.wait_ge(max_scores, n + 1)
                dve.tensor_reduce(mx[:, bass.ds(slot * (ni * QT) + i * QT + 2 * u, 2)], mx_bank[u % 2][:, :, 0:cw],
                                  AX.X, ALU.max).then_inc(max_taken, 1)

            def add_chunk(i, w):
                dve.wait_ge(help_copied, 2 * (2 * i + w) + 2)
                if i >= 2:
                    dve.wait_ge(help_taken, 2 * (i - 2) + w + 1)
                so_far = pr_low[:, 4 + 2 * w:6 + 2 * w, 0:cw]
                dve.tensor_tensor(so_far, so_far, pr_low[:, 2 * w:2 * w + 2, 0:cw], ALU.max).then_inc(help_taken, 1)

            def head_maximum(h, taken):
                dve.wait_ge(max_taken, taken)
                if not (isinstance(h, int) and h == 0):
                    dve.wait_ge(max_turned, 2 * h)
                if helped and isinstance(h, int) and h == 0:
                    t = 2 * units0
                    dve.tensor_reduce(nmax[:, 0:t], mx[:, 0:ni * QT].rearrange("p (i t) -> p t i", t=QT)[:, 0:t, :],
                                      AX.X, ALU.max, negate=True)
                    dve.wait_ge(help_taken, 2 * (ni - 1))
                    dve.tensor_reduce(nmax[:, t:QT], pr_low[:, 4:8, 0:cw], AX.X, ALU.max, negate=True)\
                       .then_inc(head_max, 1)
                    return
                slot = h % 2 if isinstance(h, int) else dve.snap(h % 2)
                dve.tensor_reduce(nmax[:], mx[:, bass.ds(slot * (ni * QT), ni * QT)].rearrange("p (i t) -> p t i", t=QT),
                                  AX.X, ALU.max, negate=True).then_inc(head_max, 1)

            def take_acc(h):
                dve.wait_ge(tile_used, (h + 1) * (TPI * ni))
                copy = dve.tensor_copy(o_raw[:, bass.ds(h * (QT * VC), split_tiles * VC)], acc[:, 0:split_tiles * VC])
                if o_whole is not None:
                    if not (isinstance(h, int) and h == 0):
                        dve.wait_ge(whole_stored, h * 16)
                    copy = dve.tensor_copy(whole_s[32:32 + WV, :], small[32:32 + WV, 0:WHOLE * P])
                copy.then_inc(acc_taken, 1)

            def low_part(tiles_before, slot, of_last_head=False):
                dve.wait_ge(exp_ready, 2 * tiles_before + 2)
                if of_last_head:
                    half, a = 2 * slot, HALF // 2
                    dve.tensor_tensor(pr_low[0:tk, half, a:HALF], pr[0:tk, half, a:HALF], high(half, a, HALF),
                                      ALU.subtract)
                half = 2 * slot + 1
                dve.tensor_tensor(pr_low[0:tk, half, 0:dve_cols], pr[0:tk, half, 0:dve_cols], high(half, 0, dve_cols),
                                  ALU.subtract).then_inc(low_dve, 1)

            def body(h, i, first, last, ahead):
                g = h * ni + i
                g = g if isinstance(g, int) else dve.snap(g)
                if last and ahead:
                    head_maximum(h + 1, TPI * (g + ni + 1) - skipped)
                for j in range(TPI):
                    if first and j == LAG and not (isinstance(h, int) and h == 0):
                        take_acc(h - 1)
                    if not (first and j == 0 and isinstance(h, int) and h == 0):
                        low_part(TPI * g + j - 1, (j - 1) % TPI, of_last_head=not ahead and not (first and j == 0))
                    if ahead and not (last and ends(h)):
                        hm, im = (h + 2, 0) if last else (h + 1, i + 1)
                        slot = hm % 2 if isinstance(hm, int) else dve.snap(hm % 2)
                        take_max(TPI * (g + ni + 1) - skipped + j, slot, im, j)

            for i in range(ni):
                for u in range(units0):
                    take_max(units0 * i + u, 0, i, u)
                    if helped and i >= 1:
                        add_chunk(i, u)
            head_maximum(0, units0 * ni)
            for u in range(TPI):
                take_max(units0 * ni + u, 1, 0, u)
            run(dve, body)
            low_part(TPI * ni * H - 1, TPI - 1, of_last_head=True)
            take_acc(H - 1)


def normalised_output(k, o_raw, out_t, o_whole=None, any_key=None):
    nc = k.nc
    split_tiles = QT if o_whole is None else QT - WHOLE
    with ExitStack() as lctx:
        sb, _, _ = scope_tools(k, lctx)
        o = sb("o", [P, H, split_tiles, HD])
        oq = sb("o_query_major", [P, split_tiles, C])
        inv = sb("inverse", [P, H, split_tiles])
        v = o_raw[:].rearrange("p (h t c) -> p h t c", h=H, t=QT)[:, :, 0:split_tiles, :]
        if o_whole is not None:
            sums = sb("whole_sums", [P, WHOLE * P])
            totals = sb("whole_totals", [P, WHOLE * P])
        total = v[:, :, :, HD]
        fns = []
        if any_key is not None:
            seen = any_key[:].unsqueeze(1).to_broadcast([P, H, QT])
            fns.append(lambda e: e.tensor_tensor(total, total, seen, ALU.mult))
        fns.append(lambda e: e.reciprocal(inv[:], total))
        if any_key is not None:
            fns.append(lambda e: e.tensor_tensor(inv[:], inv[:], seen, ALU.mult))
        fns += [
            lambda e: e.tensor_tensor(o[:], v[:, :, :, HD + 1:2 * HD + 1], v[:, :, :, 2 * HD + 1:VC], ALU.add),
            lambda e: e.tensor_tensor(o[:], o[:], v[:, :, :, 0:HD], ALU.add),
            lambda e: e.tensor_tensor(oq[:].rearrange("p t (h d) -> p h t d", h=H), o[:],
                                      inv[:].unsqueeze(3).to_broadcast([P, H, split_tiles, HD]), ALU.mult)]
        steps(k, "vector", fns)
        with ExitStack() as ctx:
            _, ps, sem = scope_tools(k, ctx)
            bank = [ps("turned", [P, HALF]) for _ in range(2)]
            turned = sem("turned")
            copied = sem("copied")
            fetched = sem("fetched")
            inverted = sem("inverted")
            block = open_phase(k, ctx)

            if o_whole is not None:
                @block.sync
                def _(sp):
                    sp.dma_start(totals[:], o_whole[:, HD:WV, :].to_broadcast([H, HD, WHOLE * P]))\
                      .then_inc(fetched, 16)
                    sp.dma_start(sums[:], o_whole[:, 0:HD, :]).then_inc(fetched, 16)

                @block.vector
                def _(dve):
                    dve.wait_ge(fetched, 32)
                    dve.reciprocal(totals[:], totals[:]).then_inc(inverted, 1)
                    dve.wait_ge(inverted, 1)
                    dve.tensor_tensor(out_t[:, split_tiles * P:N], sums[:], totals[:], ALU.mult)

            @block.tensor
            def _(pe):
                for t in range(split_tiles):
                    pe.transpose(bank[t // 4][:, P * (t % 4):P * (t % 4 + 1)], oq[:, t, :], k.ident[:])\
                      .then_inc(turned, 1)

            @block.scalar
            def _(act):
                for c in range(2):
                    tiles = min(4, split_tiles - 4 * c)
                    act.wait_ge(turned, 4 * c + tiles)
                    act.activation(out_t[:, HALF * c:HALF * c + P * tiles], bank[c][:, 0:P * tiles], ACT.Copy)\
                       .then_inc(copied, 1)


def load_ffn(k, ctx, layer, w1_d, b1_d, w2_d):
    sb, _, _ = scope_tools(k, ctx)
    w1, w2, b1 = sb("w1", [P, FF]), sb("w2", [P, FF // P, C]), sb("b1", [P, FF // P])
    start_loads(k, [(layer + "_w1", w1[:], w1_d), (layer + "_w2", w2[:], w2_d.rearrange("(g r) n -> r g n", r=P)),
                    (layer + "_b1", b1[:], b1_d)])
    return layer, w1, b1, w2


def ffn(k, x_in, weights, b2, gelu):
    layer, w1, b1, w2 = weights
    with ExitStack() as lctx:
        sb, _, _ = scope_tools(k, lctx)
        hid = sb("hidden", [P, FF // P, N])
        await_loads(k, layer + "_w1", layer + "_w2", layer + "_b1")
        jobs = [(g, c) for c in range(2) for g in range(FF // P)]
        fn = ACT.Gelu_apprx_tanh if gelu else ACT.Relu
        linear(k, [(P, HALF, [(w1[:, P * g:P * (g + 1)], cols(x_in, c))]) for g, c in jobs],
               lambda e, n, b: e.activation(hid[:, jobs[n][0], HALF * jobs[n][1]:HALF * (jobs[n][1] + 1)], b, fn,
                                            bias=b1[:, jobs[n][0]:jobs[n][0] + 1]), on="scalar")
        linear(k, [(P, HALF, [(w2[:, g, :], hid[:, g, HALF * c:HALF * (c + 1)]) for g in range(FF // P)])
                   for c in range(2)],
               lambda e, n, b: e.scalar_tensor_tensor(out=cols(k.x, n), in0=b, scalar=b2, in1=cols(k.x, n),
                                                      op0=ALU.add, op1=ALU.add))


def project_residual(k, o_t, w, b):
    linear(k, halves(P, w, o_t), lambda e, n, bank: e.scalar_tensor_tensor(
        out=cols(k.x, n), in0=bank, scalar=b, in1=cols(k.x, n), op0=ALU.add, op1=ALU.add))


def program(nc, d, out):
    with ExitStack() as ctx:
        k = Core(nc, ctx)
        q_parts = nc.dram_tensor("q_parts", [H, NPART, HD, N], BF16).ap()
        k_parts = nc.dram_tensor("k_parts", [H, NPART, HD, MP], BF16).ap()
        k_self = nc.dram_tensor("k_self", [H, NPART, HD, N], BF16).ap()
        zero_row = nc.dram_tensor("zero_row", [1, H * N], BF16).ap()
        o_whole = nc.dram_tensor("o_whole", [H, WV, WHOLE * P], F32).ap()
        load_everything(k, d)
        windowed_layer(k, d)

        sb, _, _ = scope_tools(k, ctx)
        kb = k.key_ring
        qb = k.queries
        o_raw = sb("o_raw", [P, H * QT * VC])
        hn = sb("normed", [P, N])
        o_t = hn
        with ExitStack() as c3:
            _, _, sem = scope_tools(k, c3)
            stored = sem("stored")
            block = open_phase(k, c3)

            @block.sync
            def _(sp):
                sp.dma_start(zero_row, qb[0:1, :]).then_inc(stored, 16)
                sp.wait_ge(stored, 16)

        def attend(prefix, src, w, bq, bk, bv_row, then=lambda: None):
            with ExitStack() as c2:
                vb = scope_tools(k, c2)[0]("values", [P, H, NT, VC], BF16)
                query_terms(k, src, k.w[prefix + w[0]], bq, q_parts)
                key_value_terms(k, k.ctx_t, TK, NI, k.w[prefix + w[1]], bk, k.w[prefix + w[2]], bv_row,
                                k_parts, vb, True, qb, q_parts, zero_row)
                wide_attention(k, TK, NI, kb, qb, vb, k_parts, o_raw, o_whole)
            then()
            normalised_output(k, o_raw, o_t, o_whole)

        v = k.v
        with ExitStack() as c2:
            weights = []
            attend("L1_xattn_", k.x, ("Wq", "Wk", "Wv"), v["L1_xattn_bq"], v["L1_xattn_bk"], d["bv1"],
                   then=lambda: weights.append(load_ffn(k, c2, "ff1", d["ff_w1_1"], d["ff_b1_1"], d["ff_w2_1"])))
            project_residual(k, o_t, k.w["L1_xattn_Wo"], v["L1_xattn_bo"])
            ffn(k, k.x, weights[0], v["L1_xattn_b2"], gelu=True)

        attend("L2_xattn_", k.x, ("Wq", "Wk", "Wv"), None, None, None)
        project_residual(k, o_t, k.w["L2_xattn_Wo"], v["L2_xattn_bo"])
        with ExitStack() as c2:
            s2 = scope_tools(k, c2)[0]
            m_qk = s2("mask_query_key", [P, QT * N], BF16)
            m_kq = s2("mask_key_query", [P, QT * N], BF16)
            any_key = s2("any_key", [P, QT])
            bytes_qk = s2("mask_bytes_query_key", [P, QT, N], U8)

            def turn_mask(m, raw, name):
                def work(pool):
                    pool.wait_ge(k.arrived[name], 16)
                    pool.tensor_scalar(m[:].rearrange("p (t n) -> p t n", t=QT), raw[:], -1.0, BIG, ALU.add, ALU.mult)
                return work

            with ExitStack() as c3:
                s3 = scope_tools(k, c3)[0]
                bytes_kq = s3("mask_bytes_key_query", [P, QT, N], U8)
                t1, t2 = s3("t1", [P, N]), s3("t2", [P, N])
                start_loads(k, [(n, raw[:], d[n].rearrange("(t p) n -> p t n", p=P))
                                for n, raw in (("mask_qk", bytes_qk), ("mask_kq", bytes_kq))])
                layer_norm(k, k.x[:], v["L2_xattn_ln_gamma"], v["L2_xattn_ln_beta"], k.x[:], t1[:], t2[:],
                           beside=turn_mask(m_qk, bytes_qk, "mask_qk"))
                layer_norm(k, k.x[:], v["L3_xattn_ln1_g"], v["L3_xattn_ln1_b"], hn[:], t1[:], t2[:],
                           beside=turn_mask(m_kq, bytes_kq, "mask_kq"))
            vb = s2("values", [P, H, QT, VC], BF16)
            query_terms(k, hn, k.w["L3_xattn_sa_wq"], v["L3_xattn_sa_bq"], q_parts)
            key_value_terms(k, hn, P, 2, k.w["L3_xattn_sa_wk"], v["L3_xattn_sa_bk"], k.w["L3_xattn_sa_wv"],
                            d["bv_sa"], k_self, vb, False, qb, q_parts, zero_row,
                            beside_vector=lambda dve: dve.tensor_reduce(any_key[:], bytes_qk[:], AX.X, ALU.max))
            wide_attention(k, P, 2, kb, qb, vb, k_self, o_raw, mask=(m_qk, m_kq))
            normalised_output(k, o_raw, o_t, any_key=any_key)
        project_residual(k, o_t, k.w["L3_xattn_sa_wo"], v["L3_xattn_sa_bo"])
        with ExitStack() as c2:
            s2 = scope_tools(k, c2)[0]
            t1, t2 = s2("t1", [P, N]), s2("t2", [P, N])
            layer_norm(k, k.x[:], v["L3_xattn_ln2_g"], v["L3_xattn_ln2_b"], hn[:], t1[:], t2[:])
        with ExitStack() as c2:
            weights = []
            attend("L3_xattn_", hn, ("ca_wq", "ca_wk", "ca_wv"), v["L3_xattn_ca_bq"], v["L3_xattn_ca_bk"], d["bv_ca"],
                   then=lambda: weights.append(load_ffn(k, c2, "ff3", d["ff_w1_3"], d["ff_b1_3"], d["ff_w2_3"])))
            project_residual(k, o_t, k.w["L3_xattn_ca_wo"], v["L3_xattn_ca_bo"])
            s2 = scope_tools(k, c2)[0]
            t1, t2 = s2("t1", [P, N]), s2("t2", [P, N])
            layer_norm(k, k.x[:], v["L3_xattn_ln3_g"], v["L3_xattn_ln3_b"], hn[:], t1[:], t2[:])
            ffn(k, hn, weights[0], v["L3_xattn_ff_b2"], gelu=False)

        with ExitStack() as c3:
            _, _, sem = scope_tools(k, c3)
            written = sem("written")
            block = open_phase(k, c3)

            @block.sync
            def _(sp):
                sp.dma_start(out, k.x[:]).then_inc(written, 16)
                sp.wait_ge(written, 16)


def host_layout(inp):
    c = np.ascontiguousarray
    ctx = inp["ctx_1024"][0]
    qkv = inp["L0_xattn_to_qkv_w"]
    swap = np.arange(2 * H * DH) ^ 1
    inv = (1.0 / 10000.0 ** (np.arange(0, DH, 2, dtype=np.float32) / np.float32(DH))).astype(np.float32)
    ang = np.repeat(np.arange(N, dtype=np.float32)[:, None] * inv[None, :], 2, axis=1)
    sign = np.where(np.arange(DH) % 2 == 0, -1.0, 1.0).astype(np.float32)
    qi, ki = np.arange(P)[:, None], np.arange(P)[None, :]
    window = np.where((qi >= ki) & (qi // SEG == ki // SEG), 0.0, -BIG).astype(np.float32)
    pm = inp["L0_xattn_persist_mem"]
    persist_v = np.zeros((NEX, H * DH), np.float32)
    persist_v[16:] = pm.transpose(1, 0, 2).reshape(16, H * DH)
    mask = inp["mask_1x1xSxS_bk0"][0, 0]
    pad_rows = lambda a, n: np.concatenate([a, np.zeros((n - a.shape[0],) + a.shape[1:], a.dtype)])
    b1 = inp["L0_xattn_ff_b1"]
    b1_tiles = np.zeros((P, 6), np.float32)
    for s in range(2):
        for g, (o, w) in enumerate(FFT):
            b1_tiles[0:w, 3 * s + g] = b1[s * DFF + o:s * DFF + o + w]
    w2 = np.zeros((3 * P, C), np.float32)
    w2[0:DFF] = inp["L0_xattn_ff_w2"]
    turned = ("L2_xattn_Wq", "L2_xattn_Wk", "L2_xattn_Wv", "L2_xattn_Wo")
    return {
        "x_t": c(inp["x"][0].T), "ctx_t": c(np.concatenate([ctx, ctx[0:MP - M]]).T),
        "vecs": c(np.stack([inp[n] for n in VECS], axis=1)),
        "squares": c(np.stack([inp[n].T if n in turned else inp[n] for n in SQUARES])),
        "ident": np.eye(P, dtype=np.float32),
        "last_rows": (np.arange(P) < LAST_VALID).astype(np.float32)[:, None],
        "w_qkv": c(qkv), "w_swap": c(qkv[:, 0:2 * H * DH][:, swap]),
        "cos": c(np.tile(np.cos(ang).T, (2, 1)).astype(np.float32)),
        "sin": c(np.tile((np.sin(ang) * sign).T, (2, 1)).astype(np.float32)),
        "window_mask": c(np.concatenate([np.zeros((P, NEX), np.float32), window], axis=1)),
        "persist_k": c(pm.reshape(H // 2, 2, 16, DH).transpose(1, 3, 0, 2).reshape(P, H // 2, 16)),
        "persist_v": persist_v,
        "w_out0": c(inp["L0_xattn_to_out_w"]), "ff_w1_0": c(inp["L0_xattn_ff_w1"]), "ff_w2_0": w2,
        "ff_b1_0": b1_tiles,
        "bv1": c(inp["L1_xattn_bv"]), "bv_sa": c(inp["L3_xattn_sa_bv"]), "bv_ca": c(inp["L3_xattn_ca_bv"]),
        "ff_w1_1": c(inp["L1_xattn_W1"]), "ff_b1_1": c(inp["L1_xattn_b1"].reshape(FF // P, P).T),
        "ff_w2_1": c(inp["L1_xattn_W2"]),
        "ff_w1_3": c(inp["L3_xattn_ff_w1"]), "ff_b1_3": c(inp["L3_xattn_ff_b1"].reshape(FF // P, P).T),
        "ff_w2_3": c(inp["L3_xattn_ff_w2"]),
        "mask_qk": c(mask), "mask_kq": c(mask.T),
    }


def kernel(**inputs):
    import concourse.bacc as bacc
    from concourse.bass_utils import run_bass_kernel_spmd

    nc = bacc.Bacc("TRN2", target_bir_lowering=False, num_devices=1)
    arrays = host_layout({n: np.asarray(a) for n, a in inputs.items()})
    d = {n: nc.dram_tensor(f"in_{n}", a.shape, mybir.dt.from_np(a.dtype), kind="ExternalInput").ap()
         for n, a in arrays.items()}
    out = nc.dram_tensor("out_t", (C, N), F32, kind="ExternalOutput").ap()
    program(nc, d, out)
    r = run_bass_kernel_spmd(nc, [{f"in_{n}": a for n, a in arrays.items()}], core_ids=[0])
    return np.ascontiguousarray(r.results[0]["out_t"].T)[None]
```
